# Optimizing a Trainium2 kernel written in Bass

```python
import numpy as np
import jax
import jax.numpy as jnp

def _softmax(x, axis=-1):
    return jax.nn.softmax(x, axis=axis)

def _gelu(x):
    return jax.nn.gelu(x, approximate=True)

def _silu(x):
    return jax.nn.silu(x)

def _sigmoid(x):
    return jax.nn.sigmoid(x)

def _layernorm(x, axis=-1, eps=1e-05):
    m = jnp.mean(x, axis=axis, keepdims=True)
    v = jnp.var(x, axis=axis, keepdims=True)
    return (x - m) / jnp.sqrt(v + eps)

def _scatter_add(tgt, idx, src, axis=0):
    return tgt.at[idx].add(src)

def _segment_sum(src, seg, n):
    return jax.ops.segment_sum(src, seg, n)
kernel_name = 'mk_gnn_resnorm_d2_gnn_r8_4ca959'

def setup_inputs(seed: int=0):
    np.random.seed(seed)
    _w = jnp.asarray

    def _rec_inputs():
        import jax
        import jax.numpy as jnp
        _gk = jax.random.key(seed)
        x = -8.776e-05 + 1 * jax.random.normal(jax.random.fold_in(_gk, 1), (1250, 512), jnp.float32)
        src = jax.random.randint(jax.random.fold_in(_gk, 2), (40000,), 0, 1250, jnp.int32)
        dst = jax.random.randint(jax.random.fold_in(_gk, 3), (40000,), 0, 1250, jnp.int32)
        _o = jnp.argsort(dst, stable=True)
        src = src[_o]
        dst = dst[_o]
        edge_attr_64 = -5.3897e-05 + 0.999841 * jax.random.normal(jax.random.fold_in(_gk, 11), (40000, 64), jnp.float32)
        return (x, src, dst, edge_attr_64)
    x, src, dst, edge_attr_64 = _rec_inputs()

    def _L0_gnn_setup():
        import jax, jax.numpy as jnp
        import numpy as np
        N_EMBD = 512
        HEADS = 8
        C = N_EMBD // HEADS
        N_NODES = 1250
        N_EDGES = 20000
        NEG_SLOPE = 0.2
        LN_EPS = 1e-05

        def _layer_norm(x, g, b):
            mu = jnp.mean(x, axis=-1, keepdims=True)
            var = jnp.mean(jnp.square(x - mu), axis=-1, keepdims=True)
            return (x - mu) * jax.lax.rsqrt(var + LN_EPS) * g + b

        def _gatv2(x, edge_index, Wl, Wr, att, gat_bias):
            src, dst = (edge_index[0], edge_index[1])
            xl = (x @ Wl).reshape(-1, HEADS, C)
            xr = (x @ Wr).reshape(-1, HEADS, C)
            h = jax.nn.leaky_relu(xl[src] + xr[dst], NEG_SLOPE)
            e = jnp.einsum('ehc,hc->eh', h, att)
            m = jax.ops.segment_max(e, dst, num_segments=N_NODES)
            ex = jnp.exp(e - m[dst])
            denom = jax.ops.segment_sum(ex, dst, num_segments=N_NODES)
            alpha = ex / (denom[dst] + 1e-16)
            msg = alpha[..., None] * xl[src]
            out = jax.ops.segment_sum(msg, dst, num_segments=N_NODES)
            return out.reshape(-1, HEADS * C) + gat_bias
        key = jax.random.key(seed)
        ks = jax.random.split(key, 12)
        s = 0.02
        x = jax.random.normal(ks[0], (N_NODES, N_EMBD), dtype=jnp.float32)
        edge_index = jax.random.randint(ks[1], (2, N_EDGES), 0, N_NODES, dtype=jnp.int32)
        return {'x': x, 'edge_index': edge_index, 'ln1_g': jnp.ones((N_EMBD,), jnp.float32), 'ln1_b': jnp.zeros((N_EMBD,), jnp.float32), 'Wl': jax.random.normal(ks[2], (N_EMBD, HEADS * C), jnp.float32) * s, 'Wr': jax.random.normal(ks[3], (N_EMBD, HEADS * C), jnp.float32) * s, 'att': jax.random.normal(ks[4], (HEADS, C), jnp.float32) * s, 'gat_bias': jnp.zeros((HEADS * C,), jnp.float32), 'ln2_g': jnp.ones((N_EMBD,), jnp.float32), 'ln2_b': jnp.zeros((N_EMBD,), jnp.float32), 'W1': jax.random.normal(ks[5], (N_EMBD, 4 * N_EMBD), jnp.float32) * s, 'b1': jnp.zeros((4 * N_EMBD,), jnp.float32), 'W2': jax.random.normal(ks[6], (4 * N_EMBD, N_EMBD), jnp.float32) * s, 'b2': jnp.zeros((N_EMBD,), jnp.float32)}
    _L0_gnn_all = _L0_gnn_setup()
    _L0_gnn_in = {k: v for k, v in _L0_gnn_all.items() if k in ('ln1_g', 'ln1_b', 'Wl', 'Wr', 'att', 'gat_bias', 'ln2_g', 'ln2_b', 'W1', 'b1', 'W2', 'b2')}
    del _L0_gnn_all

    def _L1_gnn_setup():
        import jax, jax.numpy as jnp
        import numpy as np
        N, E, H, ED = (6250, 50000, 512, 64)
        BN_EPS = 1e-05

        def _bn(h, g, b):
            mu = jnp.mean(h, axis=0)
            var = jnp.mean(jnp.square(h - mu), axis=0)
            return (h - mu) * jax.lax.rsqrt(var + BN_EPS) * g + b
        key = jax.random.key(seed)
        ks = jax.random.split(key, 8)
        s = lambda d: 1.0 / np.sqrt(d)
        return {'x': jax.random.normal(ks[0], (N, H), jnp.float32), 'edge_attr': jax.random.normal(ks[1], (E, ED), jnp.float32), 'edge_index': jax.random.randint(ks[2], (2, E), 0, N, jnp.int32), 'W_e': jax.random.normal(ks[3], (ED, H), jnp.float32) * s(ED), 'b_e': jnp.zeros((H,), jnp.float32), 'W1': jax.random.normal(ks[4], (H, 2 * H), jnp.float32) * s(H), 'b1': jnp.zeros((2 * H,), jnp.float32), 'g1': jnp.ones((2 * H,), jnp.float32), 'beta1': jnp.zeros((2 * H,), jnp.float32), 'W2': jax.random.normal(ks[5], (2 * H, H), jnp.float32) * s(2 * H), 'b2': jnp.zeros((H,), jnp.float32), 'g2': jnp.ones((H,), jnp.float32), 'beta2': jnp.zeros((H,), jnp.float32), 'eps': jnp.zeros((), jnp.float32)}
    _L1_gnn_all = _L1_gnn_setup()
    _L1_gnn_in = {k: v for k, v in _L1_gnn_all.items() if k in ('W_e', 'b_e', 'W1', 'b1', 'g1', 'beta1', 'W2', 'b2', 'g2', 'beta2', 'eps')}
    del _L1_gnn_all
    return {'x': x, 'src': src, 'dst': dst, 'edge_attr_64': edge_attr_64, 'L0_gnn_ln1_g': _L0_gnn_in['ln1_g'], 'L0_gnn_ln1_b': _L0_gnn_in['ln1_b'], 'L0_gnn_Wl': _L0_gnn_in['Wl'], 'L0_gnn_Wr': _L0_gnn_in['Wr'], 'L0_gnn_att': _L0_gnn_in['att'], 'L0_gnn_gat_bias': _L0_gnn_in['gat_bias'], 'L0_gnn_ln2_g': _L0_gnn_in['ln2_g'], 'L0_gnn_ln2_b': _L0_gnn_in['ln2_b'], 'L0_gnn_W1': _L0_gnn_in['W1'], 'L0_gnn_b1': _L0_gnn_in['b1'], 'L0_gnn_W2': _L0_gnn_in['W2'], 'L0_gnn_b2': _L0_gnn_in['b2'], 'L1_gnn_W_e': _L1_gnn_in['W_e'], 'L1_gnn_b_e': _L1_gnn_in['b_e'], 'L1_gnn_W1': _L1_gnn_in['W1'], 'L1_gnn_b1': _L1_gnn_in['b1'], 'L1_gnn_g1': _L1_gnn_in['g1'], 'L1_gnn_beta1': _L1_gnn_in['beta1'], 'L1_gnn_W2': _L1_gnn_in['W2'], 'L1_gnn_b2': _L1_gnn_in['b2'], 'L1_gnn_g2': _L1_gnn_in['g2'], 'L1_gnn_beta2': _L1_gnn_in['beta2'], 'L1_gnn_eps': _L1_gnn_in['eps']}

def reference(x, src, dst, edge_attr_64, L0_gnn_ln1_g, L0_gnn_ln1_b, L0_gnn_Wl, L0_gnn_Wr, L0_gnn_att, L0_gnn_gat_bias, L0_gnn_ln2_g, L0_gnn_ln2_b, L0_gnn_W1, L0_gnn_b1, L0_gnn_W2, L0_gnn_b2, L1_gnn_W_e, L1_gnn_b_e, L1_gnn_W1, L1_gnn_b1, L1_gnn_g1, L1_gnn_beta1, L1_gnn_W2, L1_gnn_b2, L1_gnn_g2, L1_gnn_beta2, L1_gnn_eps):
    import jax
    import jax.numpy as jnp

    def _L0_gnn_ref(x, edge_index, ln1_g, ln1_b, Wl, Wr, att, gat_bias, ln2_g, ln2_b, W1, b1, W2, b2):
        import jax, jax.numpy as jnp
        import numpy as np
        N_EMBD = 512
        HEADS = 8
        C = N_EMBD // HEADS
        N_NODES = 1250
        N_EDGES = 20000
        NEG_SLOPE = 0.2
        LN_EPS = 1e-05

        def _layer_norm(x, g, b):
            mu = jnp.mean(x, axis=-1, keepdims=True)
            var = jnp.mean(jnp.square(x - mu), axis=-1, keepdims=True)
            return (x - mu) * jax.lax.rsqrt(var + LN_EPS) * g + b

        def _gatv2(x, edge_index, Wl, Wr, att, gat_bias):
            src, dst = (edge_index[0], edge_index[1])
            xl = (x @ Wl).reshape(-1, HEADS, C)
            xr = (x @ Wr).reshape(-1, HEADS, C)
            h = jax.nn.leaky_relu(xl[src] + xr[dst], NEG_SLOPE)
            e = jnp.einsum('ehc,hc->eh', h, att)
            m = jax.ops.segment_max(e, dst, num_segments=N_NODES)
            ex = jnp.exp(e - m[dst])
            denom = jax.ops.segment_sum(ex, dst, num_segments=N_NODES)
            alpha = ex / (denom[dst] + 1e-16)
            msg = alpha[..., None] * xl[src]
            out = jax.ops.segment_sum(msg, dst, num_segments=N_NODES)
            return out.reshape(-1, HEADS * C) + gat_bias
        h = _layer_norm(x, ln1_g, ln1_b)
        h = _gatv2(h, edge_index, Wl, Wr, att, gat_bias)
        x = x + h
        h = _layer_norm(x, ln2_g, ln2_b)
        h = jax.nn.gelu(h @ W1 + b1, approximate=False) @ W2 + b2
        return x + h

    def _L1_gnn_ref(x, edge_attr, edge_index, W_e, b_e, W1, b1, g1, beta1, W2, b2, g2, beta2, eps):
        import jax, jax.numpy as jnp
        import numpy as np
        N, E, H, ED = (6250, 50000, 512, 64)
        BN_EPS = 1e-05

        def _bn(h, g, b):
            mu = jnp.mean(h, axis=0)
            var = jnp.mean(jnp.square(h - mu), axis=0)
            return (h - mu) * jax.lax.rsqrt(var + BN_EPS) * g + b
        src, dst = (edge_index[0], edge_index[1])
        msg = jax.nn.relu(x[src] + edge_attr @ W_e + b_e)
        aggr = jax.ops.segment_sum(msg, dst, num_segments=x.shape[0])
        h = (1.0 + eps) * x + aggr
        h = jax.nn.silu(_bn(h @ W1 + b1, g1, beta1))
        h = h @ W2 + b2
        return jax.nn.silu(_bn(h, g2, beta2))
    edge_index = jnp.stack([src, dst])
    x = _layernorm(x + _L0_gnn_ref(x, edge_index, L0_gnn_ln1_g, L0_gnn_ln1_b, L0_gnn_Wl, L0_gnn_Wr, L0_gnn_att, L0_gnn_gat_bias, L0_gnn_ln2_g, L0_gnn_ln2_b, L0_gnn_W1, L0_gnn_b1, L0_gnn_W2, L0_gnn_b2), axis=-1)
    x = _layernorm(x + _L1_gnn_ref(x, edge_attr_64, edge_index, L1_gnn_W_e, L1_gnn_b_e, L1_gnn_W1, L1_gnn_b1, L1_gnn_g1, L1_gnn_beta1, L1_gnn_W2, L1_gnn_b2, L1_gnn_g2, L1_gnn_beta2, L1_gnn_eps), axis=-1)
    return x

_drawn_inputs = setup_inputs


def setup_inputs(seed=0):
    import zlib

    import numpy as np

    out = dict(_drawn_inputs(seed))
    spreads = {'L0_gnn_ln1_g': (1.0, 0.6),
     'L0_gnn_ln1_b': (0.0, 0.366),
     'L0_gnn_gat_bias': (0.0, 0.1),
     'L0_gnn_ln2_g': (1.0, 0.6),
     'L0_gnn_ln2_b': (0.0, 0.64),
     'L0_gnn_b1': (0.0, 0.313),
     'L0_gnn_b2': (0.0, 0.1),
     'L1_gnn_b_e': (0.0, 0.1),
     'L1_gnn_b1': (0.0, 0.8),
     'L1_gnn_g1': (1.0, 0.2),
     'L1_gnn_beta1': (0.0, 0.1),
     'L1_gnn_b2': (0.0, 0.8),
     'L1_gnn_g2': (1.0, 0.2),
     'L1_gnn_beta2': (0.0, 0.1)}
    factors = {'L0_gnn_Wr': 8.0, 'L0_gnn_att': 8.0}
    for name, (base, spread) in spreads.items():
        noise = np.random.default_rng([zlib.crc32(name.encode()), seed]).standard_normal(out[name].shape)
        drawn = base * np.exp(spread * noise) if base else spread * noise
        out[name] = jnp.asarray(drawn.astype(out[name].dtype))
    for name, factor in factors.items():
        out[name] = (out[name] * factor).astype(out[name].dtype)
    return out
```

```python
from contextlib import ExitStack

import numpy as np

import concourse.bass as bass
from concourse import mybir

P = 128
N, D, E = 1250, 512, 40000
H = 8
C = D // H
FC = D // P
ED = 64
F1 = 2048
F2 = 1024
NT = (N + P - 1) // P
NP = NT * P
LAST = N - (NT - 1) * P
TPG = 4
GE = TPG * P
NG = (E + NT * (GE - 1)) // GE
NG += NG % 2
T = NG * TPG
UN = 2 * TPG
Q = NG // 2
RW = D + H
EP = E + GE
PAD_DST = 4000
KEY = 4096
CH = P // H
CT = T // CH
CL = CT * P
BIG = 1.0e30
LN_EPS = 1e-5
MAXK = (E + GE - 1) // GE + 1

ALU = mybir.AluOpType
ACT = mybir.ActivationFunctionType
F32 = mybir.dt.float32
FR = mybir.dt.float32r
I32 = mybir.dt.int32
AX = mybir.AxisListType.X


def need(eng, sem, n):
    if not isinstance(n, int) or n > 0:
        eng.wait_ge(sem, n)


def gnn_kernel(nc, x, src, dst, ea, ln1_g, ln1_b, Wl, Wr, att, gat_bias, ln2_g, ln2_b, W1, b1, W2, b2,
               W_e, b_e, V1, c1, g1, beta1, V2, c2, g2, beta2, eps, out):
    with ExitStack() as ctx:
        def sem(name):
            return ctx.enter_context(nc.semaphore(name))

        def dram(name, shape, dt=F32):
            return nc.dram_tensor(name, shape, dt).ap()

        src_pad, dst_pad = dram("src_pad", [EP], I32), dram("dst_pad", [EP], I32)
        ea_pad = dram("ea_pad", [EP, ED])
        grp_dst, grp_src = dram("grp_dst", [NG, GE], I32), dram("grp_src", [NG, GE], I32)
        xl_tab, x2_tab = dram("xl_tab", [NP, RW]), dram("x2_tab", [NP, D])

        def put(region, name, shape, dt=F32):
            size = int(np.prod(shape[1:])) * 4
            t = nc.alloc_sbuf_tensor_at(name, shape, dt, offset=region[0])
            region[0] += (size + 31) // 32 * 32
            return t

        base = [17408]
        ident = put(base, "ident", [P, P])
        iota = put(base, "iota", [P, P])
        iota_i = put(base, "iota_i", [P, P], I32)
        ones = put(base, "ones", [P, P])
        x_sb = put(base, "x_sb", [P, NT, D])
        acc = put(base, "acc", [P, NT, RW])
        e_all = put(base, "e_all", [P, T * H])
        drel = put(base, "drel", [P, T])
        src_idx = put(base, "src_idx", [P, T], I32)
        key = put(base, "key", [P, T])
        ng_i = put(base, "ng_i", [1, NG], I32)
        s_i = put(base, "s_i", [1, NG], I32)
        idx_stage = put(base, "idx_stage", [P, UN], I32)
        PAR = (("ln1_g", ln1_g, FC), ("ln1_b", ln1_b, FC), ("att", att.rearrange("h c -> (h c)"), FC),
               ("ln2_g", ln2_g, FC), ("ln2_b", ln2_b, FC), ("b1", b1, F1 // P), ("c1", c1, F2 // P), ("g1", g1, F2 // P),
               ("beta1", beta1, F2 // P), ("c2", c2, FC), ("g2", g2, FC), ("beta2", beta2, FC))
        NPAR = sum(k for _, _, k in PAR)
        par_row = put(base, "par_row", [NPAR, P])
        par = put(base, "par", [P, NPAR])
        par_at, at = {}, 0
        for name, _, k in PAR:
            par_at[name] = (at, at + k)
            at += k
        (ln1gc, ln1bc, attc, ln2gc, ln2bc, b1c, c1c, g1c, be1c, c2c, g2c, be2c) = (
            par[:, lo_:hi_] for lo_, hi_ in par_at.values())
        attblk = put(base, "attblk", [P, FC, 2])
        epsc = put(base, "epsc", [P, 1])
        att_bc = put(base, "att_bc", [P, D])
        gb_bc, b2_bc, be_bc = (put(base, n, [P, D]) for n in ("gb_bc", "b2_bc", "be_bc"))
        shift_dn, shift_up = put(base, "shift_dn", [P, P]), put(base, "shift_up", [P, P])
        stats = put(base, "stats", [P, NT, 6])
        mv = put(base, "mv", [P, NT, 2])
        rstd = put(base, "rstd", [P, NT])
        bnst = put(base, "bnst", [P, F2 // P, 3, 6])
        bnmv = put(base, "bnmv", [P, F2 // P, 2])
        bnsc, bnsh = put(base, "bnsc", [P, F2 // P]), put(base, "bnsh", [P, F2 // P])
        cols = put(base, "cols", [P, 16])
        hT = put(base, "hT", [P, FC, NP])
        lo = base[0]
        ring = [lo]
        gat = put(ring, "gat", [P, UN, RW])
        onehot = put(ring, "onehot", [P, 2, TPG, P])
        onehotT = put(ring, "onehotT", [P, 2, GE], FR)
        zbuf = put(ring, "zbuf", [P, UN, RW])
        zrel = put(ring, "zrel", [P, 2, D])
        slin = put(ring, "slin", [P, 2, TPG, H])
        ea_g = put(ring, "ea_g", [P, 2, TPG * ED])
        eaT = put(ring, "eaT", [P, 2, 2, P])
        We2 = put(ring, "We2", [P, D])
        hi = ring[0]
        ra = [hi]
        xr_hi = put(ra, "xr_hi", [P, NT, RW], FR)
        xr_lo = put(ra, "xr_lo", [P, NT, RW], FR)
        ra_end = ra[0]
        Wlr = put(ra, "Wlr", [P, 2, FC, D])
        zt = put(ra, "zt", [P, 2, D])
        rs = [lo]
        dst_i = put(rs, "dst_i", [P, E // 125], I32)
        dst_f = put(rs, "dst_f", [P, E // 125])
        cmp = put(rs, "cmp", [P, NT, E // 125])
        bounds_i = put(rs, "bounds_i", [P, 16], I32)
        bounds = put(rs, "bounds", [P, 16])
        cnt = put(rs, "cnt", [P, 16])
        iotaK_i, iotaK = put(rs, "iotaK_i", [1, P], I32), put(rs, "iotaK", [1, P])
        rows = put(rs, "rows", [1, 12, 16])
        kcmp = put(rs, "kcmp", [1, NT, MAXK])
        gcmp = put(rs, "gcmp", [1, NG, NT])
        gprod = put(rs, "gprod", [1, NG, NT])
        ngf, sf = put(rs, "ngf", [1, NG]), put(rs, "sf", [1, NG])
        ngb = put(rs, "ngb", [P, NG])
        xl_sb = put(rs, "xl_sb", [P, 2, RW])
        prod = put(rs, "prod", [P, 2, D])
        srow = put(rs, "srow", [P, 2, H])
        pads_i = put(rs, "pads_i", [4, GE // 4], I32)
        padz_i = put(rs, "padz_i", [4, GE // 4], I32)
        padz = put(rs, "padz", [P, GE * ED // P])
        rl = [rs[0]]
        lst_i = put(rl, "lst_i", [NG, 2, GE], I32)
        lst_f = put(rl, "lst_f", [NG, 2, GE])
        dcol = put(rl, "dcol", [P, T])
        assert rl[0] <= hi, (rl[0], hi)
        rb = [hi]
        X, KX, fwd, bwd = (put(rb, n, [P, CL]) for n in ("X", "KX", "fwd", "bwd"))
        pen = put(rb, "pen", [P, CL + 16])
        perm = fwd
        permk = bwd
        rowbuf = put(rb, "rowbuf", [1, 6, P])
        rw = [hi]
        W1_sb = put(rw, "W1_sb", [P, FC, F1])
        W2_sb = put(rw, "W2_sb", [P, F1 // P, D])
        rh = [lo]
        hid = put(rh, "hid", [P, F1 // P, D])
        lnz = put(rh, "lnz", [P, 2, D])
        assert rh[0] <= hi, (rh[0], hi)
        vrow = put([lo], "vrow", [P, NT, D])
        rv = [hi]
        V1_sb = put(rv, "V1_sb", [P, FC, F2])
        uT = put(rv, "uT", [P, F2 // P, NP])
        rv2 = [lo]
        yT = put(rv2, "yT", [P, FC, NP])
        fin = put(rv2, "fin", [P, 2, D])
        V2_sb = put(rv2, "V2_sb", [P, F2 // P, D])
        assert rv2[0] <= hi, (rv2[0], hi)
        end = max(r[0] for r in (ra, rb, rw, rv))
        assert end <= 229344, (lo, hi, end)

        ps = ctx.enter_context(nc.psum_tensor("ps", [P, 8, D], F32))
        psf = ps[:].rearrange("p b n -> p (b n)")
        ps_row = [psf[:, 2 * s * D:2 * s * D + RW] for s in range(2)]

        names = """x_in dst_in wqkv_in par_in bc_in pad_in cst cstv cnt_ready rp_ready tab_ready ngb_ready lists_written
        lists_in lists_f listT lists_ready ln1 zt_ready ztT hT_ready xl_mm xr_mm xl_cp xr_cp xl_dve xr_dve
        ot_p ot_ready o_ready xr_done z_ready t_done relu_done a_done e_done
        perm_ready xk_p xk_ready pen_ready chain colp_p colp rowp rowv carry_p carry carry_c m_ready ex_ready exT ex_back
        o2_ready msg_ready agg_done acc_done x1_ready w_in ln2 z2_ready z2T h2T_ready f1_mm hid_ready f2_mm u_ready
        x2_ready x2_stored we_in v2_in ea_p ea_ready tw_done t_ready m2_ready o3_ready ag2_done acc2_done v_in hhT_p hhT_ready
        u_mm u_cp bn1 bn1s sT_ready y_mm y_cp bn2 bn2s yT_ready yb_p v_ready ln4 fin_ready
        gate dvec par_T par_ready""".split()
        S = {n: sem(n) for n in names}
        gath = {ph: [sem(f"gath_{ph}{i}") for i in range(UN)] for ph in "acd"}
        staged = {ph: sem(f"staged_{ph}") for ph in "acd"}
        ea_in = [sem(f"ea_in{i}") for i in range(2)]
        xl_stored = [sem(f"xl_stored{i}") for i in range(2)]
        out_stored = [sem(f"out_stored{i}") for i in range(2)]
        x_tile = [sem(f"x_tile{t}") for t in range(NT)]
        block = ctx.enter_context(nc.Block())

        @block.sync
        def _(sp):
            sp.dma_start(dst_i[0:125, :], dst.rearrange("(p f) -> p f", p=125)).then_inc(S["dst_in"], 16)
            sp.wait_ge(S["cst"], 1)
            for t in range(NT):
                r = P if t < NT - 1 else LAST
                sp.dma_start(x_sb[0:r, t, :], x[t * P:t * P + r, :]).then_inc(x_tile[t], 16)
            sp.dma_start(Wlr[:, 0], Wl.rearrange("(c p) n -> p c n", p=P)).then_inc(S["wqkv_in"], 16)
            sp.dma_start(Wlr[:, 1], Wr.rearrange("(c p) n -> p c n", p=P)).then_inc(S["wqkv_in"], 16)
            k = 320
            sp.dma_start(ea_pad[0:E, :].rearrange("(a b) c -> a (b c)", a=k),
                         ea.rearrange("(a b) c -> a (b c)", a=k)).then_inc(S["pad_in"], 16)
            sp.wait_ge(S["tab_ready"], 1)
            sp.wait_ge(S["pad_in"], 6 * 16)
            with sp.Fori(0, NG) as g:
                s = sp.value_load(s_i[0:1, bass.ds(g, 1)], min_val=0, max_val=E)
                sp.dma_start(grp_dst[bass.ds(g, 1), :],
                             dst_pad[bass.ds(s, GE)].rearrange("(a n) -> a n", a=1)).then_inc(S["lists_written"], 16)
            sp.wait_ge(S["lists_written"], 2 * NG * 16)
            sp.dma_start(lst_i[:, 0, :], grp_dst[:, :]).then_inc(S["lists_in"], 16)
            sp.dma_start(lst_i[:, 1, :], grp_src[:, :]).then_inc(S["lists_in"], 16)
            for t in range(NT):
                sp.wait_ge(S["xl_cp"], t + 1)
                sp.wait_ge(S["xl_dve"], t + 1)
                sp.dma_start(xl_tab[t * P:(t + 1) * P, :], xl_sb[:, t % 2, :]).then_inc(xl_stored[t % 2], 16)
            sp.wait_ge(S["ex_back"], 6)
            sp.dma_start(W1_sb[:], W1.rearrange("(c p) n -> p c n", p=P)).then_inc(S["w_in"], 16)
            sp.dma_start(W2_sb[:], W2.rearrange("(c p) n -> p c n", p=P)).then_inc(S["w_in"], 16)
            for t in range(NT):
                sp.wait_ge(S["x2_ready"], t + 1)
                sp.dma_start(x2_tab[t * P:(t + 1) * P, :], vrow[:, t, :]).then_inc(S["x2_stored"], 16)
            for half in range(2):
                sp.dma_start(We2[half * ED:(half + 1) * ED, :], W_e[:, :]).then_inc(S["we_in"], 16)
            sp.dma_start(V1_sb[:], V1.rearrange("(c p) n -> p c n", p=P)).then_inc(S["v_in"], 16)

            def edge_features(q):
                for h in range(2):
                    need(sp, S["ea_p"], 2 * q + h - 1)
                    s = sp.value_load(s_i[0:1, bass.ds(2 * q + h, 1)], min_val=0, max_val=E)
                    sp.dma_start(ea_g[:, h, :].rearrange("p (k c) -> p k c", k=TPG),
                                 ea_pad[bass.ds(s, GE), :].rearrange("(k p) c -> p k c", p=P)).then_inc(ea_in[h], 16)

            edge_features(0)
            with sp.Fori(1, Q) as q:
                edge_features(q)
            sp.wait_ge(S["acc2_done"], NG)
            sp.dma_start(V2_sb[:], V2.rearrange("(c p) n -> p c n", p=P)).then_inc(S["v2_in"], 16)
            for t in range(NT):
                r = P if t < NT - 1 else LAST
                sp.wait_ge(S["fin_ready"], t + 1)
                sp.dma_start(out[t * P:t * P + r, :], fin[0:r, t % 2, :]).then_inc(out_stored[t % 2], 16)
            for half in out_stored:
                sp.wait_ge(half, NT // 2 * 16)

        @block.gpsimd
        def _(pool):
            g = nc.gpsimd
            g.memset(x_sb[:, NT - 1, :], 0.0).then_inc(S["cst"], 1)
            g.memset(xr_hi[:, NT - 1, :].bitcast(F32), 0.0).then_inc(S["cst"], 1)
            g.memset(xr_lo[:, NT - 1, :].bitcast(F32), 0.0).then_inc(S["cst"], 1)
            g.memset(pads_i[:], PAD_DST).then_inc(S["cst"], 1)
            g.memset(padz_i[:], 0).then_inc(S["cst"], 1)
            g.memset(padz[:], 0.0).then_inc(S["cst"], 1)
            g.iota(iota_i[:], pattern=[[1, P]], base=0, channel_multiplier=0).then_inc(S["cst"], 1)
            g.iota(bounds_i[:], pattern=[[P, 16]], base=0, channel_multiplier=0).then_inc(S["cst"], 1)
            g.iota(iotaK_i[:], pattern=[[GE, P]], base=0, channel_multiplier=0).then_inc(S["cst"], 1)
            g.memset(ident[:], 1.0).then_inc(S["cst"], 1)
            g.memset(shift_dn[:], 1.0).then_inc(S["cst"], 1)
            g.memset(shift_up[:], 1.0).then_inc(S["cst"], 1)
            pool.wait_ge(S["cst"], 12)
            for m, off in ((ident, 0), (shift_dn, H), (shift_up, -H)):
                g.affine_select(out=m[:], in_=m[:], compare_op=ALU.is_equal, fill=0.0, base=off,
                                pattern=[[-1, P]], channel_multiplier=1).then_inc(S["cst"], 1)
            for t_, a in ((att_bc, att.rearrange("h c -> (h c)")), (gb_bc, gat_bias), (b2_bc, b2), (be_bc, b_e)):
                g.dma_start(t_[:], a.partition_broadcast(P)).then_inc(S["bc_in"], 16)
            g.dma_start(epsc[:], eps.partition_broadcast(P)).then_inc(S["bc_in"], 16)

            def gather(q, ph, table, width, consumed):
                for h in range(2):
                    need(pool, consumed, UN * q + TPG * h + TPG - UN)
                    g.tensor_copy(idx_stage[:, TPG * h:TPG * (h + 1)],
                                  src_idx[:, bass.ds(UN * q + TPG * h, TPG)]).then_inc(staged[ph], 1)
                    pool.wait_ge(staged[ph], 2 * q + h + 1)
                    pool.sem_inc(S["gate"], 1)
                    for k in range(TPG * h, TPG * (h + 1)):
                        g.indirect_dma_start(
                            out=gat[:, k, 0:width], out_offset=None, in_=table[:, :],
                            in_offset=bass.IndirectOffsetOnAxis(ap=idx_stage[:, k:k + 1], axis=0),
                        ).then_inc(gath[ph][k], 16)

            pool.wait_ge(S["lists_ready"], 2)
            for half in xl_stored:
                pool.wait_ge(half, NT // 2 * 16)
            gather(0, "a", xl_tab, RW, S["z_ready"])
            with pool.Fori(1, Q) as q:
                gather(q, "a", xl_tab, RW, S["z_ready"])
            pool.wait_ge(S["z_ready"], T)
            gather(0, "c", xl_tab, RW, S["msg_ready"])
            with pool.Fori(1, Q) as q:
                gather(q, "c", xl_tab, RW, S["msg_ready"])
            pool.wait_ge(S["x2_stored"], NT * 16)
            gather(0, "d", x2_tab, D, S["t_ready"])
            with pool.Fori(1, Q) as q:
                gather(q, "d", x2_tab, D, S["t_ready"])

        @block.scalar
        def _(act):
            a = nc.scalar
            for name, v, _ in PAR:
                r0, r1 = par_at[name]
                act.dma_start(par_row[r0:r1, :], v.rearrange("(c p) -> c p", p=P)).then_inc(S["par_in"], 16)
            act.dma_start(src_pad[0:E].rearrange("(p f) -> p f", p=16),
                          src.rearrange("(p f) -> p f", p=16)).then_inc(S["pad_in"], 16)
            act.dma_start(dst_pad[0:E].rearrange("(p f) -> p f", p=16),
                          dst.rearrange("(p f) -> p f", p=16)).then_inc(S["pad_in"], 16)
            act.wait_ge(S["cst"], 9)
            act.dma_start(dst_pad[E:EP].rearrange("(p f) -> p f", p=4), pads_i[:]).then_inc(S["pad_in"], 16)
            act.dma_start(src_pad[E:EP].rearrange("(p f) -> p f", p=4), padz_i[:]).then_inc(S["pad_in"], 16)
            act.dma_start(ea_pad[E:EP, :].rearrange("(p f) c -> p (f c)", p=P), padz[:]).then_inc(S["pad_in"], 16)
            act.wait_ge(S["tab_ready"], 1)
            act.wait_ge(S["pad_in"], 6 * 16)
            with act.Fori(0, NG) as g:
                s = act.value_load(s_i[0:1, bass.ds(g, 1)], min_val=0, max_val=E)
                act.dma_start(grp_src[bass.ds(g, 1), :],
                              src_pad[bass.ds(s, GE)].rearrange("(a n) -> a n", a=1)).then_inc(S["lists_written"], 16)

            def ln_root(ready, n):
                act.wait_ge(ready, n)
                a.activation(rstd[:], rstd[:], ACT.Sqrt).then_inc(ready, 1)

            def affine_T(t, bank, mm, gcol, bcol, ready):
                act.wait_ge(mm, t + 1)
                for c in range(FC):
                    i = a.activation(hT[:, c, t * P:(t + 1) * P], ps[:, bank, c * P:(c + 1) * P], ACT.Identity,
                                     bias=bcol[:, c:c + 1], scale=gcol[:, c:c + 1])
                i.then_inc(ready, 1)

            ln_root(S["ln1"], 3)
            act.wait_ge(S["par_ready"], 1)
            for t in range(NT + 1):
                if t < NT:
                    affine_T(t, t % 2, S["ztT"], ln1gc, ln1bc, S["hT_ready"])
                if t > 0:
                    u = t - 1
                    act.wait_ge(S["xl_mm"], u + 1)
                    if u >= 2:
                        act.wait_ge(xl_stored[u % 2], 16 * (u // 2))
                    a.copy(xl_sb[:, u % 2, 0:D], ps[:, 2 + u % 2, :]).then_inc(S["xl_cp"], 1)
                    act.wait_ge(S["xr_mm"], u + 1)
                    if u == NT - 1:
                        act.wait_ge(S["cst"], 3)
                    a.copy(xr_hi[:, u, 0:D], ps[:, 4 + u % 2, :]).then_inc(S["xr_cp"], 1)

            def transposed_onehot(G, h):
                act.wait_ge(S["ot_p"], G + 1)
                need(act, S["a_done"], TPG * (G - 2) + TPG)
                a.copy(onehotT[:, h, :], ps[:, 4, :]).then_inc(S["ot_ready"], 1)

            def rectify(q, first, last):
                for u in range(UN):
                    i, G, h = UN * q + u, 2 * q + u // TPG, u // TPG
                    if u % TPG == 1 and not (last and h == 1):
                        transposed_onehot(G + 1, 1 - h)
                    act.wait_ge(S["t_done"], i + 1)
                    need(act, S["a_done"], i - 1)
                    a.activation(zrel[:, u % 2, :], ps[:, 2 + u % 2, :], ACT.Relu).then_inc(S["relu_done"], 1)

            transposed_onehot(0, 0)
            rectify(0, True, False)
            with act.Fori(1, Q - 1) as q:
                rectify(q, False, False)
            rectify(Q - 1, False, True)

            for b in range(6):
                w = min(4, CT - 4 * b) * P
                act.wait_ge(S["xk_p"], 2 * b + 1)
                a.copy(X[:, b * D:b * D + w], ps[:, (2 * b) % 8, 0:w]).then_inc(S["xk_ready"], 1)
                act.wait_ge(S["xk_p"], 2 * b + 2)
                a.copy(KX[:, b * D:b * D + w], ps[:, (2 * b + 1) % 8, 0:w]).then_inc(S["xk_ready"], 1)
            act.wait_ge(S["m_ready"], 1)
            a.activation(X[:], X[:], ACT.Exp).then_inc(S["ex_ready"], 1)

            ln_root(S["ln2"], 3)
            for t in range(NT):
                affine_T(t, t % 2, S["z2T"], ln2gc, ln2bc, S["h2T_ready"])
            n = 0
            for ch in range(3):
                w = min(D, NP - ch * D)
                if ch:
                    act.wait_ge(S["f2_mm"], TPG * ch)
                for f in range(F1 // P):
                    act.wait_ge(S["f1_mm"], n + 1)
                    a.activation(hid[:, f, 0:w], ps[:, 2 + n % 2, 0:w], ACT.Gelu,
                                 bias=b1c[:, f:f + 1]).then_inc(S["hid_ready"], 1)
                    n += 1
            ln_root(S["ln2"], 7)

            def edge_T(G, h):
                act.wait_ge(S["ea_p"], G + 1)
                need(act, S["tw_done"], TPG * (G - 2) + TPG)
                a.copy(eaT[:, h, :, :].rearrange("p a b -> p (a b)"), ps[:, 6, 0:2 * P]).then_inc(S["ea_ready"], 1)

            def messages(q, first, last):
                for u in range(UN):
                    i, G, h = UN * q + u, 2 * q + u // TPG, u // TPG
                    if u % TPG == 1 and not (last and h == 1):
                        edge_T(G + 1, 1 - h)
                    act.wait_ge(S["t_ready"], i + 1)
                    need(act, S["ag2_done"], i - 3)
                    a.activation(zbuf[:, 4 + u % 4, 0:D], zbuf[:, u % 4, 0:D], ACT.Relu).then_inc(S["m2_ready"], 1)

            edge_T(0, 0)
            messages(0, True, False)
            with act.Fori(1, Q - 1) as q:
                messages(q, False, False)
            messages(Q - 1, False, True)

            for t in range(NT):
                act.wait_ge(S["hhT_p"], t + 1)
                a.copy(hT[:, :, t * P:(t + 1) * P], ps[:, t % 2, :].rearrange("p (c n) -> p c n", c=FC)).then_inc(S["hhT_ready"], 1)
            n = 0
            for f in range(F2 // P):
                for ch in range(3):
                    w = min(D, NP - ch * D)
                    act.wait_ge(S["u_mm"], n + 1)
                    a.activation(uT[:, f, ch * D:ch * D + w], ps[:, 2 + n % 2, 0:w], ACT.Identity,
                                 bias=c1c[:, f:f + 1]).then_inc(S["u_cp"], 1)
                    n += 1
            act.wait_ge(S["bn1"], 4)
            a.activation(bnsc[:], bnsc[:], ACT.Sqrt).then_inc(S["bn1"], 1)
            act.wait_ge(S["bn1s"], 1)
            for f in range(F2 // P):
                a.activation(uT[:, f, :], uT[:, f, :], ACT.Silu, bias=bnsh[:, f:f + 1],
                             scale=bnsc[:, f:f + 1]).then_inc(S["sT_ready"], 1)
            n = 0
            for f in range(FC):
                for ch in range(3):
                    w = min(D, NP - ch * D)
                    act.wait_ge(S["y_mm"], n + 1)
                    a.activation(yT[:, f, ch * D:ch * D + w], ps[:, 4 + n % 2, 0:w], ACT.Identity,
                                 bias=c2c[:, f:f + 1]).then_inc(S["y_cp"], 1)
                    n += 1
            act.wait_ge(S["bn2"], 4)
            a.activation(bnsc[:, 0:FC], bnsc[:, 0:FC], ACT.Sqrt).then_inc(S["bn2"], 1)
            act.wait_ge(S["bn2s"], 1)
            for f in range(FC):
                a.activation(yT[:, f, :], yT[:, f, :], ACT.Silu, bias=bnsh[:, f:f + 1],
                             scale=bnsc[:, f:f + 1]).then_inc(S["yT_ready"], 1)
            ln_root(S["ln4"], 3)

        @block.vector
        def _(dve):
            v = nc.vector
            count = [0]

            def link(ins):
                count[0] += 1
                ins.then_inc(S["dvec"], 1)
                dve.wait_ge(S["dvec"], count[0])

            v.memset(ones[:], 1.0).then_inc(S["cstv"], 1)
            dve.wait_ge(S["cst"], 9)
            link(v.tensor_copy(iota[:], iota_i[:]))
            link(v.tensor_copy(bounds[:], bounds_i[:]))
            link(v.tensor_copy(iotaK[:], iotaK_i[:]))
            dve.wait_ge(S["dst_in"], 16)
            link(v.tensor_copy(dst_f[0:125, :], dst_i[0:125, :]))
            link(v.tensor_tensor(cmp[0:125], dst_f[0:125, :].unsqueeze(1).broadcast_to([125, NT, E // 125]),
                                 bounds[0:125, 0:NT].unsqueeze(2).broadcast_to([125, NT, E // 125]), ALU.is_lt))
            v.tensor_reduce(cnt[0:125, 0:NT], cmp[0:125], AX, ALU.add).then_inc(S["cnt_ready"], 1)
            rp, cn, kn, ginc, gexc, bs, db, zr = (rows[:, j, 0:NT] for j in range(8))
            link(v.memset(rows[:], 0.0))
            dve.wait_ge(S["rp_ready"], 1)
            link(v.tensor_copy(rp, ps[0:1, 7, 0:NT]))
            link(v.memset(rows[:, 0, NT:NT + 1], float(E)))
            link(v.tensor_tensor(cn, rows[:, 0, 1:NT + 1], rp, ALU.subtract))
            link(v.tensor_tensor(kcmp[:], cn.unsqueeze(2).broadcast_to([1, NT, MAXK]),
                                 iotaK[:, 0:MAXK].unsqueeze(1).broadcast_to([1, NT, MAXK]), ALU.is_gt))
            link(v.tensor_reduce(kn, kcmp[:], AX, ALU.add))
            link(v.tensor_tensor_scan(ginc, kn, zr, 0.0, ALU.add, ALU.add))
            link(v.tensor_tensor(gexc, ginc, kn, ALU.subtract))
            link(v.scalar_tensor_tensor(bs, gexc, -float(GE), rp, ALU.mult, ALU.add))
            link(v.tensor_copy(rows[:, 6, 0:1], rows[:, 5, 0:1]))
            link(v.tensor_tensor(rows[:, 6, 1:NT], rows[:, 5, 1:NT], rows[:, 5, 0:NT - 1], ALU.subtract))
            link(v.tensor_tensor(gcmp[:], iota[0:1, 0:NG].unsqueeze(2).broadcast_to([1, NG, NT]),
                                 gexc.unsqueeze(1).broadcast_to([1, NG, NT]), ALU.is_ge))
            link(v.tensor_tensor(gprod[:], gcmp[:], db.unsqueeze(1).broadcast_to([1, NG, NT]), ALU.mult))
            link(v.tensor_reduce(ngf[:], gcmp[:], AX, ALU.add))
            link(v.tensor_scalar(ngf[:], ngf[:], -1.0, None, ALU.add))
            link(v.tensor_reduce(sf[:], gprod[:], AX, ALU.add))
            link(v.tensor_tensor(sf[:], sf[:], iotaK[:, 0:NG], ALU.add))
            link(v.tensor_scalar(sf[:], sf[:], float(E), None, ALU.min))
            link(v.tensor_copy(ng_i[:], ngf[:]))
            v.tensor_copy(s_i[:], sf[:]).then_inc(S["tab_ready"], 1)
            dve.wait_ge(S["par_T"], 1)
            v.tensor_copy(par[:], ps[:, 7, P:P + NPAR]).then_inc(S["par_ready"], 1)
            dve.wait_ge(S["par_ready"], 1)
            link(v.memset(attblk[:], 0.0))
            for i in range(2):
                v.tensor_scalar(attblk[i * C:(i + 1) * C, :, i], attc[i * C:(i + 1) * C, :], 0.8, None,
                                ALU.mult).then_inc(S["cstv"], 1)
            dve.wait_ge(S["bc_in"], 5 * 16)
            link(v.tensor_scalar(att_bc[:], att_bc[:], 0.2, None, ALU.mult))

            def ln_stats(srcs, lnsem, n0, waits=None):
                for t in range(NT):
                    if waits:
                        waits(t)
                    i = v.bn_stats(stats[:, t, :], srcs(t))
                link(i)
                for t in range(NT):
                    i = v.bn_aggr(mv[:, t, :], stats[:, t, :])
                link(i)
                v.tensor_scalar(rstd[:], mv[:, :, 1], LN_EPS, None, ALU.add).then_inc(lnsem, 3)
                dve.wait_ge(lnsem, n0 + 4)
                link(v.reciprocal(rstd[:], rstd[:]))

            def ln_rows(o, i, t):
                return v.tensor_scalar(o, i, mv[:, t, 0:1], rstd[:, t:t + 1], ALU.subtract, ALU.mult)

            ln_stats(lambda t: x_sb[:, t, :], S["ln1"], 0, lambda t: dve.wait_ge(x_tile[t], 16))
            for t in range(NT + 2):
                if t < NT:
                    if t >= 2:
                        dve.wait_ge(S["ztT"], t - 1)
                    ln_rows(zt[:, t % 2, :], x_sb[:, t, :], t).then_inc(S["zt_ready"], 1)
                if t >= 2:
                    u = t - 2
                    dve.wait_ge(S["xl_cp"], u + 1)
                    link(v.tensor_tensor(prod[:, 0, :], xl_sb[:, u % 2, 0:D], att_bc[:], ALU.mult))
                    v.tensor_reduce(xl_sb[:, u % 2, D:RW], prod[:, 0, :].rearrange("p (h c) -> p h c", h=H), AX,
                                    ALU.add).then_inc(S["xl_dve"], 1)
                    dve.wait_ge(S["xr_cp"], u + 1)
                    link(v.tensor_tensor(prod[:, 1, :], ps[:, 4 + u % 2, :], att_bc[:], ALU.mult))
                    link(v.tensor_reduce(srow[:, 0, :], prod[:, 1, :].rearrange("p (h c) -> p h c", h=H), AX, ALU.add))
                    if u == NT - 1:
                        dve.wait_ge(S["cst"], 3)
                    link(v.tensor_copy(xr_hi[:, u, D:RW], srow[:, 0, :]))
                    v.tensor_tensor(xr_lo[:, u, D:RW], srow[:, 0, :], xr_hi[:, u, D:RW].bitcast(F32), ALU.subtract)
                    v.tensor_tensor(xr_lo[:, u, 0:D], ps[:, 4 + u % 2, :], xr_hi[:, u, 0:D].bitcast(F32),
                                    ALU.subtract).then_inc(S["xr_dve"], 1)

            dve.wait_ge(S["ngb_ready"], 1)
            link(v.tensor_copy(ngb[:], ps[:, 6, 0:NG]))
            dve.wait_ge(S["lists_in"], 32)
            for j in range(2):
                v.tensor_copy(lst_f[:, j, :], lst_i[:, j, :]).then_inc(S["lists_f"], 1)
            dve.wait_ge(S["listT"], 2)

            def by_tile(t_):
                return t_[:].rearrange("p (g k) -> p g k", k=TPG)

            def from_lists(bank):
                return ps[:, bank, 0:TPG * NG].rearrange("p (k g) -> p g k", k=TPG)

            ngb_t = ngb[:].unsqueeze(2).broadcast_to([P, NG, TPG])
            v.tensor_copy(by_tile(src_idx), from_lists(1)).then_inc(S["lists_ready"], 1)
            link(v.tensor_copy(by_tile(dcol), from_lists(0)))
            link(v.scalar_tensor_tensor(by_tile(drel), ngb_t, -float(P), by_tile(dcol), ALU.mult, ALU.add))
            link(v.scalar_tensor_tensor(by_tile(key), ngb_t, float(KEY), by_tile(dcol), ALU.mult, ALU.add))
            link(v.tensor_scalar(key[:], key[:], 1.0, None, ALU.add))
            v.memset(cols[:], 0.0).then_inc(S["lists_ready"], 1)

            def build_onehot(G, h, ready):
                for k in range(TPG):
                    i = v.tensor_scalar(onehot[:, h, k, :], iota[:], drel[:, bass.ds(TPG * G + k, 1)], None, ALU.is_equal)
                i.then_inc(ready, 1)

            def scores_out(G, h):
                dve.wait_ge(S["a_done"], TPG * G + TPG)
                v.tensor_tensor(
                    e_all[:, bass.ds(G * TPG * H, TPG * H)].rearrange("p (k h) -> p k h", k=TPG),
                    ps[:, 5 + h, 0:TPG * H].rearrange("p (k h) -> p k h", k=TPG),
                    slin[:, h], ALU.add).then_inc(S["e_done"], 1)

            def sum_rows(q, first, last):
                for u in range(UN):
                    i, G, h = UN * q + u, 2 * q + u // TPG, u // TPG
                    dve.wait_ge(S["xr_done"], i + 1)
                    dve.wait_ge(gath["a"][u], 16 * q + 16)
                    need(dve, S["t_done"], i - UN + 1)
                    if u % TPG == TPG - 1:
                        need(dve, S["e_done"], G - 1)
                        v.tensor_copy(slin[:, h], gat[:, TPG * h:TPG * (h + 1), D:RW])
                    v.tensor_tensor(zbuf[:, u, 0:D], gat[:, u, 0:D], ps[:, u % 2, :], ALU.add).then_inc(S["z_ready"], 1)
                    if u % TPG == 1 and not (first and h == 0):
                        scores_out(G - 1, 1 - h)
                    if u % TPG == 2 and not last:
                        dve.wait_ge(S["ot_p"], G + 1)
                        build_onehot(G + 2, h, S["o_ready"])

            build_onehot(0, 0, S["o_ready"])
            build_onehot(1, 1, S["o_ready"])
            sum_rows(0, True, False)
            with dve.Fori(1, Q - 1) as q:
                sum_rows(q, False, False)
            sum_rows(Q - 1, False, True)
            scores_out(NG - 1, 1)

            dve.wait_ge(S["e_done"], NG)
            v.tensor_copy(perm[:].rearrange("p (b j h) -> p b j h", b=CT, j=CH),
                          e_all[:].rearrange("p (j b h) -> p b j h", j=CH, b=CT)).then_inc(S["perm_ready"], 1)
            for b in range(CT):
                i = v.tensor_copy(permk[:, b * P:(b + 1) * P].rearrange("p (j h) -> p j h", j=CH),
                                  key[:].rearrange("p (j b) -> p b j", b=CT)[:, b, :].unsqueeze(2).broadcast_to([P, CH, H]))
            i.then_inc(S["perm_ready"], 1)
            dve.wait_ge(S["xk_ready"], 12)
            link(v.memset(pen[:], 0.0))
            link(v.tensor_tensor(pen[:, 1:CL], KX[:, 1:CL], KX[:, 0:CL - 1], ALU.not_equal))
            link(v.tensor_scalar(pen[:, 1:CL], pen[:, 1:CL], -BIG, None, ALU.mult))
            link(v.tensor_copy(cols[:, 0:1], KX[:, 0:1]))
            link(v.tensor_copy(cols[:, 1:2], KX[:, CL - 1:CL]))
            link(v.tensor_tensor(cols[:, 2:3], cols[:, 0:1], cols[:, 1:2], ALU.is_equal))
            v.memset(rowbuf[:], 0.0).then_inc(S["colp"], 1)
            for way in range(2):
                o = fwd if way == 0 else bwd
                step = 1 if way == 0 else -1
                data = X if way == 0 else fwd
                p_ = pen[:, 0:CL] if way == 0 else pen[:, 1:CL + 1]

                def scan(initial):
                    return v.tensor_tensor_scan(o[:, ::step], p_[:, ::step], data[:, ::step], initial, ALU.add, ALU.max)

                link(scan(-BIG))
                endcol = CL - 1 if way == 0 else 0
                k0 = 3 + 6 * way
                link(v.tensor_copy(cols[:, k0:k0 + 1], o[:, endcol:endcol + 1]))
                dve.wait_ge(S["colp_p"], way + 1)
                link(v.tensor_tensor(cols[:, k0 + 1:k0 + 2], ps[:, 0, 2 * way:2 * way + 1], cols[:, way:way + 1], ALU.is_equal))
                link(v.tensor_tensor(cols[:, k0 + 2:k0 + 3], cols[:, k0 + 1:k0 + 2], cols[:, 2:3], ALU.mult))
                link(v.tensor_scalar(cols[:, k0 + 1:k0 + 3], cols[:, k0 + 1:k0 + 3], -1.0, BIG, ALU.add, ALU.mult))
                v.memset(cols[:, k0 + 3:k0 + 4], 0.0).then_inc(S["colp"], 1)
                dve.wait_ge(S["rowp"], way + 1)
                for j in range(2):
                    link(v.tensor_copy(rowbuf[:, j, :].rearrange("p (h j) -> p h j", h=H),
                                       ps[0:1, 1, j * P:(j + 1) * P].rearrange("p (j h) -> p h j", h=H)))
                link(v.tensor_tensor_scan(rowbuf[:, 2, ::step], rowbuf[:, 1, ::step], rowbuf[:, 0, ::step], -BIG,
                                          ALU.add, ALU.max))
                v.tensor_copy(rowbuf[:, 3, :].rearrange("p (j h) -> p j h", h=H),
                              rowbuf[:, 2, :].rearrange("p (h j) -> p j h", h=H)).then_inc(S["rowv"], 1)
                dve.wait_ge(S["carry_p"], 2 * way + 1)
                v.tensor_copy(cols[:, k0 + 4:k0 + 5], ps[:, 2, 0:1]).then_inc(S["carry_c"], 1)
                dve.wait_ge(S["carry_p"], 2 * way + 2)
                link(v.tensor_tensor(cols[:, k0 + 5:k0 + 6], ps[:, 2, 2:3], cols[:, k0 + 1:k0 + 2], ALU.add))
                link(scan(cols[:, k0 + 5:k0 + 6]))
            v.tensor_tensor(X[:], X[:], bwd[:], ALU.subtract).then_inc(S["m_ready"], 1)
            for b in range(6):
                n = min(4, CT - 4 * b)
                dve.wait_ge(S["exT"], b + 1)
                v.tensor_copy(e_all[:].rearrange("p (j b h) -> p b j h", j=CH, b=CT)[:, 4 * b:4 * b + n],
                              ps[:, b % 4, 0:n * P].rearrange("p (b j h) -> p b j h", b=n, j=CH)).then_inc(S["ex_back"], 1)

            def add_sums(G, h, src_ps, width, done, agg):
                n = dve.value_load(ng_i[0:1, bass.ds(G, 1)], min_val=0, max_val=NT - 1)
                dve.wait_ge(agg, TPG * G + TPG)
                need(dve, done, G)
                v.tensor_tensor(acc[:, bass.ds(n, 1), 0:width], acc[:, bass.ds(n, 1), 0:width],
                                src_ps.unsqueeze(1), ALU.add).then_inc(done, 1)

            def weigh_rows(q, first, last):
                for u in range(UN):
                    i, G, h = UN * q + u, 2 * q + u // TPG, u // TPG
                    dve.wait_ge(gath["c"][u], 16 * q + 16)
                    need(dve, S["agg_done"], i - UN + 1)
                    v.tensor_tensor(zbuf[:, u, 0:D].rearrange("p (h c) -> p h c", h=H),
                                    gat[:, u, 0:D].rearrange("p (h c) -> p h c", h=H),
                                    e_all[:, bass.ds(i * H, H)].unsqueeze(2).broadcast_to([P, H, C]),
                                    ALU.mult).then_inc(S["msg_ready"], 1)
                    if u % TPG == 1 and not (first and h == 0):
                        add_sums(G - 1, 1 - h, ps_row[1 - h], RW, S["acc_done"], S["agg_done"])
                    if u % TPG == 2 and not (last and h == 1):
                        need(dve, S["agg_done"], TPG * G)
                        build_onehot(G + 1, 1 - h, S["o2_ready"])

            link(v.memset(acc[:], 0.0))
            dve.wait_ge(S["ex_back"], 6)
            build_onehot(0, 0, S["o2_ready"])
            weigh_rows(0, True, False)
            with dve.Fori(1, Q - 1) as q:
                weigh_rows(q, False, False)
            weigh_rows(Q - 1, False, True)
            add_sums(NG - 1, 1, ps_row[1], RW, S["acc_done"], S["agg_done"])

            dve.wait_ge(S["acc_done"], NG)
            den = acc[:, :, D:RW]
            link(v.tensor_scalar(den, den, 1e-16, None, ALU.add))
            link(v.reciprocal(den, den))
            for t in range(NT):
                i = v.tensor_tensor(acc[:, t, 0:D].rearrange("p (h c) -> p h c", h=H),
                                    acc[:, t, 0:D].rearrange("p (h c) -> p h c", h=H),
                                    acc[:, t, D:RW].unsqueeze(2).broadcast_to([P, H, C]), ALU.mult)
            link(i)
            for t in range(NT):
                i = v.tensor_tensor(acc[:, t, 0:D], acc[:, t, 0:D], gb_bc[:], ALU.add)
            link(i)
            x1 = acc[:, :, 0:D]
            link(v.tensor_tensor(x1, x1, x_sb[:], ALU.add))
            ln_stats(lambda t: acc[:, t, 0:D], S["ln2"], 0)
            for t in range(NT):
                if t >= 2:
                    dve.wait_ge(S["z2T"], t - 1)
                ln_rows(lnz[:, t % 2, :], acc[:, t, 0:D], t).then_inc(S["z2_ready"], 1)
            link(v.tensor_tensor(x_sb[:], x_sb[:], x1, ALU.add))
            for t in range(NT):
                i = v.tensor_tensor(x_sb[:, t, :], x_sb[:, t, :], b2_bc[:], ALU.add)
            link(i)
            for t in range(NT):
                dve.wait_ge(S["f2_mm"], t + 1)
                i = v.tensor_tensor(x_sb[:, t, :], x_sb[:, t, :], ps[:, 4 + t % 2, :], ALU.add)
                i.then_inc(S["u_ready"], 1)
            dve.wait_ge(S["u_ready"], NT)
            ln_stats(lambda t: x_sb[:, t, :], S["ln2"], 4)
            for t in range(NT):
                i = ln_rows(x_sb[:, t, :], x_sb[:, t, :], t)
            link(i)
            for t in range(NT):
                v.tensor_tensor(vrow[:, t, :], x_sb[:, t, :], be_bc[:], ALU.add).then_inc(S["x2_ready"], 1)
            link(v.tensor_scalar(cols[:, 15:16], epsc[:], 1.0, None, ALU.add))
            link(v.tensor_scalar(acc[:, :, 0:D], x_sb[:], cols[:, 15:16], None, ALU.mult))

            def edge_sum(q, first, last):
                for u in range(UN):
                    i, G, h = UN * q + u, 2 * q + u // TPG, u // TPG
                    dve.wait_ge(gath["d"][u], 16 * q + 16)
                    dve.wait_ge(S["tw_done"], i + 1)
                    need(dve, S["m2_ready"], i - 3)
                    v.tensor_tensor(zbuf[:, u % 4, 0:D], gat[:, u, 0:D], ps[:, 4 + u % 2, :], ALU.add).then_inc(S["t_ready"], 1)
                    if u % TPG == 1 and not (first and h == 0):
                        add_sums(G - 1, 1 - h, ps[:, 2 * (1 - h), :], D, S["acc2_done"], S["ag2_done"])
                    if u % TPG == 2 and not (last and h == 1):
                        need(dve, S["ag2_done"], TPG * G)
                        build_onehot(G + 1, 1 - h, S["o3_ready"])

            dve.wait_ge(S["x2_stored"], NT * 16)
            build_onehot(0, 0, S["o3_ready"])
            edge_sum(0, True, False)
            with dve.Fori(1, Q - 1) as q:
                edge_sum(q, False, False)
            edge_sum(Q - 1, False, True)
            add_sums(NG - 1, 1, ps[:, 2, :], D, S["acc2_done"], S["ag2_done"])

            def bn(data, nf, cp, s, g_, be_, ssc):
                for f in range(nf):
                    dve.wait_ge(cp, 3 * f + 3)
                    for ch in range(3):
                        w = min(D, N - ch * D)
                        i = v.bn_stats(bnst[:, f, ch, :], data[:, f, ch * D:ch * D + w])
                link(i)
                for f in range(nf):
                    i = v.bn_aggr(bnmv[:, f, :], bnst[:, f, :, :].rearrange("p a b -> p (a b)"))
                link(i)
                v.tensor_scalar(bnsc[:, 0:nf], bnmv[:, 0:nf, 1], 1e-5, None, ALU.add).then_inc(s, 4)
                dve.wait_ge(s, 5)
                link(v.reciprocal(bnsc[:, 0:nf], bnsc[:, 0:nf]))
                link(v.tensor_tensor(bnsc[:, 0:nf], bnsc[:, 0:nf], g_, ALU.mult))
                link(v.tensor_tensor(bnsh[:, 0:nf], bnmv[:, 0:nf, 0], bnsc[:, 0:nf], ALU.mult))
                v.tensor_tensor(bnsh[:, 0:nf], be_, bnsh[:, 0:nf], ALU.subtract).then_inc(ssc, 1)

            bn(uT, F2 // P, S["u_cp"], S["bn1"], g1c, be1c, S["bn1s"])
            dve.wait_ge(S["sT_ready"], F2 // P)
            bn(yT, FC, S["y_cp"], S["bn2"], g2c, be2c, S["bn2s"])
            for t in range(NT):
                dve.wait_ge(S["yb_p"], t + 1)
                i = v.tensor_tensor(acc[:, t, 0:D], x_sb[:, t, :], ps[:, 6 + t % 2, :], ALU.add)
                i.then_inc(S["v_ready"], 1)
            dve.wait_ge(S["v_ready"], NT)
            ln_stats(lambda t: acc[:, t, 0:D], S["ln4"], 0)
            for t in range(NT):
                if t >= 2:
                    dve.wait_ge(out_stored[t % 2], 16 * (t // 2))
                ln_rows(fin[:, t % 2, :], acc[:, t, 0:D], t).then_inc(S["fin_ready"], 1)

        @block.tensor
        def _(pe):
            tm = nc.tensor
            pe.wait_ge(S["cnt_ready"], 1)
            pe.wait_ge(S["cstv"], 1)
            tm.matmul(ps[0:1, 7, 0:NT], ones[0:125, 0:1], cnt[0:125, 0:NT], start=True, stop=True).then_inc(S["rp_ready"], 1)
            pe.wait_ge(S["tab_ready"], 1)
            tm.matmul(ps[:, 6, 0:NG], ones[0:1, :], ngf[:], start=True, stop=True).then_inc(S["ngb_ready"], 1)
            pe.wait_ge(S["cst"], 15)
            pe.wait_ge(S["par_in"], 16 * len(PAR))
            tm.transpose(ps[:, 7, P:P + NPAR], par_row[:], ident[0:NPAR, 0:NPAR]).then_inc(S["par_T"], 1)

            def transpose_rows(o, i):
                for c in range(FC):
                    m = tm.transpose(o[:, c * P:(c + 1) * P], i[:, c * P:(c + 1) * P], ident[:])
                return m

            for t in range(NT + 1):
                if t < NT:
                    pe.wait_ge(S["zt_ready"], t + 1)
                    if t >= 2:
                        pe.wait_ge(S["hT_ready"], t - 1)
                    transpose_rows(ps[:, t % 2, :], zt[:, t % 2, :]).then_inc(S["ztT"], 1)
                if t > 0:
                    u = t - 1
                    pe.wait_ge(S["hT_ready"], u + 1)
                    if u == 0:
                        pe.wait_ge(S["wqkv_in"], 32)
                    for w, bank, done in ((0, 2, S["xl_mm"]), (1, 4, S["xr_mm"])):
                        if u >= 2:
                            pe.wait_ge(S["xl_cp" if w == 0 else "xr_dve"], u - 1)
                        for c in range(FC):
                            m = tm.matmul(ps[:, bank + u % 2, :], hT[:, c, u * P:(u + 1) * P], Wlr[:, w, c, :],
                                          start=(c == 0), stop=(c == FC - 1))
                        m.then_inc(done, 1)
            for j in range(2):
                pe.wait_ge(S["lists_f"], j + 1)
                pe.wait_ge(S["hT_ready"], NT)
                for k in range(TPG):
                    m = tm.transpose(ps[:, j, k * NG:(k + 1) * NG], lst_f[:, j, k * P:(k + 1) * P], ident[0:NG, 0:NG])
                m.then_inc(S["listT"], 1)

            def onehot_T(G, h):
                pe.wait_ge(S["o_ready"], G + 1)
                need(pe, S["ot_ready"], G)
                for k in range(TPG):
                    m = tm.transpose(ps[:, 4, k * P:(k + 1) * P], onehot[:, h, k, :], ident[:])
                m.then_inc(S["ot_p"], 1)

            def dst_rows(i, G, u, h, n):
                if u % TPG == 0:
                    pe.wait_ge(S["ot_ready"], G + 1)
                need(pe, S["z_ready"], i - 1)
                k = u % TPG
                w = onehotT[:, h, k * P:(k + 1) * P]
                for part, tab in enumerate((xr_hi, xr_lo)):
                    m = tm.matmul(ps[:, u % 2, :], w, tab[:, bass.ds(n, 1), 0:D], start=(part == 0), stop=(part == 1))
                m.then_inc(S["xr_done"], 1)

            def z_T(i, u):
                pe.wait_ge(S["z_ready"], i + 1)
                need(pe, S["relu_done"], i - 1)
                transpose_rows(ps[:, 2 + u % 2, :], zbuf[:, u, :]).then_inc(S["t_done"], 1)

            def scores(i, u, G, h, n):
                pe.wait_ge(S["relu_done"], i + 1)
                if u % TPG == 0:
                    need(pe, S["e_done"], G - 1)
                k = u % TPG
                o = ps[:, 5 + h, k * H:(k + 1) * H]
                for part, tab in enumerate((xr_hi, xr_lo)):
                    tm.matmul(o, onehotT[:, h, k * P:(k + 1) * P], tab[:, bass.ds(n, 1), D:RW], start=(part == 0), stop=False)
                for c in range(FC):
                    m = tm.matmul(o[:, 2 * c:2 * c + 2], zrel[:, u % 2, c * P:(c + 1) * P], attblk[:, c, :],
                                  start=False, stop=(c == FC - 1))
                m.then_inc(S["a_done"], 1)

            def tile_of(G):
                return pe.value_load(ng_i[0:1, bass.ds(G, 1)], min_val=0, max_val=NT - 1)

            def phase_a(q, first, last):
                n = [None if first else tile_of(2 * q - 1), tile_of(2 * q), tile_of(2 * q + 1),
                     None if last else tile_of(2 * q + 2)]
                for u in range(UN):
                    i, G, h = UN * q + u, 2 * q + u // TPG, u // TPG
                    if u % TPG == 1 and not (last and h == 1):
                        onehot_T(G + 1, 1 - h)
                    z_T(i, u)
                    if not (first and u == 0):
                        w = (u - 1) % UN
                        scores(i - 1, w, 2 * q + (u - 1) // TPG, w // TPG, n[1 + (u - 1) // TPG])
                    if not (last and u >= UN - 2):
                        w = u + 2
                        dst_rows(i + 2, 2 * q + w // TPG, w % UN, (w % UN) // TPG, n[1 + w // TPG])

            pe.wait_ge(S["lists_ready"], 2)
            pe.wait_ge(S["xr_dve"], NT)
            pe.wait_ge(S["xr_cp"], NT)
            pe.wait_ge(S["xl_dve"], NT)
            pe.wait_ge(S["cstv"], 3)
            onehot_T(0, 0)
            n0 = tile_of(0)
            dst_rows(0, 0, 0, 0, n0)
            dst_rows(1, 0, 1, 0, n0)
            phase_a(0, True, False)
            with pe.Fori(1, Q - 1) as q:
                phase_a(q, False, False)
            phase_a(Q - 1, False, True)
            scores(T - 1, UN - 1, NG - 1, 1, tile_of(NG - 1))

            pe.wait_ge(S["perm_ready"], 2)
            for b in range(6):
                for j, t_ in enumerate((perm, permk)):
                    bank = (2 * b + j) % 8
                    if 2 * b + j >= 8:
                        pe.wait_ge(S["xk_ready"], 2 * b + j - 7)
                    for k in range(min(4, CT - 4 * b)):
                        m = tm.transpose(ps[:, bank, k * P:(k + 1) * P], t_[:, (4 * b + k) * P:(4 * b + k + 1) * P], ident[:])
                    m.then_inc(S["xk_p"], 1)
            for way in range(2):
                shift = shift_dn if way == 0 else shift_up
                k0 = 3 + 6 * way
                pe.wait_ge(S["colp"], 1 + way)
                tm.matmul(ps[:, 0, 2 * way:2 * way + 1], shift[:], cols[:, 1 - way:2 - way], start=True, stop=True).then_inc(S["colp_p"], 1)
                pe.wait_ge(S["colp"], 2 + way)
                tm.matmul(ps[0:1, 1, 0:P], cols[:, k0:k0 + 1], ident[:], start=True, stop=True)
                tm.matmul(ps[0:1, 1, P:2 * P], cols[:, k0 + 2:k0 + 3], ident[:], start=True, stop=True).then_inc(S["rowp"], 1)
                pe.wait_ge(S["rowv"], way + 1)
                tm.matmul(ps[:, 2, 0:1], rowbuf[:, 3, :], ones[0:1, 0:1], start=True, stop=True).then_inc(S["carry_p"], 1)
                pe.wait_ge(S["carry_c"], way + 1)
                tm.matmul(ps[:, 2, 2:3], shift[:], cols[:, k0 + 4:k0 + 5], start=True, stop=True).then_inc(S["carry_p"], 1)
            pe.wait_ge(S["ex_ready"], 1)
            for b in range(6):
                if b >= 4:
                    pe.wait_ge(S["ex_back"], b - 3)
                for k in range(min(4, CT - 4 * b)):
                    m = tm.transpose(ps[:, b % 4, k * P:(k + 1) * P], X[:, (4 * b + k) * P:(4 * b + k + 1) * P], ident[:])
                m.then_inc(S["exT"], 1)

            def sum_by_dst(q, first, last):
                for u in range(UN):
                    i, G, h, k = UN * q + u, 2 * q + u // TPG, u // TPG, u % TPG
                    if k == 0:
                        pe.wait_ge(S["o2_ready"], G + 1)
                        need(pe, S["acc_done"], G - 1)
                    pe.wait_ge(S["msg_ready"], i + 1)
                    o = ps_row[h]
                    tm.matmul(o[:, 0:D], onehot[:, h, k, :], zbuf[:, u, 0:D], start=(k == 0), stop=(k == TPG - 1))
                    tm.matmul(o[:, D:RW], onehot[:, h, k, :], e_all[:, bass.ds(i * H, H)], start=(k == 0),
                              stop=(k == TPG - 1)).then_inc(S["agg_done"], 1)

            pe.wait_ge(S["ex_back"], 6)
            sum_by_dst(0, True, False)
            with pe.Fori(1, Q - 1) as q:
                sum_by_dst(q, False, False)
            sum_by_dst(Q - 1, False, True)

            pe.wait_ge(S["acc_done"], NG)
            for t in range(NT):
                pe.wait_ge(S["z2_ready"], t + 1)
                if t >= 2:
                    pe.wait_ge(S["h2T_ready"], t - 1)
                transpose_rows(ps[:, t % 2, :], lnz[:, t % 2, :]).then_inc(S["z2T"], 1)
            pe.wait_ge(S["w_in"], 32)
            pe.wait_ge(S["h2T_ready"], NT)
            n = 0
            for ch in range(3):
                w = min(D, NP - ch * D)
                for f in range(F1 // P):
                    if n >= 2:
                        pe.wait_ge(S["hid_ready"], n - 1)
                    for c in range(FC):
                        m = tm.matmul(ps[:, 2 + n % 2, 0:w], W1_sb[:, c, f * P:(f + 1) * P], hT[:, c, ch * D:ch * D + w],
                                      start=(c == 0), stop=(c == FC - 1))
                    m.then_inc(S["f1_mm"], 1)
                    n += 1
                for t in range(4 * ch, 4 * ch + w // P):
                    if t >= 2:
                        pe.wait_ge(S["u_ready"], t - 1)
                    for f in range(F1 // P):
                        if t == 4 * ch:
                            pe.wait_ge(S["hid_ready"], ch * (F1 // P) + f + 1)
                        m = tm.matmul(ps[:, 4 + t % 2, :], hid[:, f, (t - 4 * ch) * P:(t - 4 * ch + 1) * P], W2_sb[:, f, :],
                                      start=(f == 0), stop=(f == F1 // P - 1))
                    m.then_inc(S["f2_mm"], 1)

            def edge_T(G, h):
                pe.wait_ge(ea_in[h], 16 * (G // 2) + 16 if isinstance(G, int) else 8 * (G - h) + 16)
                need(pe, S["ea_ready"], G)
                for k in range(2):
                    m = tm.transpose(ps[:, 6, k * P:(k + 1) * P], ea_g[:, h, k * P:(k + 1) * P], ident[:])
                m.then_inc(S["ea_p"], 1)

            def edge_project(i, u, G, h):
                k = u % TPG
                if k == 0:
                    pe.wait_ge(S["ea_ready"], G + 1)
                need(pe, S["t_ready"], i - 1)
                r = (k % 2) * ED
                tm.matmul(ps[:, 4 + u % 2, :], eaT[r:r + ED, h, k // 2, :], We2[r:r + ED, :], start=True,
                          stop=True).then_inc(S["tw_done"], 1)

            def sum_messages(i, u, G, h):
                k = u % TPG
                if k == 0:
                    pe.wait_ge(S["o3_ready"], G + 1)
                    need(pe, S["acc2_done"], G - 1)
                pe.wait_ge(S["m2_ready"], i + 1)
                tm.matmul(ps[:, 2 * h, :], onehot[:, h, k, :], zbuf[:, 4 + u % 4, 0:D], start=(k == 0),
                          stop=(k == TPG - 1)).then_inc(S["ag2_done"], 1)

            def phase_d(q, first, last):
                for u in range(UN):
                    i, G, h = UN * q + u, 2 * q + u // TPG, u // TPG
                    if u % TPG == 1 and not (last and h == 1):
                        edge_T(G + 1, 1 - h)
                    if not (last and u >= UN - 2):
                        w = u + 2
                        edge_project(i + 2, w % UN, 2 * q + w // TPG, (w % UN) // TPG)
                    sum_messages(i, u, G, h)

            pe.wait_ge(S["we_in"], 32)
            pe.wait_ge(S["u_ready"], NT)
            edge_T(0, 0)
            edge_project(0, 0, 0, 0)
            edge_project(1, 1, 0, 0)
            phase_d(0, True, False)
            with pe.Fori(1, Q - 1) as q:
                phase_d(q, False, False)
            phase_d(Q - 1, False, True)

            pe.wait_ge(S["acc2_done"], NG)
            for t in range(NT):
                if t >= 2:
                    pe.wait_ge(S["hhT_ready"], t - 1)
                transpose_rows(ps[:, t % 2, :], acc[:, t, :]).then_inc(S["hhT_p"], 1)
            pe.wait_ge(S["v_in"], 16)
            pe.wait_ge(S["hhT_ready"], NT)
            n = 0
            for f in range(F2 // P):
                for ch in range(3):
                    w = min(D, NP - ch * D)
                    if n >= 2:
                        pe.wait_ge(S["u_cp"], n - 1)
                    for c in range(FC):
                        m = tm.matmul(ps[:, 2 + n % 2, 0:w], V1_sb[:, c, f * P:(f + 1) * P], hT[:, c, ch * D:ch * D + w],
                                      start=(c == 0), stop=(c == FC - 1))
                    m.then_inc(S["u_mm"], 1)
                    n += 1
            n = 0
            pe.wait_ge(S["v2_in"], 16)
            pe.wait_ge(S["sT_ready"], F2 // P)
            for f in range(FC):
                for ch in range(3):
                    w = min(D, NP - ch * D)
                    if n >= 2:
                        pe.wait_ge(S["y_cp"], n - 1)
                    for k in range(F2 // P):
                        m = tm.matmul(ps[:, 4 + n % 2, 0:w], V2_sb[:, k, f * P:(f + 1) * P], uT[:, k, ch * D:ch * D + w],
                                      start=(k == 0), stop=(k == F2 // P - 1))
                    m.then_inc(S["y_mm"], 1)
                    n += 1
            pe.wait_ge(S["yT_ready"], FC)
            for t in range(NT):
                if t >= 2:
                    pe.wait_ge(S["v_ready"], t - 1)
                for f in range(FC):
                    m = tm.transpose(ps[:, 6 + t % 2, f * P:(f + 1) * P], yT[:, f, t * P:(t + 1) * P], ident[:])
                m.then_inc(S["yb_p"], 1)


_INS = ['x', 'src', 'dst', 'edge_attr_64', 'L0_gnn_ln1_g', 'L0_gnn_ln1_b', 'L0_gnn_Wl', 'L0_gnn_Wr', 'L0_gnn_att',
        'L0_gnn_gat_bias', 'L0_gnn_ln2_g', 'L0_gnn_ln2_b', 'L0_gnn_W1', 'L0_gnn_b1', 'L0_gnn_W2', 'L0_gnn_b2',
        'L1_gnn_W_e', 'L1_gnn_b_e', 'L1_gnn_W1', 'L1_gnn_b1', 'L1_gnn_g1', 'L1_gnn_beta1', 'L1_gnn_W2', 'L1_gnn_b2',
        'L1_gnn_g2', 'L1_gnn_beta2', 'L1_gnn_eps']
_OUTS = [((1250, 512), 'float32')]


def kernel(**inputs):
    import numpy as _np
    import concourse.bacc as _bacc
    from concourse import mybir as _mybir
    from concourse.bass_utils import run_bass_kernel_spmd as _run

    nc = _bacc.Bacc("TRN2", target_bir_lowering=False, num_devices=1)
    arrays, args = {}, []
    for name in _INS:
        a = _np.ascontiguousarray(inputs[name])
        if a.ndim == 0:
            a = a.reshape(1)
        arrays[f"in_{name}_dram"] = a
        args.append(nc.dram_tensor(f"in_{name}_dram", a.shape, _mybir.dt.from_np(a.dtype), kind="ExternalInput").ap())
    for i, (shape, dtype) in enumerate(_OUTS):
        dt = _mybir.dt.from_np(_np.dtype(dtype))
        args.append(nc.dram_tensor(f"out_{i}_dram", shape, dt, kind="ExternalOutput").ap())
    gnn_kernel(nc, *args)
    r = _run(nc, [arrays], core_ids=[0])
    got = tuple(r.results[0][f"out_{i}_dram"] for i in range(len(_OUTS)))
    return got[0]
```

```python
from contextlib import ExitStack

import numpy as np

import concourse.bass as bass
from concourse import mybir

P = 128
N, D, E = 1250, 512, 40000
H = 8
C = D // H
FC = D // P
ED = 64
F1 = 2048
F2 = 1024
NT = (N + P - 1) // P
NP = NT * P
LAST = N - (NT - 1) * P
TPG = 4
GE = TPG * P
NC = (E + GE - 1) // GE + 1
NG = NC - 1 + NT - 1
NG += NG % 2
T = NG * TPG
UN = 2 * TPG
Q = NG // 2
RW = D + H
EP = NC * GE
NPAD = EP - E
PADP = max(d for d in range(1, P + 1) if NPAD % d == 0)
PAD_DST = 4000
KEY = 4096
CH = P // H
CT = T // CH
CL = CT * P
BIG = 1.0e30
LN_EPS = 1e-5
SPLIT = 3

ALU = mybir.AluOpType
ACT = mybir.ActivationFunctionType
F32 = mybir.dt.float32
FR = mybir.dt.float32r
I32 = mybir.dt.int32
AX = mybir.AxisListType.X


def need(eng, sem, n):
    if not isinstance(n, int) or n > 0:
        eng.wait_ge(sem, n)


def gnn_kernel(nc, x, src, dst, ea, ln1_g, ln1_b, Wl, Wr, att, gat_bias, ln2_g, ln2_b, W1, b1, W2, b2,
               W_e, b_e, V1, c1, g1, beta1, V2, c2, g2, beta2, eps, out):
    with ExitStack() as ctx:
        def sem(name):
            return ctx.enter_context(nc.semaphore(name))

        def dram(name, shape, dt=F32):
            return nc.dram_tensor(name, shape, dt).ap()

        src_pad, dst_pad = dram("src_pad", [EP], I32), dram("dst_pad", [EP], I32)
        ea_pad = dram("ea_pad", [EP, ED])
        e_scr = dram("e_scr", [2 * H, T * P])
        xl_tab, x2_tab = dram("xl_tab", [NP, RW]), dram("x2_tab", [NP, D])

        def put(region, name, shape, dt=F32):
            size = int(np.prod(shape[1:])) * 4
            t = nc.alloc_sbuf_tensor_at(name, shape, dt, offset=region[0])
            region[0] += (size + 31) // 32 * 32
            return t

        base = [17408]
        ident = put(base, "ident", [P, P])
        iota = put(base, "iota", [P, P])
        iota_i = put(base, "iota_i", [P, P], I32)
        ones = put(base, "ones", [P, P])
        x_sb = put(base, "x_sb", [P, NT, D])
        acc = put(base, "acc", [P, NT, RW])
        e_all = put(base, "e_all", [P, T * H])
        drel = put(base, "drel", [P, T])
        src_idx = put(base, "src_idx", [P, T], I32)
        key = put(base, "key", [P, T])
        ng_i = put(base, "ng_i", [1, NG], I32)
        s_i = put(base, "s_i", [1, NG], I32)
        chunk_i = put(base, "chunk_i", [NG, 1], I32)
        idx_stage = put(base, "idx_stage", [P, UN], I32)
        PAR = (("ln1_g", ln1_g, FC), ("ln1_b", ln1_b, FC), ("att", att.rearrange("h c -> (h c)"), FC),
               ("ln2_g", ln2_g, FC), ("ln2_b", ln2_b, FC), ("b1", b1, F1 // P), ("c1", c1, F2 // P), ("g1", g1, F2 // P),
               ("beta1", beta1, F2 // P), ("c2", c2, FC), ("g2", g2, FC), ("beta2", beta2, FC))
        NPAR = sum(k for _, _, k in PAR)
        par_row = put(base, "par_row", [NPAR, P])
        par = put(base, "par", [P, NPAR])
        par_at, at = {}, 0
        for name, _, k in PAR:
            par_at[name] = (at, at + k)
            at += k
        (ln1gc, ln1bc, attc, ln2gc, ln2bc, b1c, c1c, g1c, be1c, c2c, g2c, be2c) = (
            par[:, lo_:hi_] for lo_, hi_ in par_at.values())
        att_parts = put(base, "att_parts", [P, FC * 2 * H], FR)
        att_full = put(base, "att_full", [P, FC * 2 * H])
        att8 = put(base, "att8", [P, 2, FC])
        epsc = put(base, "epsc", [P, 1])
        att_bc = put(base, "att_bc", [P, D])
        gb_bc, b2_bc, be_bc = (put(base, n, [P, D]) for n in ("gb_bc", "b2_bc", "be_bc"))
        shift_dn, shift_up = put(base, "shift_dn", [P, P]), put(base, "shift_up", [P, P])
        stats = put(base, "stats", [P, NT, 6])
        mv = put(base, "mv", [P, NT, 2])
        rstd = put(base, "rstd", [P, NT])
        bnst = put(base, "bnst", [P, F2 // P, 3, 6])
        bnmv = put(base, "bnmv", [P, F2 // P, 2])
        bnsc, bnsh = put(base, "bnsc", [P, F2 // P]), put(base, "bnsh", [P, F2 // P])
        cols = put(base, "cols", [P, 16])
        hT = put(base, "hT", [P, FC, NP])
        lo = base[0]
        ring = [lo]
        gat = put(ring, "gat", [P, UN, RW])
        onehot = put(ring, "onehot", [P, 2, TPG, P])
        onehotT = put(ring, "onehotT", [P, 2, GE], FR)
        zbuf = put(ring, "zbuf", [P, UN, RW])
        est = put(ring, "est", [2 * H, 2, GE])
        hi = ring[0]
        ra = [hi]
        xr_hi = put(ra, "xr_hi", [P, NT, RW], FR)
        xr_lo = put(ra, "xr_lo", [P, NT, RW], FR)
        ra_end = ra[0]
        rz = [ra_end]
        Wlr = put(ra, "Wlr", [P, 2, FC, D])
        zt = put(ra, "zt", [P, 2, D])
        zr_hi = put(rz, "zr_hi", [P, 2, SPLIT, 2 * P], FR)
        zr_lo = put(rz, "zr_lo", [P, 2, SPLIT, 2 * P], FR)
        zr_full = put(rz, "zr_full", [P, 2, FC - SPLIT, 2 * P])
        rs = [lo]
        dst_i = put(rs, "dst_i", [P, E // 125], I32)
        dst_f = put(rs, "dst_f", [P, E // 125])
        rl = [rs[0]]
        cmp = put(rs, "cmp", [P, NT, E // 125])
        bounds_i = put(rs, "bounds_i", [P, 16], I32)
        bounds = put(rs, "bounds", [P, 16])
        cnt = put(rs, "cnt", [P, 16])
        iotaK_i, iotaK = put(rs, "iotaK_i", [1, P], I32), put(rs, "iotaK", [1, P])
        rows = put(rs, "rows", [1, 12, 16])
        kcmp = put(rs, "kcmp", [1, NT, NC - 1])
        gcmp = put(rs, "gcmp", [1, NG, NT])
        gprod = put(rs, "gprod", [1, NG, NT])
        ngf, sf = put(rs, "ngf", [1, NG]), put(rs, "sf", [1, NG])
        ngb = put(rs, "ngb", [P, NG])
        xl_sb = put(rs, "xl_sb", [P, 2, RW])
        prod = put(rs, "prod", [P, 2, D])
        srow = put(rs, "srow", [P, 2, H])
        pads_i = put(rs, "pads_i", [4, NPAD // 4], I32)
        padz_i = put(rs, "padz_i", [4, NPAD // 4], I32)
        padz = put(rs, "padz", [PADP, NPAD * ED // PADP])
        lst_i = put(rl, "lst_i", [NG, 2, GE], I32)
        lst_f = put(rl, "lst_f", [NG, 2, GE])
        dcol = put(rl, "dcol", [P, T])
        assert max(rl[0], rs[0]) <= hi, (rl[0], rs[0], hi)
        rb = [hi]
        X, KX, fwd, bwd = (put(rb, n, [P, CL]) for n in ("X", "KX", "fwd", "bwd"))
        pen = put(rb, "pen", [P, CL + 16])
        perm = fwd
        permk = bwd
        rowbuf = put(rb, "rowbuf", [1, 6, P])
        rw = [hi]
        W1_sb = put(rw, "W1_sb", [P, FC, F1])
        W2_sb = put(rw, "W2_sb", [P, F1 // P, D])
        rh = [lo]
        hid = put(rh, "hid", [P, F1 // P, D])
        lnz = put(rh, "lnz", [P, 2, D])
        assert rh[0] <= hi, (rh[0], hi)
        vrow = put([lo], "vrow", [P, NT, D])
        rv = [hi]
        V1_sb = put(rv, "V1_sb", [P, FC, F2])
        rd = [rv[0]]
        uT = put(rv, "uT", [P, F2 // P, NP])
        ea_g = put(rd, "ea_g", [P, 2, TPG * ED])
        ea_hl = put(rd, "ea_hl", [P, 2, TPG, 2 * ED], FR)
        eaT = put(rd, "eaT", [P, 2, GE], FR)
        We2 = put(rd, "We2", [P, D])
        We_hi, We_lo = put(rd, "We_hi", [P, D], FR), put(rd, "We_lo", [P, D], FR)
        rv2 = [lo]
        yT = put(rv2, "yT", [P, FC, NP])
        fin = put(rv2, "fin", [P, 2, D])
        V2_sb = put(rv2, "V2_sb", [P, F2 // P, D])
        assert rv2[0] <= hi, (rv2[0], hi)
        end = max(r[0] for r in (ra, rz, rb, rw, rv, rd))
        assert end <= 229344, (lo, hi, end)

        ps = ctx.enter_context(nc.psum_tensor("ps", [P, 8, D], F32))
        psf = ps[:].rearrange("p b n -> p (b n)")
        ps_row = [psf[:, 2 * s * D:2 * s * D + RW] for s in range(2)]

        names = """dst_in wqkv_in par_in bc_in pad_in cst cstv cnt_ready rp_ready tab_ready ngb_ready chunk_ready
        lists_in lists_f listT lists_ready ln1 zt_ready ztT hT_ready xl_mm xr_mm xl_cp xr_cp xl_dve xr_dve
        ot_p ot_ready o_ready xr_done z_ready t_done hi_ready lo_ready sc_done e_out slin_ready es_loaded
        perm_ready xk_p k_ready xs_ready pen_ready chain colp_p colp rowp rowv carry_p carry carry_c m_ready ex_ready exT ex_back
        o2_ready msg_ready agg_done acc_done x1_ready w_in ln2 z2_ready z2T h2T_ready f1_mm hid_ready f2_mm u_ready
        x2_ready x2_stored we_in We_ready v2_in ea_hi ea_split ea_p ea_ready tw_done t_ready m2_ready o3_ready ag2_done acc2_done v_in hhT_p hhT_ready
        u_mm u_cp bn1 bn1s sT_ready y_mm y_cp bn2 bn2s yT_ready yb_p v_ready ln4 fin_ready
        gate dvec par_T par_ready""".split()
        S = {n: sem(n) for n in names}
        gath = {ph: [sem(f"gath_{ph}{i}") for i in range(UN)] for ph in "acd"}
        staged = {ph: sem(f"staged_{ph}") for ph in "acd"}
        ea_in = [sem(f"ea_in{i}") for i in range(2)]
        est_stored = [sem(f"est_stored{i}") for i in range(2)]
        xl_stored = [sem(f"xl_stored{i}") for i in range(2)]
        out_stored = [sem(f"out_stored{i}") for i in range(2)]
        x_tile = [sem(f"x_tile{t}") for t in range(NT)]
        block = ctx.enter_context(nc.Block())

        @block.sync
        def _(sp):
            sp.dma_start(dst_i[0:125, :], dst.rearrange("(p f) -> p f", p=125)).then_inc(S["dst_in"], 16)
            sp.wait_ge(S["cst"], 1)
            for t in range(NT):
                r = P if t < NT - 1 else LAST
                sp.dma_start(x_sb[0:r, t, :], x[t * P:t * P + r, :]).then_inc(x_tile[t], 16)
            sp.dma_start(Wlr[:, 0], Wl.rearrange("(c p) n -> p c n", p=P)).then_inc(S["wqkv_in"], 16)
            sp.dma_start(Wlr[:, 1], Wr.rearrange("(c p) n -> p c n", p=P)).then_inc(S["wqkv_in"], 16)
            k = 320
            sp.dma_start(ea_pad[0:E, :].rearrange("(a b) c -> a (b c)", a=k),
                         ea.rearrange("(a b) c -> a (b c)", a=k)).then_inc(S["pad_in"], 16)
            for t in range(NT):
                sp.wait_ge(S["xl_cp"], t + 1)
                sp.wait_ge(S["xl_dve"], t + 1)
                sp.dma_start(xl_tab[t * P:(t + 1) * P, :], xl_sb[:, t % 2, :]).then_inc(xl_stored[t % 2], 16)
            def store_scores(q):
                for h in range(2):
                    sp.wait_ge(S["e_out"], 2 * q + h + 1)
                    sp.dma_start(e_scr[:, bass.ds((2 * q + h) * GE, GE)], est[:, h, :]).then_inc(est_stored[h], 16)

            store_scores(0)
            with sp.Fori(1, Q) as q:
                store_scores(q)
            for h in range(2):
                sp.wait_ge(est_stored[h], Q * 16 + 16 * h)
            sp.wait_ge(S["sc_done"], T // 2)
            for j in range(CH):
                sp.dma_start(X[j * H:(j + 1) * H, :], e_scr[0:H, j * CL:(j + 1) * CL]).then_inc(S["es_loaded"], 16)
            sp.wait_ge(S["ex_back"], 6)
            sp.dma_start(W1_sb[:], W1.rearrange("(c p) n -> p c n", p=P)).then_inc(S["w_in"], 16)
            sp.dma_start(W2_sb[:], W2.rearrange("(c p) n -> p c n", p=P)).then_inc(S["w_in"], 16)
            for t in range(NT):
                sp.wait_ge(S["x2_ready"], t + 1)
                sp.dma_start(x2_tab[t * P:(t + 1) * P, :], vrow[:, t, :]).then_inc(S["x2_stored"], 16)
            for half in range(2):
                sp.dma_start(We2[half * ED:(half + 1) * ED, :], W_e[:, :]).then_inc(S["we_in"], 16)
            sp.dma_start(V1_sb[:], V1.rearrange("(c p) n -> p c n", p=P)).then_inc(S["v_in"], 16)

            def edge_features(q):
                for h in range(2):
                    need(sp, S["ea_split"], 2 * q + h - 1)
                    s = sp.value_load(s_i[0:1, bass.ds(2 * q + h, 1)], min_val=0, max_val=EP - GE)
                    sp.dma_start(ea_g[:, h, :].rearrange("p (k c) -> p k c", k=TPG),
                                 ea_pad[bass.ds(s, GE), :].rearrange("(k p) c -> p k c", p=P)).then_inc(ea_in[h], 16)

            edge_features(0)
            with sp.Fori(1, Q) as q:
                edge_features(q)
            sp.wait_ge(S["acc2_done"], NG)
            sp.dma_start(V2_sb[:], V2.rearrange("(c p) n -> p c n", p=P)).then_inc(S["v2_in"], 16)
            for t in range(NT):
                r = P if t < NT - 1 else LAST
                sp.wait_ge(S["fin_ready"], t + 1)
                sp.dma_start(out[t * P:t * P + r, :], fin[0:r, t % 2, :]).then_inc(out_stored[t % 2], 16)
            for half in out_stored:
                sp.wait_ge(half, NT // 2 * 16)

        @block.gpsimd
        def _(pool):
            g = nc.gpsimd
            g.memset(x_sb[:, NT - 1, :], 0.0).then_inc(S["cst"], 1)
            g.memset(xr_hi[:, NT - 1, :].bitcast(F32), 0.0).then_inc(S["cst"], 1)
            g.memset(xr_lo[:, NT - 1, :].bitcast(F32), 0.0).then_inc(S["cst"], 1)
            g.memset(pads_i[:], PAD_DST).then_inc(S["cst"], 1)
            g.memset(padz_i[:], 0).then_inc(S["cst"], 1)
            g.memset(padz[:], 0.0).then_inc(S["cst"], 1)
            g.iota(iota_i[:], pattern=[[1, P]], base=0, channel_multiplier=0).then_inc(S["cst"], 1)
            g.iota(bounds_i[:], pattern=[[P, 16]], base=0, channel_multiplier=0).then_inc(S["cst"], 1)
            g.iota(iotaK_i[:], pattern=[[GE, P]], base=0, channel_multiplier=0).then_inc(S["cst"], 1)
            g.memset(ident[:], 1.0).then_inc(S["cst"], 1)
            g.memset(shift_dn[:], 1.0).then_inc(S["cst"], 1)
            g.memset(shift_up[:], 1.0).then_inc(S["cst"], 1)
            pool.wait_ge(S["cst"], 12)
            for m, off in ((ident, 0), (shift_dn, H), (shift_up, -H)):
                g.affine_select(out=m[:], in_=m[:], compare_op=ALU.is_equal, fill=0.0, base=off,
                                pattern=[[-1, P]], channel_multiplier=1).then_inc(S["cst"], 1)
            for t_, a in ((att_bc, att.rearrange("h c -> (h c)")), (gb_bc, gat_bias), (b2_bc, b2), (be_bc, b_e)):
                g.dma_start(t_[:], a.partition_broadcast(P)).then_inc(S["bc_in"], 16)
            g.dma_start(epsc[:], eps.partition_broadcast(P)).then_inc(S["bc_in"], 16)

            def gather(q, ph, table, width, consumed):
                for m in range(UN // 2):
                    need(pool, consumed, UN * q + 2 * m + 2 - UN)
                    g.tensor_copy(idx_stage[:, 2 * m:2 * m + 2],
                                  src_idx[:, bass.ds(UN * q + 2 * m, 2)]).then_inc(staged[ph], 1)
                    pool.wait_ge(staged[ph], UN // 2 * q + m + 1)
                    pool.sem_inc(S["gate"], 1)
                    for k in range(2 * m, 2 * m + 2):
                        g.indirect_dma_start(
                            out=gat[:, k, 0:width], out_offset=None, in_=table[:, :],
                            in_offset=bass.IndirectOffsetOnAxis(ap=idx_stage[:, k:k + 1], axis=0),
                        ).then_inc(gath[ph][k], 16)

            pool.wait_ge(S["chunk_ready"], 1)
            pool.wait_ge(S["pad_in"], 6 * 16)
            for j, lst in enumerate((dst_pad, src_pad)):
                g.indirect_dma_start(
                    out=lst_i[:, j, :], out_offset=None, in_=lst.rearrange("(c n) -> c n", n=GE),
                    in_offset=bass.IndirectOffsetOnAxis(ap=chunk_i[:, 0:1], axis=0),
                ).then_inc(S["lists_in"], 16)
            pool.wait_ge(S["lists_ready"], 2)
            for half in xl_stored:
                pool.wait_ge(half, NT // 2 * 16)
            gather(0, "a", xl_tab, RW, S["z_ready"])
            with pool.Fori(1, Q) as q:
                gather(q, "a", xl_tab, RW, S["z_ready"])
            pool.wait_ge(S["z_ready"], T)
            gather(0, "c", xl_tab, RW, S["msg_ready"])
            with pool.Fori(1, Q) as q:
                gather(q, "c", xl_tab, RW, S["msg_ready"])
            pool.wait_ge(S["x2_stored"], NT * 16)
            gather(0, "d", x2_tab, D, S["t_ready"])
            with pool.Fori(1, Q) as q:
                gather(q, "d", x2_tab, D, S["t_ready"])

        @block.scalar
        def _(act):
            a = nc.scalar
            for name, v, _ in PAR:
                r0, r1 = par_at[name]
                act.dma_start(par_row[r0:r1, :], v.rearrange("(c p) -> c p", p=P)).then_inc(S["par_in"], 16)
            act.dma_start(src_pad[0:E].rearrange("(p f) -> p f", p=16),
                          src.rearrange("(p f) -> p f", p=16)).then_inc(S["pad_in"], 16)
            act.dma_start(dst_pad[0:E].rearrange("(p f) -> p f", p=16),
                          dst.rearrange("(p f) -> p f", p=16)).then_inc(S["pad_in"], 16)
            act.wait_ge(S["cst"], 9)
            act.dma_start(dst_pad[E:EP].rearrange("(p f) -> p f", p=4), pads_i[:]).then_inc(S["pad_in"], 16)
            act.dma_start(src_pad[E:EP].rearrange("(p f) -> p f", p=4), padz_i[:]).then_inc(S["pad_in"], 16)
            act.dma_start(ea_pad[E:EP, :].rearrange("(p f) c -> p (f c)", p=PADP), padz[:]).then_inc(S["pad_in"], 16)

            def ln_root(ready, n):
                act.wait_ge(ready, n)
                a.activation(rstd[:], rstd[:], ACT.Sqrt).then_inc(ready, 1)

            def affine_T(t, bank, mm, gcol, bcol, ready):
                act.wait_ge(mm, t + 1)
                for c in range(FC):
                    i = a.activation(hT[:, c, t * P:(t + 1) * P], ps[:, bank, c * P:(c + 1) * P], ACT.Identity,
                                     bias=bcol[:, c:c + 1], scale=gcol[:, c:c + 1])
                i.then_inc(ready, 1)

            ln_root(S["ln1"], 3)
            act.wait_ge(S["par_ready"], 1)
            for t in range(NT + 1):
                if t < NT:
                    affine_T(t, t % 2, S["ztT"], ln1gc, ln1bc, S["hT_ready"])
                if t > 0:
                    u = t - 1
                    act.wait_ge(S["xl_mm"], u + 1)
                    if u >= 2:
                        act.wait_ge(xl_stored[u % 2], 16 * (u // 2))
                    a.copy(xl_sb[:, u % 2, 0:D], ps[:, 2 + u % 2, :]).then_inc(S["xl_cp"], 1)
                    act.wait_ge(S["xr_mm"], u + 1)
                    if u == NT - 1:
                        act.wait_ge(S["cst"], 3)
                    a.copy(xr_hi[:, u, 0:D], ps[:, 4 + u % 2, :]).then_inc(S["xr_cp"], 1)

            def transposed_onehot(G, h):
                act.wait_ge(S["ot_p"], G + 1)
                need(act, S["xr_done"], TPG * (G - 2) + TPG)
                a.copy(onehotT[:, h, :], ps[:, 6, :]).then_inc(S["ot_ready"], 1)

            def scores_out(G, h):
                act.wait_ge(S["sc_done"], 2 * G + 2)
                need(act, est_stored[h], 8 * (G - h) + 16 * h)
                a.copy(est[:, h, :], ps[0:2 * H, 7, :]).then_inc(S["e_out"], 1)

            def rectify(q, first, last):
                for u in range(UN):
                    i, G, h = UN * q + u, 2 * q + u // TPG, u // TPG
                    if u % TPG == 0 and not (last and h == 1):
                        transposed_onehot(G + 1, 1 - h)
                    act.wait_ge(S["t_done"], i + 1)
                    m, w = (u // 2) % 2, u % 2
                    need(act, S["sc_done"], 4 * q + u // 2 - 1)
                    z = ps[:, 2 + u % 4, :].rearrange("p (c n) -> p c n", c=FC)
                    a.activation(zr_hi[:, m, :, w * P:(w + 1) * P], z[:, 0:SPLIT], ACT.Relu)
                    a.activation(zr_full[:, m, :, w * P:(w + 1) * P], z[:, SPLIT:FC], ACT.Relu).then_inc(S["hi_ready"], 1)
                    if u % TPG == 2 and not (first and h == 0):
                        scores_out(G - 1, 1 - h)

            act.sem_inc(est_stored[1], 16)
            transposed_onehot(0, 0)
            rectify(0, True, False)
            with act.Fori(1, Q - 1) as q:
                rectify(q, False, False)
            rectify(Q - 1, False, True)
            scores_out(NG - 1, 1)

            for h in range(2):
                act.wait_ge(est_stored[h], Q * 16 + 16 * h)
            for j in range(CH):
                act.dma_start(pen[j * H:(j + 1) * H, 0:CL], e_scr[H:2 * H, j * CL:(j + 1) * CL]).then_inc(S["es_loaded"], 16)
            for b in range(6):
                w = min(4, CT - 4 * b) * P
                act.wait_ge(S["xk_p"], 2 * b + 2)
                a.copy(KX[:, b * D:b * D + w], ps[:, (2 * b + 1) % 8, 0:w]).then_inc(S["k_ready"], 1)
            act.wait_ge(S["m_ready"], 1)
            a.activation(X[:], X[:], ACT.Exp).then_inc(S["ex_ready"], 1)

            ln_root(S["ln2"], 3)
            for t in range(NT):
                affine_T(t, t % 2, S["z2T"], ln2gc, ln2bc, S["h2T_ready"])
            n = 0
            for ch in range(3):
                w = min(D, NP - ch * D)
                if ch:
                    act.wait_ge(S["f2_mm"], TPG * ch)
                for f in range(F1 // P):
                    act.wait_ge(S["f1_mm"], n + 1)
                    a.activation(hid[:, f, 0:w], ps[:, 2 + n % 2, 0:w], ACT.Gelu,
                                 bias=b1c[:, f:f + 1]).then_inc(S["hid_ready"], 1)
                    n += 1
            ln_root(S["ln2"], 7)

            def edge_hi(G, h):
                act.wait_ge(ea_in[h], 16 * (G // 2) + 16 if isinstance(G, int) else 8 * (G - h) + 16)
                need(act, S["ea_p"], G - 1)
                a.copy(ea_hl[:, h, :, 0:ED], ea_g[:, h, :].rearrange("p (k c) -> p k c", k=TPG)).then_inc(S["ea_hi"], 1)

            def edge_T(G, h):
                act.wait_ge(S["ea_p"], G + 1)
                need(act, S["tw_done"], TPG * (G - 2) + TPG)
                a.copy(eaT[:, h, :], ps[:, 6, :]).then_inc(S["ea_ready"], 1)

            def messages(q, first, last):
                for u in range(UN):
                    i, G, h = UN * q + u, 2 * q + u // TPG, u // TPG
                    if u % TPG == 1 and not (last and h == 1):
                        edge_T(G + 1, 1 - h)
                    if u % TPG == 3 and not last:
                        edge_hi(G + 2, h)
                    act.wait_ge(S["t_ready"], i + 1)
                    need(act, S["ag2_done"], i - 3)
                    a.activation(zbuf[:, 4 + u % 4, 0:D], zbuf[:, u % 4, 0:D], ACT.Relu).then_inc(S["m2_ready"], 1)

            act.wait_ge(S["we_in"], 32)
            a.copy(We_hi[:], We2[:]).then_inc(S["We_ready"], 1)
            edge_hi(0, 0)
            edge_hi(1, 1)
            edge_T(0, 0)
            messages(0, True, False)
            with act.Fori(1, Q - 1) as q:
                messages(q, False, False)
            messages(Q - 1, False, True)

            for t in range(NT):
                act.wait_ge(S["hhT_p"], t + 1)
                a.copy(hT[:, :, t * P:(t + 1) * P], ps[:, t % 2, :].rearrange("p (c n) -> p c n", c=FC)).then_inc(S["hhT_ready"], 1)
            n = 0
            for f in range(F2 // P):
                for ch in range(3):
                    w = min(D, NP - ch * D)
                    act.wait_ge(S["u_mm"], n + 1)
                    a.activation(uT[:, f, ch * D:ch * D + w], ps[:, 2 + n % 2, 0:w], ACT.Identity,
                                 bias=c1c[:, f:f + 1]).then_inc(S["u_cp"], 1)
                    n += 1
            act.wait_ge(S["bn1"], 4)
            a.activation(bnsc[:], bnsc[:], ACT.Sqrt).then_inc(S["bn1"], 1)
            act.wait_ge(S["bn1s"], 1)
            for f in range(F2 // P):
                a.activation(uT[:, f, :], uT[:, f, :], ACT.Silu, bias=bnsh[:, f:f + 1],
                             scale=bnsc[:, f:f + 1]).then_inc(S["sT_ready"], 1)
            n = 0
            for f in range(FC):
                for ch in range(3):
                    w = min(D, NP - ch * D)
                    act.wait_ge(S["y_mm"], n + 1)
                    a.activation(yT[:, f, ch * D:ch * D + w], ps[:, 4 + n % 2, 0:w], ACT.Identity,
                                 bias=c2c[:, f:f + 1]).then_inc(S["y_cp"], 1)
                    n += 1
            act.wait_ge(S["bn2"], 4)
            a.activation(bnsc[:, 0:FC], bnsc[:, 0:FC], ACT.Sqrt).then_inc(S["bn2"], 1)
            act.wait_ge(S["bn2s"], 1)
            for f in range(FC):
                a.activation(yT[:, f, :], yT[:, f, :], ACT.Silu, bias=bnsh[:, f:f + 1],
                             scale=bnsc[:, f:f + 1]).then_inc(S["yT_ready"], 1)
            ln_root(S["ln4"], 3)

        @block.vector
        def _(dve):
            v = nc.vector
            count = [0]

            def link(ins):
                count[0] += 1
                ins.then_inc(S["dvec"], 1)
                dve.wait_ge(S["dvec"], count[0])

            v.memset(ones[:], 1.0).then_inc(S["cstv"], 1)
            dve.wait_ge(S["cst"], 9)
            link(v.tensor_copy(iota[:], iota_i[:]))
            link(v.tensor_copy(bounds[:], bounds_i[:]))
            link(v.tensor_copy(iotaK[:], iotaK_i[:]))
            dve.wait_ge(S["dst_in"], 16)
            link(v.tensor_copy(dst_f[0:125, :], dst_i[0:125, :]))
            link(v.tensor_tensor(cmp[0:125], dst_f[0:125, :].unsqueeze(1).broadcast_to([125, NT, E // 125]),
                                 bounds[0:125, 0:NT].unsqueeze(2).broadcast_to([125, NT, E // 125]), ALU.is_lt))
            v.tensor_reduce(cnt[0:125, 0:NT], cmp[0:125], AX, ALU.add).then_inc(S["cnt_ready"], 1)
            rp, cn, kn, ginc, gexc, bs, db, zr, first, final = (rows[:, j, 0:NT] for j in range(10))
            link(v.memset(rows[:], 0.0))
            dve.wait_ge(S["rp_ready"], 1)
            link(v.tensor_copy(rp, ps[0:1, 7, 0:NT]))
            link(v.memset(rows[:, 0, NT:NT + 1], float(E)))
            link(v.tensor_tensor(cn, rows[:, 0, 1:NT + 1], rp, ALU.subtract))
            for edge, op, o in ((rp, ALU.is_ge, first), (rows[:, 0, 1:NT + 1], ALU.is_gt, final)):
                link(v.tensor_tensor(kcmp[:], edge.unsqueeze(2).broadcast_to([1, NT, NC - 1]),
                                     iotaK[:, 1:NC].unsqueeze(1).broadcast_to([1, NT, NC - 1]), op))
                link(v.tensor_reduce(o, kcmp[:], AX, ALU.add))
            link(v.tensor_scalar(cn, cn, 0.0, None, ALU.is_gt))
            link(v.scalar_tensor_tensor(kn, first, -1.0, final, ALU.mult, ALU.add))
            link(v.scalar_tensor_tensor(kn, kn, 1.0, cn, ALU.add, ALU.mult))
            link(v.tensor_tensor_scan(ginc, kn, zr, 0.0, ALU.add, ALU.add))
            link(v.tensor_tensor(gexc, ginc, kn, ALU.subtract))
            link(v.scalar_tensor_tensor(bs, gexc, -1.0, first, ALU.mult, ALU.add))
            link(v.tensor_copy(rows[:, 6, 0:1], rows[:, 5, 0:1]))
            link(v.tensor_tensor(rows[:, 6, 1:NT], rows[:, 5, 1:NT], rows[:, 5, 0:NT - 1], ALU.subtract))
            link(v.tensor_tensor(gcmp[:], iota[0:1, 0:NG].unsqueeze(2).broadcast_to([1, NG, NT]),
                                 gexc.unsqueeze(1).broadcast_to([1, NG, NT]), ALU.is_ge))
            link(v.tensor_tensor(gprod[:], gcmp[:], db.unsqueeze(1).broadcast_to([1, NG, NT]), ALU.mult))
            link(v.tensor_reduce(ngf[:], gcmp[:], AX, ALU.add))
            link(v.tensor_scalar(ngf[:], ngf[:], -1.0, None, ALU.add))
            link(v.tensor_reduce(sf[:], gprod[:], AX, ALU.add))
            link(v.tensor_tensor(sf[:], sf[:], iota[0:1, 0:NG], ALU.add))
            link(v.tensor_scalar(sf[:], sf[:], float(NC - 1), None, ALU.min))
            v.tensor_copy(ng_i[:], ngf[:])
            v.tensor_scalar(s_i[:], sf[:], float(GE), None, ALU.mult).then_inc(S["tab_ready"], 1)
            dve.wait_ge(S["ngb_ready"], 1)
            v.tensor_copy(chunk_i[:], ps[0:NG, 6, NG:NG + 1]).then_inc(S["chunk_ready"], 1)
            link(v.tensor_copy(ngb[:], ps[:, 6, 0:NG]))
            dve.wait_ge(S["par_T"], 1)
            v.tensor_copy(par[:], ps[:, 7, P:P + NPAR]).then_inc(S["par_ready"], 1)
            dve.wait_ge(S["par_ready"], 1)
            link(v.memset(att_parts[:].bitcast(F32), 0.0))
            link(v.memset(att_full[:], 0.0))
            link(v.tensor_scalar(att8[:, 0, :], attc, 0.8, None, ALU.mult))
            for i in range(2):
                r, d = slice(i * C, (i + 1) * C), 2 * H + 2
                v.tensor_copy(att_full[r, i::d], att8[r, 0, :])
                link(v.tensor_copy(att_parts[r, i::d][:, 0:FC], att8[r, 0, :]))
                v.tensor_tensor(att_parts[r, H + i::d], att8[r, 0, :], att_parts[r, i::d][:, 0:FC].bitcast(F32),
                                ALU.subtract).then_inc(S["cstv"], 1)
            dve.wait_ge(S["bc_in"], 5 * 16)
            link(v.tensor_scalar(att_bc[:], att_bc[:], 0.2, None, ALU.mult))

            def ln_stats(srcs, lnsem, n0, waits=None):
                for t in range(NT):
                    if waits:
                        waits(t)
                    i = v.bn_stats(stats[:, t, :], srcs(t))
                link(i)
                for t in range(NT):
                    i = v.bn_aggr(mv[:, t, :], stats[:, t, :])
                link(i)
                v.tensor_scalar(rstd[:], mv[:, :, 1], LN_EPS, None, ALU.add).then_inc(lnsem, 3)
                dve.wait_ge(lnsem, n0 + 4)
                link(v.reciprocal(rstd[:], rstd[:]))

            def ln_rows(o, i, t):
                return v.tensor_scalar(o, i, mv[:, t, 0:1], rstd[:, t:t + 1], ALU.subtract, ALU.mult)

            ln_stats(lambda t: x_sb[:, t, :], S["ln1"], 0, lambda t: dve.wait_ge(x_tile[t], 16))
            for t in range(NT + 2):
                if t < NT:
                    if t >= 2:
                        dve.wait_ge(S["ztT"], t - 1)
                    ln_rows(zt[:, t % 2, :], x_sb[:, t, :], t).then_inc(S["zt_ready"], 1)
                if t >= 2:
                    u = t - 2
                    dve.wait_ge(S["xl_cp"], u + 1)
                    link(v.tensor_tensor(prod[:, 0, :], xl_sb[:, u % 2, 0:D], att_bc[:], ALU.mult))
                    v.tensor_reduce(xl_sb[:, u % 2, D:RW], prod[:, 0, :].rearrange("p (h c) -> p h c", h=H), AX,
                                    ALU.add).then_inc(S["xl_dve"], 1)
                    dve.wait_ge(S["xr_cp"], u + 1)
                    link(v.tensor_tensor(prod[:, 1, :], ps[:, 4 + u % 2, :], att_bc[:], ALU.mult))
                    link(v.tensor_reduce(srow[:, 0, :], prod[:, 1, :].rearrange("p (h c) -> p h c", h=H), AX, ALU.add))
                    if u == NT - 1:
                        dve.wait_ge(S["cst"], 3)
                    link(v.tensor_copy(xr_hi[:, u, D:RW], srow[:, 0, :]))
                    v.tensor_tensor(xr_lo[:, u, D:RW], srow[:, 0, :], xr_hi[:, u, D:RW].bitcast(F32), ALU.subtract)
                    v.tensor_tensor(xr_lo[:, u, 0:D], ps[:, 4 + u % 2, :], xr_hi[:, u, 0:D].bitcast(F32),
                                    ALU.subtract).then_inc(S["xr_dve"], 1)

            dve.wait_ge(S["lists_in"], 32)
            for j in range(2):
                v.tensor_copy(lst_f[:, j, :], lst_i[:, j, :]).then_inc(S["lists_f"], 1)
            dve.wait_ge(S["listT"], 2)

            def by_tile(t_):
                return t_[:].rearrange("p (g k) -> p g k", k=TPG)

            def from_lists(bank):
                return ps[:, bank, 0:TPG * NG].rearrange("p (k g) -> p g k", k=TPG)

            ngb_t = ngb[:].unsqueeze(2).broadcast_to([P, NG, TPG])
            v.tensor_copy(by_tile(src_idx), from_lists(1)).then_inc(S["lists_ready"], 1)
            link(v.tensor_copy(by_tile(dcol), from_lists(0)))
            link(v.scalar_tensor_tensor(by_tile(drel), ngb_t, -float(P), by_tile(dcol), ALU.mult, ALU.add))
            link(v.scalar_tensor_tensor(by_tile(key), ngb_t, float(KEY), by_tile(dcol), ALU.mult, ALU.add))
            link(v.tensor_scalar(key[:], key[:], 1.0, None, ALU.add))
            v.memset(cols[:], 0.0).then_inc(S["lists_ready"], 1)

            def build_onehot_tile(G, h, k, ready):
                v.tensor_scalar(onehot[:, h, k, :], iota[:], drel[:, bass.ds(TPG * G + k, 1)], None,
                                ALU.is_equal).then_inc(ready, 1)

            def build_onehot(G, h, ready):
                for k in range(TPG):
                    build_onehot_tile(G, h, k, ready)

            def rest(i, u):
                dve.wait_ge(S["hi_ready"], i + 1)
                m, w = (u // 2) % 2, u % 2
                z = ps[:, 2 + u % 4, 0:SPLIT * P].rearrange("p (c n) -> p c n", c=SPLIT)
                v.scalar_tensor_tensor(zr_lo[:, m, :, w * P:(w + 1) * P], z, 0.0,
                                       zr_hi[:, m, :, w * P:(w + 1) * P].bitcast(F32), ALU.max, ALU.subtract
                                       ).then_inc(S["lo_ready"], 1)

            def sum_rows(q, first, last):
                for u in range(UN):
                    i, G, h = UN * q + u, 2 * q + u // TPG, u // TPG
                    dve.wait_ge(S["xr_done"], i + 1)
                    dve.wait_ge(gath["a"][u], 16 * q + 16)
                    need(dve, S["t_done"], i - UN + 1)
                    if u % 2:
                        v.tensor_copy(e_all[:, bass.ds((i - 1) * H, 2 * H)].rearrange("p (k h) -> p k h", k=2),
                                      gat[:, u - 1:u + 1, D:RW]).then_inc(S["slin_ready"], 1)
                    v.tensor_tensor(zbuf[:, u, 0:D], gat[:, u, 0:D], ps[:, u % 2, :], ALU.add).then_inc(S["z_ready"], 1)
                    if not (first and u < 2):
                        rest(i - 2, (u - 2) % UN)
                    if not last:
                        need(dve, S["ot_p"], G + 1)
                        build_onehot_tile(G + 2, h, u % TPG, S["o_ready"])

            build_onehot(0, 0, S["o_ready"])
            build_onehot(1, 1, S["o_ready"])
            sum_rows(0, True, False)
            with dve.Fori(1, Q - 1) as q:
                sum_rows(q, False, False)
            sum_rows(Q - 1, False, True)
            rest(T - 2, UN - 2)
            rest(T - 1, UN - 1)

            dve.wait_ge(S["slin_ready"], T // 2)
            dve.wait_ge(S["sc_done"], T // 2)
            v.tensor_copy(perm[:].rearrange("p (b j h) -> p b j h", b=CT, j=CH),
                          e_all[:].rearrange("p (j b h) -> p b j h", j=CH, b=CT)).then_inc(S["perm_ready"], 1)
            for b in range(CT):
                i = v.tensor_copy(permk[:, b * P:(b + 1) * P].rearrange("p (j h) -> p j h", j=CH),
                                  key[:].rearrange("p (j b) -> p b j", b=CT)[:, b, :].unsqueeze(2).broadcast_to([P, CH, H]))
            i.then_inc(S["perm_ready"], 1)
            dve.wait_ge(S["es_loaded"], 2 * CH * 16)
            link(v.tensor_tensor(X[:], X[:], pen[:, 0:CL], ALU.add))
            for b in range(6):
                w = min(4, CT - 4 * b) * P
                dve.wait_ge(S["xk_p"], 2 * b + 1)
                v.tensor_tensor(X[:, b * D:b * D + w], X[:, b * D:b * D + w], ps[:, (2 * b) % 8, 0:w],
                                ALU.add).then_inc(S["xs_ready"], 1)
            dve.wait_ge(S["xs_ready"], 6)
            dve.wait_ge(S["k_ready"], 6)
            link(v.memset(pen[:], 0.0))
            link(v.tensor_tensor(pen[:, 1:CL], KX[:, 1:CL], KX[:, 0:CL - 1], ALU.not_equal))
            link(v.tensor_scalar(pen[:, 1:CL], pen[:, 1:CL], -BIG, None, ALU.mult))
            link(v.tensor_copy(cols[:, 0:1], KX[:, 0:1]))
            link(v.tensor_copy(cols[:, 1:2], KX[:, CL - 1:CL]))
            link(v.tensor_tensor(cols[:, 2:3], cols[:, 0:1], cols[:, 1:2], ALU.is_equal))
            v.memset(rowbuf[:], 0.0).then_inc(S["colp"], 1)
            for way in range(2):
                o = fwd if way == 0 else bwd
                step = 1 if way == 0 else -1
                data = X if way == 0 else fwd
                p_ = pen[:, 0:CL] if way == 0 else pen[:, 1:CL + 1]

                def scan(initial):
                    return v.tensor_tensor_scan(o[:, ::step], p_[:, ::step], data[:, ::step], initial, ALU.add, ALU.max)

                link(scan(-BIG))
                endcol = CL - 1 if way == 0 else 0
                k0 = 3 + 6 * way
                link(v.tensor_copy(cols[:, k0:k0 + 1], o[:, endcol:endcol + 1]))
                dve.wait_ge(S["colp_p"], way + 1)
                link(v.tensor_tensor(cols[:, k0 + 1:k0 + 2], ps[:, 0, 2 * way:2 * way + 1], cols[:, way:way + 1], ALU.is_equal))
                link(v.tensor_tensor(cols[:, k0 + 2:k0 + 3], cols[:, k0 + 1:k0 + 2], cols[:, 2:3], ALU.mult))
                link(v.tensor_scalar(cols[:, k0 + 1:k0 + 3], cols[:, k0 + 1:k0 + 3], -1.0, BIG, ALU.add, ALU.mult))
                v.memset(cols[:, k0 + 3:k0 + 4], 0.0).then_inc(S["colp"], 1)
                dve.wait_ge(S["rowp"], way + 1)
                for j in range(2):
                    link(v.tensor_copy(rowbuf[:, j, :].rearrange("p (h j) -> p h j", h=H),
                                       ps[0:1, 1, j * P:(j + 1) * P].rearrange("p (j h) -> p h j", h=H)))
                link(v.tensor_tensor_scan(rowbuf[:, 2, ::step], rowbuf[:, 1, ::step], rowbuf[:, 0, ::step], -BIG,
                                          ALU.add, ALU.max))
                v.tensor_copy(rowbuf[:, 3, :].rearrange("p (j h) -> p j h", h=H),
                              rowbuf[:, 2, :].rearrange("p (h j) -> p j h", h=H)).then_inc(S["rowv"], 1)
                dve.wait_ge(S["carry_p"], 2 * way + 1)
                v.tensor_copy(cols[:, k0 + 4:k0 + 5], ps[:, 2, 0:1]).then_inc(S["carry_c"], 1)
                dve.wait_ge(S["carry_p"], 2 * way + 2)
                link(v.tensor_tensor(cols[:, k0 + 5:k0 + 6], ps[:, 2, 2:3], cols[:, k0 + 1:k0 + 2], ALU.add))
                link(scan(cols[:, k0 + 5:k0 + 6]))
            v.tensor_tensor(X[:], X[:], bwd[:], ALU.subtract).then_inc(S["m_ready"], 1)
            for b in range(6):
                n = min(4, CT - 4 * b)
                dve.wait_ge(S["exT"], b + 1)
                v.tensor_copy(e_all[:].rearrange("p (j b h) -> p b j h", j=CH, b=CT)[:, 4 * b:4 * b + n],
                              ps[:, b % 4, 0:n * P].rearrange("p (b j h) -> p b j h", b=n, j=CH)).then_inc(S["ex_back"], 1)

            def add_sums(G, h, src_ps, width, done, agg):
                n = dve.value_load(ng_i[0:1, bass.ds(G, 1)], min_val=0, max_val=NT - 1)
                dve.wait_ge(agg, TPG * G + TPG)
                need(dve, done, G)
                v.tensor_tensor(acc[:, bass.ds(n, 1), 0:width], acc[:, bass.ds(n, 1), 0:width],
                                src_ps.unsqueeze(1), ALU.add).then_inc(done, 1)

            def weigh_rows(q, first, last):
                for u in range(UN):
                    i, G, h = UN * q + u, 2 * q + u // TPG, u // TPG
                    dve.wait_ge(gath["c"][u], 16 * q + 16)
                    need(dve, S["agg_done"], i - UN + 1)
                    v.tensor_tensor(zbuf[:, u, 0:D].rearrange("p (h c) -> p h c", h=H),
                                    gat[:, u, 0:D].rearrange("p (h c) -> p h c", h=H),
                                    e_all[:, bass.ds(i * H, H)].unsqueeze(2).broadcast_to([P, H, C]),
                                    ALU.mult).then_inc(S["msg_ready"], 1)
                    if u % TPG == 1 and not (first and h == 0):
                        add_sums(G - 1, 1 - h, ps_row[1 - h], RW, S["acc_done"], S["agg_done"])
                    if u % TPG == 2 and not (last and h == 1):
                        need(dve, S["agg_done"], TPG * G)
                        build_onehot(G + 1, 1 - h, S["o2_ready"])

            link(v.memset(acc[:], 0.0))
            dve.wait_ge(S["ex_back"], 6)
            build_onehot(0, 0, S["o2_ready"])
            weigh_rows(0, True, False)
            with dve.Fori(1, Q - 1) as q:
                weigh_rows(q, False, False)
            weigh_rows(Q - 1, False, True)
            add_sums(NG - 1, 1, ps_row[1], RW, S["acc_done"], S["agg_done"])

            dve.wait_ge(S["acc_done"], NG)
            den = acc[:, :, D:RW]
            link(v.tensor_scalar(den, den, 1e-16, None, ALU.add))
            link(v.reciprocal(den, den))
            for t in range(NT):
                i = v.tensor_tensor(acc[:, t, 0:D].rearrange("p (h c) -> p h c", h=H),
                                    acc[:, t, 0:D].rearrange("p (h c) -> p h c", h=H),
                                    acc[:, t, D:RW].unsqueeze(2).broadcast_to([P, H, C]), ALU.mult)
            link(i)
            for t in range(NT):
                i = v.tensor_tensor(acc[:, t, 0:D], acc[:, t, 0:D], gb_bc[:], ALU.add)
            link(i)
            x1 = acc[:, :, 0:D]
            link(v.tensor_tensor(x1, x1, x_sb[:], ALU.add))
            ln_stats(lambda t: acc[:, t, 0:D], S["ln2"], 0)
            for t in range(NT):
                if t >= 2:
                    dve.wait_ge(S["z2T"], t - 1)
                ln_rows(lnz[:, t % 2, :], acc[:, t, 0:D], t).then_inc(S["z2_ready"], 1)
            link(v.tensor_tensor(x_sb[:], x_sb[:], x1, ALU.add))
            for t in range(NT):
                i = v.tensor_tensor(x_sb[:, t, :], x_sb[:, t, :], b2_bc[:], ALU.add)
            link(i)
            for t in range(NT):
                dve.wait_ge(S["f2_mm"], t + 1)
                i = v.tensor_tensor(x_sb[:, t, :], x_sb[:, t, :], ps[:, 4 + t % 2, :], ALU.add)
                i.then_inc(S["u_ready"], 1)
            dve.wait_ge(S["u_ready"], NT)
            ln_stats(lambda t: x_sb[:, t, :], S["ln2"], 4)
            for t in range(NT):
                i = ln_rows(x_sb[:, t, :], x_sb[:, t, :], t)
            link(i)
            for t in range(NT):
                v.tensor_tensor(vrow[:, t, :], x_sb[:, t, :], be_bc[:], ALU.add).then_inc(S["x2_ready"], 1)
            link(v.tensor_scalar(cols[:, 15:16], epsc[:], 1.0, None, ALU.add))
            link(v.tensor_scalar(acc[:, :, 0:D], x_sb[:], cols[:, 15:16], None, ALU.mult))

            def edge_rest(G, h):
                dve.wait_ge(S["ea_hi"], G + 1)
                v.tensor_tensor(ea_hl[:, h, :, ED:2 * ED], ea_g[:, h, :].rearrange("p (k c) -> p k c", k=TPG),
                                ea_hl[:, h, :, 0:ED].bitcast(F32), ALU.subtract).then_inc(S["ea_split"], 1)

            def edge_sum(q, first, last):
                for u in range(UN):
                    i, G, h = UN * q + u, 2 * q + u // TPG, u // TPG
                    dve.wait_ge(gath["d"][u], 16 * q + 16)
                    dve.wait_ge(S["tw_done"], i + 1)
                    need(dve, S["m2_ready"], i - 3)
                    v.tensor_tensor(zbuf[:, u % 4, 0:D], gat[:, u, 0:D], ps[:, 4 + u % 2, :], ALU.add).then_inc(S["t_ready"], 1)
                    if u % TPG == 1 and not (first and h == 0):
                        add_sums(G - 1, 1 - h, ps[:, 2 * (1 - h), :], D, S["acc2_done"], S["ag2_done"])
                    if u % TPG == 2 and not (last and h == 1):
                        need(dve, S["ag2_done"], TPG * G)
                        build_onehot(G + 1, 1 - h, S["o3_ready"])
                    if u % TPG == 3 and not last:
                        edge_rest(G + 2, h)

            dve.wait_ge(S["We_ready"], 1)
            v.tensor_tensor(We_lo[:], We2[:], We_hi[:].bitcast(F32), ALU.subtract).then_inc(S["We_ready"], 1)
            edge_rest(0, 0)
            edge_rest(1, 1)
            dve.wait_ge(S["x2_stored"], NT * 16)
            build_onehot(0, 0, S["o3_ready"])
            edge_sum(0, True, False)
            with dve.Fori(1, Q - 1) as q:
                edge_sum(q, False, False)
            edge_sum(Q - 1, False, True)
            add_sums(NG - 1, 1, ps[:, 2, :], D, S["acc2_done"], S["ag2_done"])

            def bn(data, nf, cp, s, g_, be_, ssc):
                for f in range(nf):
                    dve.wait_ge(cp, 3 * f + 3)
                    for ch in range(3):
                        w = min(D, N - ch * D)
                        i = v.bn_stats(bnst[:, f, ch, :], data[:, f, ch * D:ch * D + w])
                link(i)
                for f in range(nf):
                    i = v.bn_aggr(bnmv[:, f, :], bnst[:, f, :, :].rearrange("p a b -> p (a b)"))
                link(i)
                v.tensor_scalar(bnsc[:, 0:nf], bnmv[:, 0:nf, 1], 1e-5, None, ALU.add).then_inc(s, 4)
                dve.wait_ge(s, 5)
                link(v.reciprocal(bnsc[:, 0:nf], bnsc[:, 0:nf]))
                link(v.tensor_tensor(bnsc[:, 0:nf], bnsc[:, 0:nf], g_, ALU.mult))
                link(v.tensor_tensor(bnsh[:, 0:nf], bnmv[:, 0:nf, 0], bnsc[:, 0:nf], ALU.mult))
                v.tensor_tensor(bnsh[:, 0:nf], be_, bnsh[:, 0:nf], ALU.subtract).then_inc(ssc, 1)

            bn(uT, F2 // P, S["u_cp"], S["bn1"], g1c, be1c, S["bn1s"])
            dve.wait_ge(S["sT_ready"], F2 // P)
            bn(yT, FC, S["y_cp"], S["bn2"], g2c, be2c, S["bn2s"])
            for t in range(NT):
                dve.wait_ge(S["yb_p"], t + 1)
                i = v.tensor_tensor(acc[:, t, 0:D], x_sb[:, t, :], ps[:, 6 + t % 2, :], ALU.add)
                i.then_inc(S["v_ready"], 1)
            dve.wait_ge(S["v_ready"], NT)
            ln_stats(lambda t: acc[:, t, 0:D], S["ln4"], 0)
            for t in range(NT):
                if t >= 2:
                    dve.wait_ge(out_stored[t % 2], 16 * (t // 2))
                ln_rows(fin[:, t % 2, :], acc[:, t, 0:D], t).then_inc(S["fin_ready"], 1)

        @block.tensor
        def _(pe):
            tm = nc.tensor
            pe.wait_ge(S["cnt_ready"], 1)
            pe.wait_ge(S["cstv"], 1)
            tm.matmul(ps[0:1, 7, 0:NT], ones[0:125, 0:1], cnt[0:125, 0:NT], start=True, stop=True).then_inc(S["rp_ready"], 1)
            pe.wait_ge(S["tab_ready"], 1)
            tm.matmul(ps[:, 6, 0:NG], ones[0:1, :], ngf[:], start=True, stop=True)
            tm.matmul(ps[0:NG, 6, NG:NG + 1], sf[:], ones[0:1, 0:1], start=True, stop=True).then_inc(S["ngb_ready"], 1)
            pe.wait_ge(S["cst"], 15)
            pe.wait_ge(S["par_in"], 16 * len(PAR))
            tm.transpose(ps[:, 7, P:P + NPAR], par_row[:], ident[0:NPAR, 0:NPAR]).then_inc(S["par_T"], 1)

            def transpose_rows(o, i):
                for c in range(FC):
                    m = tm.transpose(o[:, c * P:(c + 1) * P], i[:, c * P:(c + 1) * P], ident[:])
                return m

            for t in range(NT + 1):
                if t < NT:
                    pe.wait_ge(S["zt_ready"], t + 1)
                    if t >= 2:
                        pe.wait_ge(S["hT_ready"], t - 1)
                    transpose_rows(ps[:, t % 2, :], zt[:, t % 2, :]).then_inc(S["ztT"], 1)
                if t > 0:
                    u = t - 1
                    pe.wait_ge(S["hT_ready"], u + 1)
                    if u == 0:
                        pe.wait_ge(S["wqkv_in"], 32)
                    for w, bank, done in ((0, 2, S["xl_mm"]), (1, 4, S["xr_mm"])):
                        if u >= 2:
                            pe.wait_ge(S["xl_cp" if w == 0 else "xr_dve"], u - 1)
                        for c in range(FC):
                            m = tm.matmul(ps[:, bank + u % 2, :], hT[:, c, u * P:(u + 1) * P], Wlr[:, w, c, :],
                                          start=(c == 0), stop=(c == FC - 1))
                        m.then_inc(done, 1)
            for j in range(2):
                pe.wait_ge(S["lists_f"], j + 1)
                pe.wait_ge(S["hT_ready"], NT)
                for k in range(TPG):
                    m = tm.transpose(ps[:, j, k * NG:(k + 1) * NG], lst_f[:, j, k * P:(k + 1) * P], ident[0:NG, 0:NG])
                m.then_inc(S["listT"], 1)

            def onehot_T(G, h):
                pe.wait_ge(S["o_ready"], TPG * G + TPG)
                need(pe, S["ot_ready"], G)
                for k in range(TPG):
                    m = tm.transpose(ps[:, 6, k * P:(k + 1) * P], onehot[:, h, k, :], ident[:])
                m.then_inc(S["ot_p"], 1)

            def dst_rows(i, G, u, h, n):
                if u % TPG == 0:
                    pe.wait_ge(S["ot_ready"], G + 1)
                need(pe, S["z_ready"], i - 1)
                k = u % TPG
                w = onehotT[:, h, k * P:(k + 1) * P]
                for part, tab in enumerate((xr_hi, xr_lo)):
                    m = tm.matmul(ps[:, u % 2, :], w, tab[:, bass.ds(n, 1), 0:D], start=(part == 0), stop=(part == 1))
                m.then_inc(S["xr_done"], 1)

            def z_T(i, u):
                pe.wait_ge(S["z_ready"], i + 1)
                need(pe, S["lo_ready"], i - 3)
                transpose_rows(ps[:, 2 + u % 4, :], zbuf[:, u, :]).then_inc(S["t_done"], 1)

            def scores(m, G, pair):
                pe.wait_ge(S["lo_ready"], 2 * m + 2)
                if pair % 2 == 0:
                    need(pe, S["e_out"], G)
                o = ps[0:2 * H, 7, (pair % 2) * 2 * P:(pair % 2 + 1) * 2 * P]
                for c in range(FC):
                    w = slice(c * 2 * H, (c + 1) * 2 * H)
                    if c < SPLIT:
                        tm.matmul(o, att_parts[:, w], zr_hi[:, pair % 2, c, :], start=(c == 0), stop=False)
                        i = tm.matmul(o, att_parts[:, w], zr_lo[:, pair % 2, c, :], start=False, stop=(c == FC - 1))
                    else:
                        i = tm.matmul(o, att_full[:, w], zr_full[:, pair % 2, c - SPLIT, :], start=(c == 0),
                                      stop=(c == FC - 1))
                i.then_inc(S["sc_done"], 1)

            def tile_of(G):
                return pe.value_load(ng_i[0:1, bass.ds(G, 1)], min_val=0, max_val=NT - 1)

            def phase_a(q, first, last):
                n = [tile_of(2 * q), tile_of(2 * q + 1), None if last else tile_of(2 * q + 2)]
                for u in range(UN):
                    i, G, h = UN * q + u, 2 * q + u // TPG, u // TPG
                    if u % TPG == 0 and not (last and h == 1):
                        onehot_T(G + 1, 1 - h)
                    z_T(i, u)
                    if not (last and u >= UN - 2):
                        w = u + 2
                        dst_rows(i + 2, 2 * q + w // TPG, w % UN, (w % UN) // TPG, n[w // TPG])
                    if u % 2 and not (first and u == 1):
                        pair = (u - 3) // 2
                        scores(4 * q + pair, 2 * q + pair // 2, pair % 4)

            pe.wait_ge(S["lists_ready"], 2)
            pe.wait_ge(S["xr_dve"], NT)
            pe.wait_ge(S["xr_cp"], NT)
            pe.wait_ge(S["xl_dve"], NT)
            pe.wait_ge(S["cstv"], 3)
            onehot_T(0, 0)
            n0 = tile_of(0)
            dst_rows(0, 0, 0, 0, n0)
            dst_rows(1, 0, 1, 0, n0)
            phase_a(0, True, False)
            with pe.Fori(1, Q - 1) as q:
                phase_a(q, False, False)
            phase_a(Q - 1, False, True)
            scores(T // 2 - 1, NG - 1, 3)

            pe.wait_ge(S["e_out"], NG)
            pe.wait_ge(S["perm_ready"], 2)
            for b in range(6):
                for j, t_ in enumerate((perm, permk)):
                    bank = (2 * b + j) % 8
                    if b >= 4:
                        pe.wait_ge(S["xs_ready" if j == 0 else "k_ready"], b - 3)
                    for k in range(min(4, CT - 4 * b)):
                        m = tm.transpose(ps[:, bank, k * P:(k + 1) * P], t_[:, (4 * b + k) * P:(4 * b + k + 1) * P], ident[:])
                    m.then_inc(S["xk_p"], 1)
            for way in range(2):
                shift = shift_dn if way == 0 else shift_up
                k0 = 3 + 6 * way
                pe.wait_ge(S["colp"], 1 + way)
                tm.matmul(ps[:, 0, 2 * way:2 * way + 1], shift[:], cols[:, 1 - way:2 - way], start=True, stop=True).then_inc(S["colp_p"], 1)
                pe.wait_ge(S["colp"], 2 + way)
                tm.matmul(ps[0:1, 1, 0:P], cols[:, k0:k0 + 1], ident[:], start=True, stop=True)
                tm.matmul(ps[0:1, 1, P:2 * P], cols[:, k0 + 2:k0 + 3], ident[:], start=True, stop=True).then_inc(S["rowp"], 1)
                pe.wait_ge(S["rowv"], way + 1)
                tm.matmul(ps[:, 2, 0:1], rowbuf[:, 3, :], ones[0:1, 0:1], start=True, stop=True).then_inc(S["carry_p"], 1)
                pe.wait_ge(S["carry_c"], way + 1)
                tm.matmul(ps[:, 2, 2:3], shift[:], cols[:, k0 + 4:k0 + 5], start=True, stop=True).then_inc(S["carry_p"], 1)
            pe.wait_ge(S["ex_ready"], 1)
            for b in range(6):
                if b >= 4:
                    pe.wait_ge(S["ex_back"], b - 3)
                for k in range(min(4, CT - 4 * b)):
                    m = tm.transpose(ps[:, b % 4, k * P:(k + 1) * P], X[:, (4 * b + k) * P:(4 * b + k + 1) * P], ident[:])
                m.then_inc(S["exT"], 1)

            def sum_by_dst(q, first, last):
                for u in range(UN):
                    i, G, h, k = UN * q + u, 2 * q + u // TPG, u // TPG, u % TPG
                    if k == 0:
                        pe.wait_ge(S["o2_ready"], TPG * G + TPG)
                        need(pe, S["acc_done"], G - 1)
                    pe.wait_ge(S["msg_ready"], i + 1)
                    o = ps_row[h]
                    tm.matmul(o[:, 0:D], onehot[:, h, k, :], zbuf[:, u, 0:D], start=(k == 0), stop=(k == TPG - 1))
                    tm.matmul(o[:, D:RW], onehot[:, h, k, :], e_all[:, bass.ds(i * H, H)], start=(k == 0),
                              stop=(k == TPG - 1)).then_inc(S["agg_done"], 1)

            pe.wait_ge(S["ex_back"], 6)
            sum_by_dst(0, True, False)
            with pe.Fori(1, Q - 1) as q:
                sum_by_dst(q, False, False)
            sum_by_dst(Q - 1, False, True)

            pe.wait_ge(S["acc_done"], NG)
            for t in range(NT):
                pe.wait_ge(S["z2_ready"], t + 1)
                if t >= 2:
                    pe.wait_ge(S["h2T_ready"], t - 1)
                transpose_rows(ps[:, t % 2, :], lnz[:, t % 2, :]).then_inc(S["z2T"], 1)
            pe.wait_ge(S["w_in"], 32)
            pe.wait_ge(S["h2T_ready"], NT)
            n = 0
            for ch in range(3):
                w = min(D, NP - ch * D)
                for f in range(F1 // P):
                    if n >= 2:
                        pe.wait_ge(S["hid_ready"], n - 1)
                    for c in range(FC):
                        m = tm.matmul(ps[:, 2 + n % 2, 0:w], W1_sb[:, c, f * P:(f + 1) * P], hT[:, c, ch * D:ch * D + w],
                                      start=(c == 0), stop=(c == FC - 1))
                    m.then_inc(S["f1_mm"], 1)
                    n += 1
                for t in range(4 * ch, 4 * ch + w // P):
                    if t >= 2:
                        pe.wait_ge(S["u_ready"], t - 1)
                    for f in range(F1 // P):
                        if t == 4 * ch:
                            pe.wait_ge(S["hid_ready"], ch * (F1 // P) + f + 1)
                        m = tm.matmul(ps[:, 4 + t % 2, :], hid[:, f, (t - 4 * ch) * P:(t - 4 * ch + 1) * P], W2_sb[:, f, :],
                                      start=(f == 0), stop=(f == F1 // P - 1))
                    m.then_inc(S["f2_mm"], 1)

            def edge_T(G, h):
                pe.wait_ge(S["ea_split"], G + 1)
                need(pe, S["ea_ready"], G)
                for k in range(TPG):
                    m = tm.transpose(ps[:, 6, k * P:(k + 1) * P], ea_hl[:, h, k, :].bitcast(F32), ident[:])
                m.then_inc(S["ea_p"], 1)

            def edge_project(i, u, G, h):
                k = u % TPG
                if k == 0:
                    pe.wait_ge(S["ea_ready"], G + 1)
                need(pe, S["t_ready"], i - 1)
                for part, tab in enumerate((We_hi, We_lo)):
                    m = tm.matmul(ps[:, 4 + u % 2, :], eaT[:, h, k * P:(k + 1) * P], tab[:], start=(part == 0), stop=(part == 1))
                m.then_inc(S["tw_done"], 1)

            def sum_messages(i, u, G, h):
                k = u % TPG
                if k == 0:
                    pe.wait_ge(S["o3_ready"], TPG * G + TPG)
                    need(pe, S["acc2_done"], G - 1)
                pe.wait_ge(S["m2_ready"], i + 1)
                tm.matmul(ps[:, 2 * h, :], onehot[:, h, k, :], zbuf[:, 4 + u % 4, 0:D], start=(k == 0),
                          stop=(k == TPG - 1)).then_inc(S["ag2_done"], 1)

            def phase_d(q, first, last):
                for u in range(UN):
                    i, G, h = UN * q + u, 2 * q + u // TPG, u // TPG
                    if u % TPG == 1 and not (last and h == 1):
                        edge_T(G + 1, 1 - h)
                    if not (last and u >= UN - 2):
                        w = u + 2
                        edge_project(i + 2, w % UN, 2 * q + w // TPG, (w % UN) // TPG)
                    sum_messages(i, u, G, h)

            pe.wait_ge(S["We_ready"], 2)
            pe.wait_ge(S["u_ready"], NT)
            edge_T(0, 0)
            edge_project(0, 0, 0, 0)
            edge_project(1, 1, 0, 0)
            phase_d(0, True, False)
            with pe.Fori(1, Q - 1) as q:
                phase_d(q, False, False)
            phase_d(Q - 1, False, True)

            pe.wait_ge(S["acc2_done"], NG)
            for t in range(NT):
                if t >= 2:
                    pe.wait_ge(S["hhT_ready"], t - 1)
                transpose_rows(ps[:, t % 2, :], acc[:, t, :]).then_inc(S["hhT_p"], 1)
            pe.wait_ge(S["v_in"], 16)
            pe.wait_ge(S["hhT_ready"], NT)
            n = 0
            for f in range(F2 // P):
                for ch in range(3):
                    w = min(D, NP - ch * D)
                    if n >= 2:
                        pe.wait_ge(S["u_cp"], n - 1)
                    for c in range(FC):
                        m = tm.matmul(ps[:, 2 + n % 2, 0:w], V1_sb[:, c, f * P:(f + 1) * P], hT[:, c, ch * D:ch * D + w],
                                      start=(c == 0), stop=(c == FC - 1))
                    m.then_inc(S["u_mm"], 1)
                    n += 1
            n = 0
            pe.wait_ge(S["v2_in"], 16)
            pe.wait_ge(S["sT_ready"], F2 // P)
            for f in range(FC):
                for ch in range(3):
                    w = min(D, NP - ch * D)
                    if n >= 2:
                        pe.wait_ge(S["y_cp"], n - 1)
                    for k in range(F2 // P):
                        m = tm.matmul(ps[:, 4 + n % 2, 0:w], V2_sb[:, k, f * P:(f + 1) * P], uT[:, k, ch * D:ch * D + w],
                                      start=(k == 0), stop=(k == F2 // P - 1))
                    m.then_inc(S["y_mm"], 1)
                    n += 1
            pe.wait_ge(S["yT_ready"], FC)
            for t in range(NT):
                if t >= 2:
                    pe.wait_ge(S["v_ready"], t - 1)
                for f in range(FC):
                    m = tm.transpose(ps[:, 6 + t % 2, f * P:(f + 1) * P], yT[:, f, t * P:(t + 1) * P], ident[:])
                m.then_inc(S["yb_p"], 1)


_INS = ['x', 'src', 'dst', 'edge_attr_64', 'L0_gnn_ln1_g', 'L0_gnn_ln1_b', 'L0_gnn_Wl', 'L0_gnn_Wr', 'L0_gnn_att',
        'L0_gnn_gat_bias', 'L0_gnn_ln2_g', 'L0_gnn_ln2_b', 'L0_gnn_W1', 'L0_gnn_b1', 'L0_gnn_W2', 'L0_gnn_b2',
        'L1_gnn_W_e', 'L1_gnn_b_e', 'L1_gnn_W1', 'L1_gnn_b1', 'L1_gnn_g1', 'L1_gnn_beta1', 'L1_gnn_W2', 'L1_gnn_b2',
        'L1_gnn_g2', 'L1_gnn_beta2', 'L1_gnn_eps']
_OUTS = [((1250, 512), 'float32')]


def kernel(**inputs):
    import numpy as _np
    import concourse.bacc as _bacc
    from concourse import mybir as _mybir
    from concourse.bass_utils import run_bass_kernel_spmd as _run

    nc = _bacc.Bacc("TRN2", target_bir_lowering=False, num_devices=1)
    arrays, args = {}, []
    for name in _INS:
        a = _np.ascontiguousarray(inputs[name])
        if a.ndim == 0:
            a = a.reshape(1)
        arrays[f"in_{name}_dram"] = a
        args.append(nc.dram_tensor(f"in_{name}_dram", a.shape, _mybir.dt.from_np(a.dtype), kind="ExternalInput").ap())
    for i, (shape, dtype) in enumerate(_OUTS):
        dt = _mybir.dt.from_np(_np.dtype(dtype))
        args.append(nc.dram_tensor(f"out_{i}_dram", shape, dt, kind="ExternalOutput").ap())
    gnn_kernel(nc, *args)
    r = _run(nc, [arrays], core_ids=[0])
    got = tuple(r.results[0][f"out_{i}_dram"] for i in range(len(_OUTS)))
    return got[0]
```

```python
from contextlib import ExitStack

import numpy as np

import concourse.bass as bass
from concourse import mybir

P = 128
N, D, E = 1250, 512, 40000
H = 8
C = D // H
FC = D // P
ED = 64
F1 = 2048
F2 = 1024
NT = (N + P - 1) // P
NP = NT * P
LAST = N - (NT - 1) * P
TPG = 4
GE = TPG * P
NC = (E + GE - 1) // GE + 1
NG = NC - 1 + NT - 1
NG += -NG % 4
T = NG * TPG
UN = 2 * TPG
Q = NG // 2
GA = 4
QA = NG // GA
RW = D + H
EP = NC * GE
NPAD = EP - E
PADP = max(d for d in range(1, P + 1) if NPAD % d == 0)
PAD_DST = 4000
KEY = 4096
CH = P // H
CT = T // CH
CL = CT * P
BIG = 2.0 ** 100
MS = 224
LN_EPS = 1e-5

ALU = mybir.AluOpType
ACT = mybir.ActivationFunctionType
F32 = mybir.dt.float32
FR = mybir.dt.float32r
BF = mybir.dt.bfloat16
I32 = mybir.dt.int32
AX = mybir.AxisListType.X


def need(eng, sem, n):
    if not isinstance(n, int) or n > 0:
        eng.wait_ge(sem, n)


def gnn_kernel(nc, x, src, dst, ea, ln1_g, ln1_b, Wl, Wr, att, gat_bias, ln2_g, ln2_b, W1, b1, W2, b2,
               W_e, b_e, V1, c1, g1, beta1, V2, c2, g2, beta2, eps, out):
    with ExitStack() as ctx:
        def sem(name):
            return ctx.enter_context(nc.semaphore(name))

        def dram(name, shape, dt=F32):
            return nc.dram_tensor(name, shape, dt).ap()

        src_pad, dst_pad = dram("src_pad", [EP], I32), dram("dst_pad", [EP], I32)
        ea_pad = dram("ea_pad", [EP, ED])
        e_scr = dram("e_scr", [2 * H, T * P])
        xl_tab, x2_tab = dram("xl_tab", [NP, RW]), dram("x2_tab", [NP, D])

        def put(region, name, shape, dt=F32):
            size = int(np.prod(shape[1:])) * (2 if dt == BF else 4)
            t = nc.alloc_sbuf_tensor_at(name, shape, dt, offset=region[0])
            region[0] += (size + 31) // 32 * 32
            return t

        base = [17408]
        ident = put(base, "ident", [P, P])
        iota = put(base, "iota", [P, P])
        iota_b, ident_b = put(base, "iota_b", [P, P], BF), put(base, "ident_b", [P, P], BF)
        ident_r = put(base, "ident_r", [P, P], FR)
        iota_i = put(base, "iota_i", [P, P], I32)
        ones = put(base, "ones", [P, P])
        x_sb = put(base, "x_sb", [P, NT, D])
        acc = put(base, "acc", [P, NT, RW])
        runs = nc.alloc_sbuf_tensor_at("runs", [P, CL + 16], F32, offset=base[0] - (NT * RW * 4 + 31) // 32 * 32)
        assert CL + 16 <= NT * RW
        e_all = put(base, "e_all", [P, T * H])
        drel = put(base, "drel", [P, T])
        drel_b = put(base, "drel_b", [P, T], BF)
        src_idx = put(base, "src_idx", [P, T], I32)
        key = put(base, "key", [P, T])
        ng_i = put(base, "ng_i", [1, NG], I32)
        s_i = put(base, "s_i", [1, NG], I32)
        chunk_i = put(base, "chunk_i", [NG, 1], I32)
        idx_stage = put(base, "idx_stage", [P, GA * TPG], I32)
        PAR = (("ln1_g", ln1_g, FC), ("ln1_b", ln1_b, FC), ("att", att.rearrange("h c -> (h c)"), FC),
               ("ln2_g", ln2_g, FC), ("ln2_b", ln2_b, FC), ("b1", b1, F1 // P), ("c1", c1, F2 // P), ("g1", g1, F2 // P),
               ("beta1", beta1, F2 // P), ("c2", c2, FC), ("g2", g2, FC), ("beta2", beta2, FC))
        NPAR = sum(k for _, _, k in PAR)
        NPAR1 = sum(k for _, _, k in PAR[:3])
        par_row = put(base, "par_row", [NPAR1, P])
        par_row2 = put(base, "par_row2", [NPAR - NPAR1, P])
        par = put(base, "par", [P, NPAR])
        par_at, at = {}, 0
        for name, _, k in PAR:
            par_at[name] = (at, at + k)
            at += k
        (ln1gc, ln1bc, attc, ln2gc, ln2bc, b1c, c1c, g1c, be1c, c2c, g2c, be2c) = (
            par[:, lo_:hi_] for lo_, hi_ in par_at.values())
        att_parts = put(base, "att_parts", [P, FC * 2 * H], FR)
        att8 = put(base, "att8", [P, FC])
        epsc = put(base, "epsc", [P, 1])
        att_bc = put(base, "att_bc", [P, D])
        gb_bc, b2_bc, be_bc = (put(base, n, [P, D]) for n in ("gb_bc", "b2_bc", "be_bc"))
        shift_dn, shift_up = put(base, "shift_dn", [P, P]), put(base, "shift_up", [P, P])
        stats = put(base, "stats", [P, NT, 6])
        mv = put(base, "mv", [P, NT, 2])
        rstd = put(base, "rstd", [P, NT])
        bnst = put(base, "bnst", [P, F2 // P, 3, 6])
        bnmv = put(base, "bnmv", [P, F2 // P, 2])
        bnsc, bnsh = put(base, "bnsc", [P, F2 // P]), put(base, "bnsh", [P, F2 // P])
        cols = put(base, "cols", [P, 16])
        hT = put(base, "hT", [P, FC, NP])
        lo = base[0]
        ring = [lo]
        gat = put(ring, "gat", [P, UN, RW])
        zbuf = put(ring, "zbuf", [P, UN, RW])
        gat_a = nc.alloc_sbuf_tensor_at("gat_a", [P, GA * TPG, RW], FR, offset=lo)
        gat_c = nc.alloc_sbuf_tensor_at("gat_c", [P, GA * TPG, RW], F32, offset=lo)
        assert UN * RW * 4 % 32 == 0 and GA * TPG == 2 * UN
        onehot = put(ring, "onehot", [P, 2, TPG, P], FR)
        onehot_b = put(ring, "onehot_b", [P, 2, TPG, P], BF)
        onehotT = put(ring, "onehotT", [P, 2, GE], FR)
        est = put(ring, "est", [2 * H, 2, GE])
        hi = ring[0]
        ra = [hi]
        xr_tab = put(ra, "xr_tab", [P, NT, 2, D], FR)
        xr_hi, xr_lo = xr_tab[:, :, 0, :], xr_tab[:, :, 1, :]
        ra_end = ra[0]
        rz = [ra_end]
        Wlr = put(ra, "Wlr", [P, 2, FC, D])
        zt = put(ra, "zt", [P, 4, D])
        zr_hi = put(rz, "zr_hi", [P, FC, GE], FR)
        zr_lo = put(rz, "zr_lo", [P, FC, GE], FR)
        xr_now = put(rz, "xr_now", [P, 2, 2, D], FR)
        rs = [lo]
        dst_i = put(rs, "dst_i", [P, E // 125], I32)
        dst_f = put(rs, "dst_f", [P, E // 125])
        rl = [rs[0]]
        cmp = put(rs, "cmp", [P, NT, E // 125])
        bounds_i = put(rs, "bounds_i", [P, 16], I32)
        bounds = put(rs, "bounds", [P, 16])
        cnt = put(rs, "cnt", [P, 16])
        iotaK_i, iotaK = put(rs, "iotaK_i", [1, P], I32), put(rs, "iotaK", [1, P])
        rows = put(rs, "rows", [1, 12, 16])
        rk = [rs[0]]
        kcmp = put(rs, "kcmp", [1, NT, NC - 1])
        gcmp = put(rs, "gcmp", [1, NG, NT])
        gprod = put(rs, "gprod", [1, NG, NT])
        permk = put(rk, "permk", [P, CL])
        rs[0] = max(rs[0], rk[0])
        ngf, sf = put(rs, "ngf", [1, NG]), put(rs, "sf", [1, NG])
        ngb = put(rs, "ngb", [P, NG])
        xl_sb = put(rs, "xl_sb", [P, 2, RW])
        prod = put(rs, "prod", [P, D])
        pads_i = put(rs, "pads_i", [4, NPAD // 4], I32)
        padz_i = put(rs, "padz_i", [4, NPAD // 4], I32)
        padz = put(rs, "padz", [PADP, NPAD * ED // PADP])
        lst_i = put(rl, "lst_i", [NG, 2, GE], I32)
        lst_f = put(rl, "lst_f", [NG, 2, GE])
        dcol = put(rl, "dcol", [P, T])
        assert max(rl[0], rs[0]) <= hi, (rl[0], rs[0], hi)
        rb = [hi]
        X, fwd, bwd = (put(rb, n, [P, CL]) for n in ("X", "fwd", "bwd"))
        perm = fwd
        X2 = bwd
        assert rb[0] <= ra_end
        rowbuf = put(rb, "rowbuf", [1, 6, P])
        rw = [hi]
        W1_sb = put(rw, "W1_sb", [P, FC, F1])
        W2_sb = put(rw, "W2_sb", [P, F1 // P, D])
        rh = [lo]
        hid = put(rh, "hid", [P, F1 // P, D])
        lnz = put(rh, "lnz", [P, 2, D])
        vrow = put(rh, "vrow", [P, 4, D])
        assert rh[0] <= hi
        rv = [hi]
        V1_sb = put(rv, "V1_sb", [P, FC, F2])
        rd = [rv[0]]
        uT = put(rv, "uT", [P, F2 // P, NP])
        ea_g = put(rd, "ea_g", [P, 2, TPG * ED])
        ea_hl = put(rd, "ea_hl", [P, 2, TPG, 2 * ED], FR)
        eaT = put(rd, "eaT", [P, 2, GE], FR)
        We2 = put(rd, "We2", [P, D])
        We_hi, We_lo = put(rd, "We_hi", [P, D], FR), put(rd, "We_lo", [P, D], FR)
        assert rd[0] <= hi + FC * F1 * 4
        m_hi, m_lo = put(rd, "m_hi", [P, 4, MS], FR), put(rd, "m_lo", [P, 4, MS], FR)
        rv2 = [lo]
        yT = put(rv2, "yT", [P, FC, NP])
        fin = put([hi], "fin", [P, NT, D])
        V2_sb = put(rv2, "V2_sb", [P, F2 // P, D])
        assert rv2[0] <= hi, (rv2[0], hi)
        end = max(r[0] for r in (ra, rz, rb, rw, rv, rd))
        assert end <= 229344, (lo, hi, end)

        ps = ctx.enter_context(nc.psum_tensor("ps", [P, 8, D], F32))
        psf = ps[:].rearrange("p b n -> p (b n)")
        ps_bf = [ps[:, 6 + h, :].bitcast(BF) for h in range(2)]
        ps_row = [psf[:, 2 * s * D:2 * s * D + RW] for s in range(2)]

        names = """dst_in wqkv_in par_in par2_in bc_in pad_in ea_pad_in cst cstv cnt_ready rp_ready tab_ready ngb_ready chunk_ready
        lists_in lists_f listT lists_ready var_ready root_ready zt_ready ztT hT_ready xl_mm xr_mm xl_cp xr_cp xl_dve xr_dve
        ot_p ot_ready o_ready xr_staged t_done hi_ready lo_ready sc_done e_out slin_ready xg_ready es_hi es_lo
        perm_ready permk_ready kT xk_p k_ready xs_ready colp_p colp rowp rowv carry_p carry_c m_ready ex_ready exT ex_back
        o2_ready msg_ready agg_done acc_done acc_zero w_in z2_ready z2T h2T_ready f1_mm hid_ready f2_mm u_ready
        x2_ready we_in We_ready v2_in ea_hi ea_split ea_p ea_ready tw_done t_ready m2_ready m2_rest o3_ready ag2_done acc2_done v_in hhT_p hhT_ready
        u_mm u_cp bn_scaled sT_ready y_mm y_cp yT_ready yb_p yb_last v_ready v_last fin_ready
        gate dvec par_T par_ready""".split()
        S = {n: sem(n) for n in names}
        gath = {ph: [sem(f"gath_{ph}{i}") for i in range(GA * TPG if ph == "a" else UN)] for ph in "ad"}
        gath["c"] = gath["a"]
        staged = {ph: sem(f"staged_{ph}") for ph in "acd"}
        ea_in = [sem(f"ea_in{i}") for i in range(2)]
        est_stored = [sem(f"est_stored{i}") for i in range(2)]
        xl_stored = [sem(f"xl_stored{i}") for i in range(2)]
        out_stored = [sem(f"out_stored{i}") for i in range(2)]
        x_part = [sem(f"x_part{t}") for t in range(4)]
        x2_stored = [sem(f"x2_stored{t}") for t in range(4)]
        f1_bank = (2, 3, 6, 7)
        early_bank = (0, 1, 2, 3, 6, 7)
        pr_bank = (1, 3, 4, 5)
        block = ctx.enter_context(nc.Block())

        def load_scores(eng, first):
            for part, (o, done) in enumerate(((X, S["es_hi"]), (X2, S["es_lo"]))):
                for j in range(first, H, 2):
                    eng.dma_start(o[j:P:H, :], e_scr[part * H + j, :].rearrange("(j c) -> j c", j=CH)).then_inc(done, 16)

        @block.sync
        def _(sp):
            for j in range(3):
                sp.dma_start(x_sb[:, 3 * j:3 * j + 3, :],
                             x[3 * j * P:(3 * j + 3) * P, :].rearrange("(t p) d -> p t d", p=P)).then_inc(x_part[j], 16)
            sp.wait_ge(S["cst"], 1)
            sp.dma_start(x_sb[0:LAST, NT - 1, :], x[(NT - 1) * P:N, :]).then_inc(x_part[3], 16)
            sp.wait_ge(S["par_in"], 48)
            sp.dma_start(Wlr[:, 0], Wl.rearrange("(c p) n -> p c n", p=P)).then_inc(S["wqkv_in"], 16)
            sp.dma_start(Wlr[:, 1], Wr.rearrange("(c p) n -> p c n", p=P)).then_inc(S["wqkv_in"], 16)
            sp.dma_start(dst_i[0:125, :], dst.rearrange("(p f) -> p f", p=125)).then_inc(S["dst_in"], 16)
            sp.wait_ge(S["wqkv_in"], 32)
            k = 320
            sp.dma_start(ea_pad[0:E, :].rearrange("(a b) c -> a (b c)", a=k),
                         ea.rearrange("(a b) c -> a (b c)", a=k)).then_inc(S["ea_pad_in"], 16)
            for t in range(NT):
                sp.wait_ge(S["xl_cp"], t + 1)
                sp.wait_ge(S["xl_dve"], t + 1)
                sp.dma_start(xl_tab[t * P:(t + 1) * P, :], xl_sb[:, t % 2, :]).then_inc(xl_stored[t % 2], 16)
            def store_scores(q):
                for h in range(2):
                    sp.wait_ge(S["e_out"], 2 * q + h + 1)
                    sp.dma_start(e_scr[:, bass.ds((2 * q + h) * GE, GE)], est[:, h, :]).then_inc(est_stored[h], 16)

            store_scores(0)
            with sp.Fori(1, Q) as q:
                store_scores(q)
            for h in range(2):
                sp.wait_ge(est_stored[h], Q * 16 + 16 * h)
            sp.wait_ge(S["t_done"], T)
            load_scores(sp, 0)
            sp.wait_ge(S["ex_back"], 6)
            for j in range(F1 // P):
                sp.wait_ge(S["msg_ready"], (j + 1) * T // (F1 // P + 2))
                if j % 4 == 0:
                    sp.dma_start(W1_sb[:, j // 4, :], W1[j // 4 * P:(j // 4 + 1) * P, :]).then_inc(S["w_in"], 16)
                sp.dma_start(W2_sb[:, j, :], W2[j * P:(j + 1) * P, :]).then_inc(S["w_in"], 16)
            def store_table(t0, t1):
                for t in range(t0, t1):
                    sp.wait_ge(S["x2_ready"], t + 1)
                    sp.dma_start(x2_tab[t * P:(t + 1) * P, :], vrow[:, t % 4, :]).then_inc(x2_stored[t % 4], 16)

            store_table(0, NT - 2)
            sp.wait_ge(S["f1_mm"], 3 * F1 // P)
            for half in range(2):
                sp.dma_start(We2[half * ED:(half + 1) * ED, :], W_e[:, :]).then_inc(S["we_in"], 16)
            sp.dma_start(V1_sb[:], V1.rearrange("(c p) n -> p c n", p=P)).then_inc(S["v_in"], 16)
            sp.wait_ge(S["ea_pad_in"], 16)
            sp.wait_ge(S["pad_in"], 5 * 16)

            def edge_features(q):
                for h in range(2):
                    need(sp, S["ea_split"], 2 * q + h - 1)
                    s = sp.value_load(s_i[0:1, bass.ds(2 * q + h, 1)], min_val=0, max_val=EP - GE)
                    sp.dma_start(ea_g[:, h, :].rearrange("p (k c) -> p k c", k=TPG),
                                 ea_pad[bass.ds(s, GE), :].rearrange("(k p) c -> p k c", p=P)).then_inc(ea_in[h], 16)

            edge_features(0)
            store_table(NT - 2, NT)
            with sp.Fori(1, Q) as q:
                edge_features(q)
            sp.wait_ge(S["acc2_done"], NG)
            sp.dma_start(V2_sb[:], V2.rearrange("(c p) n -> p c n", p=P)).then_inc(S["v2_in"], 16)
            for t in range(NT):
                r = P if t < NT - 1 else LAST
                sp.wait_ge(S["fin_ready"], t + 1)
                sp.dma_start(out[t * P:t * P + r, :], fin[0:r, t, :]).then_inc(out_stored[t % 2], 16)
            for half in out_stored:
                sp.wait_ge(half, NT // 2 * 16)

        @block.gpsimd
        def _(pool):
            g = nc.gpsimd
            g.memset(x_sb[:, NT - 1, :], 0.0).then_inc(S["cst"], 1)
            g.memset(xr_tab[:, NT - 1, 0, :].bitcast(F32), 0.0).then_inc(S["cst"], 1)
            g.memset(xr_tab[:, NT - 1, 1, :].bitcast(F32), 0.0).then_inc(S["cst"], 1)
            g.memset(pads_i[:], PAD_DST).then_inc(S["cst"], 1)
            g.memset(padz_i[:], 0).then_inc(S["cst"], 1)
            g.memset(padz[:], 0.0).then_inc(S["cst"], 1)
            g.iota(iota_i[:], pattern=[[1, P]], base=0, channel_multiplier=0).then_inc(S["cst"], 1)
            g.iota(bounds_i[:], pattern=[[P, 16]], base=0, channel_multiplier=0).then_inc(S["cst"], 1)
            g.iota(iotaK_i[:], pattern=[[GE, P]], base=0, channel_multiplier=0).then_inc(S["cst"], 1)
            g.memset(ident[:], 1.0).then_inc(S["cst"], 1)
            g.memset(shift_dn[:], 1.0).then_inc(S["cst"], 1)
            g.memset(shift_up[:], 1.0).then_inc(S["cst"], 1)
            pool.wait_ge(S["cst"], 12)
            for m, off in ((ident, 0), (shift_dn, H), (shift_up, -H)):
                g.affine_select(out=m[:], in_=m[:], compare_op=ALU.is_equal, fill=0.0, base=off,
                                pattern=[[-1, P]], channel_multiplier=1).then_inc(S["cst"], 1)
            for t_, a in ((att_bc, att.rearrange("h c -> (h c)")), (gb_bc, gat_bias), (b2_bc, b2), (be_bc, b_e)):
                g.dma_start(t_[:], a.partition_broadcast(P)).then_inc(S["bc_in"], 16)
            g.dma_start(epsc[:], eps.partition_broadcast(P)).then_inc(S["bc_in"], 16)

            def gather(q, ph, table, width, consumed, step):
                for k0 in range(0, UN, step):
                    need(pool, consumed, UN * q + k0 + step - UN)
                    g.tensor_copy(idx_stage[:, k0:k0 + step],
                                  src_idx[:, bass.ds(UN * q + k0, step)]).then_inc(staged[ph], 1)
                    pool.wait_ge(staged[ph], UN // step * q + k0 // step + 1)
                    pool.sem_inc(S["gate"], 1)
                    for k in range(k0, k0 + step):
                        g.indirect_dma_start(
                            out=gat[:, k, 0:width], out_offset=None, in_=table[:, :],
                            in_offset=bass.IndirectOffsetOnAxis(ap=idx_stage[:, k:k + 1], axis=0),
                        ).then_inc(gath[ph][k], 16)

            pool.wait_ge(S["chunk_ready"], 1)
            pool.wait_ge(S["pad_in"], 5 * 16)
            for j, lst in enumerate((dst_pad, src_pad)):
                g.indirect_dma_start(
                    out=lst_i[:, j, :], out_offset=None, in_=lst.rearrange("(c n) -> c n", n=GE),
                    in_offset=bass.IndirectOffsetOnAxis(ap=chunk_i[:, 0:1], axis=0),
                ).then_inc(S["lists_in"], 16)
            pool.wait_ge(S["zt_ready"], NT)
            pool.wait_ge(S["bc_in"], 5 * 16)
            for t in range(NT):
                g.tensor_tensor(x_sb[:, t, :], x_sb[:, t, :], gb_bc[:], ALU.add).then_inc(S["xg_ready"], 1)
            g.tensor_tensor(b2_bc[:], b2_bc[:], gb_bc[:], ALU.subtract).then_inc(S["xg_ready"], 1)
            pool.wait_ge(S["lists_ready"], 2)
            for half in xl_stored:
                pool.wait_ge(half, NT // 2 * 16)
            pool.wait_ge(S["kT"], 6)

            def gather_groups(q):
                for j in range(GA):
                    G, k0 = GA * q + j, j * TPG
                    need(pool, S["t_done"], FC * (G - GA + 1))
                    need(pool, S["slin_ready"], G - GA + 1)
                    g.tensor_copy(idx_stage[:, k0:k0 + TPG],
                                  src_idx[:, bass.ds(TPG * G, TPG)]).then_inc(staged["a"], 1)
                    pool.wait_ge(staged["a"], G + 1)
                    pool.sem_inc(S["gate"], 1)
                    for k in range(k0, k0 + TPG):
                        g.indirect_dma_start(
                            out=gat_a[:, k, :].bitcast(F32), out_offset=None, in_=xl_tab[:, :],
                            in_offset=bass.IndirectOffsetOnAxis(ap=idx_stage[:, k:k + 1], axis=0),
                        ).then_inc(gath["a"][k], 16)

            gather_groups(0)
            with pool.Fori(1, QA) as q:
                gather_groups(q)
            pool.wait_ge(S["t_done"], T)
            pool.wait_ge(S["slin_ready"], NG)
            def gather_again(q):
                for j in range(GA):
                    G, k0 = GA * q + j, j * TPG
                    need(pool, S["agg_done"], TPG * (G - GA + 1))
                    pool.wait_ge(staged["c"], G + 1)
                    pool.sem_inc(S["gate"], 1)
                    for k in range(k0, k0 + TPG):
                        g.indirect_dma_start(
                            out=gat_c[:, k, :], out_offset=None, in_=xl_tab[:, :],
                            in_offset=bass.IndirectOffsetOnAxis(ap=idx_stage[:, k:k + 1], axis=0),
                        ).then_inc(gath["c"][k], 16)

            pool.wait_ge(S["es_hi"], H * 16)
            pool.wait_ge(S["es_lo"], H * 16)
            gather_again(0)
            pool.wait_ge(S["m_ready"], 1)
            g.memset(acc[:], 0.0).then_inc(S["acc_zero"], 1)
            with pool.Fori(1, QA) as q:
                gather_again(q)
            for j in range(4):
                pool.wait_ge(x2_stored[j], len(range(j, NT, 4)) * 16)
            gather(0, "d", x2_tab, D, S["t_ready"], 2)
            with pool.Fori(1, Q) as q:
                gather(q, "d", x2_tab, D, S["t_ready"], 2)

        @block.scalar
        def _(act):
            a = nc.scalar
            for j, (name, v, _) in enumerate(PAR):
                r0, r1 = par_at[name]
                if j < 3:
                    act.dma_start(par_row[r0:r1, :], v.rearrange("(c p) -> c p", p=P)).then_inc(S["par_in"], 16)
                else:
                    act.dma_start(par_row2[r0 - NPAR1:r1 - NPAR1, :],
                                  v.rearrange("(c p) -> c p", p=P)).then_inc(S["par2_in"], 16)
            act.dma_start(src_pad[0:E].rearrange("(p f) -> p f", p=16),
                          src.rearrange("(p f) -> p f", p=16)).then_inc(S["pad_in"], 16)
            act.dma_start(dst_pad[0:E].rearrange("(p f) -> p f", p=16),
                          dst.rearrange("(p f) -> p f", p=16)).then_inc(S["pad_in"], 16)
            act.wait_ge(S["cst"], 9)
            act.dma_start(dst_pad[E:EP].rearrange("(p f) -> p f", p=4), pads_i[:]).then_inc(S["pad_in"], 16)
            act.dma_start(src_pad[E:EP].rearrange("(p f) -> p f", p=4), padz_i[:]).then_inc(S["pad_in"], 16)
            act.dma_start(ea_pad[E:EP, :].rearrange("(p f) c -> p (f c)", p=PADP), padz[:]).then_inc(S["pad_in"], 16)

            roots = [0]

            def root(o):
                roots[0] += 1
                act.wait_ge(S["var_ready"], roots[0])
                a.activation(o, o, ACT.Sqrt).then_inc(S["root_ready"], 1)

            def affine_T(t, bank, mm, gcol, bcol, ready):
                act.wait_ge(mm, t + 1)
                for c in range(FC):
                    i = a.activation(hT[:, c, t * P:(t + 1) * P], ps[:, bank, c * P:(c + 1) * P], ACT.Identity,
                                     bias=bcol[:, c:c + 1], scale=gcol[:, c:c + 1])
                i.then_inc(ready, 1)

            root(rstd[:])
            act.wait_ge(S["par_ready"], 1)
            for t in range(NT + 1):
                if t < NT:
                    affine_T(t, t % 2, S["ztT"], ln1gc, ln1bc, S["hT_ready"])
                if t > 0:
                    u = t - 1
                    act.wait_ge(S["xl_mm"], u + 1)
                    if u >= 2:
                        act.wait_ge(xl_stored[u % 2], 16 * (u // 2))
                    a.copy(xl_sb[:, u % 2, 0:D], ps[:, 2 + u % 2, :]).then_inc(S["xl_cp"], 1)
                    act.wait_ge(S["xr_mm"], u + 1)
                    if u == NT - 1:
                        act.wait_ge(S["cst"], 3)
                    a.copy(xr_hi[:, u, :], ps[:, 4 + u % 2, :]).then_inc(S["xr_cp"], 1)

            for b in range(6):
                w = min(4, CT - 4 * b) * P
                act.wait_ge(S["kT"], b + 1)
                a.mul(runs[:, 1 + b * D:1 + b * D + w], ps[:, b % 2, 0:w], BIG).then_inc(S["k_ready"], 1)

            def transposed_onehot(G, h):
                act.wait_ge(S["ot_p"], G + 1)
                need(act, S["t_done"], FC * (G - 1))
                a.copy(onehotT[:, h, :], ps_bf[h][:, 0:GE]).then_inc(S["ot_ready"], 1)

            def scores_out(G, h):
                act.wait_ge(S["sc_done"], FC * G + FC)
                need(act, est_stored[h], 8 * (G - h) + 16 * h)
                a.copy(est[:, h, :], ps[0:2 * H, 4 + h, :]).then_inc(S["e_out"], 1)

            def rectify(q, first, last):
                for u in range(GA * FC):
                    i, G, c = GA * FC * q + u, GA * q + u // FC, u % FC
                    h = G % 2 if isinstance(G, int) else u // FC % 2
                    if c == 1 and not (last and u // FC == GA - 1):
                        transposed_onehot(G + 1, 1 - h)
                    act.wait_ge(S["t_done"], i + 1)
                    need(act, S["sc_done"], i - 3)
                    a.activation(zr_hi[:, c, :], ps[:, c, :], ACT.Relu).then_inc(S["hi_ready"], 1)
                    if c == 3 and not (first and u < FC):
                        scores_out(G - 1, 1 - h)

            act.sem_inc(est_stored[1], 16)
            transposed_onehot(0, 0)
            rectify(0, True, False)
            with act.Fori(1, QA - 1) as q:
                rectify(q, False, False)
            rectify(QA - 1, False, True)
            scores_out(NG - 1, 1)

            act.wait_ge(S["t_done"], T)
            for h in range(2):
                act.wait_ge(est_stored[h], Q * 16 + 16 * h)
            load_scores(act, 1)
            for b in range(6):
                w = min(4, CT - 4 * b) * P
                act.wait_ge(S["m_ready"], b + 1)
                a.activation(X[:, b * D:b * D + w], X[:, b * D:b * D + w], ACT.Exp).then_inc(S["ex_ready"], 1)

            act.wait_ge(S["par_ready"], 2)
            for t0, t1 in ((0, TPG), (TPG, NT)):
                root(rstd[:, t0:t1])
                for t in range(t0, min(t1, TPG)):
                    affine_T(t, t % 2, S["z2T"], ln2gc, ln2bc, S["h2T_ready"])
            n = 0
            for ch in range(3):
                w = min(D, N - ch * D)
                if ch:
                    act.wait_ge(S["f2_mm"], TPG * ch)
                for f in range(F1 // P):
                    act.wait_ge(S["f1_mm"], n + 1)
                    a.activation(hid[:, f, 0:w], ps[:, f1_bank[n % 4], 0:w], ACT.Gelu,
                                 bias=b1c[:, f:f + 1]).then_inc(S["hid_ready"], 1)
                    if TPG <= n + TPG < NT:
                        affine_T(n + TPG, (n + TPG) % 2, S["z2T"], ln2gc, ln2bc, S["h2T_ready"])
                    n += 1
                    if ch == 2 and f == F1 // P // 2:
                        root(rstd[:, 0:NT - 2])
            def edge_hi(G, h):
                act.wait_ge(ea_in[h], 16 * (G // 2) + 16 if isinstance(G, int) else 8 * (G - h) + 16)
                need(act, S["ea_p"], G - 1)
                a.copy(ea_hl[:, h, :, 0:ED], ea_g[:, h, :].rearrange("p (k c) -> p k c", k=TPG)).then_inc(S["ea_hi"], 1)

            def edge_T(G, h):
                act.wait_ge(S["ea_p"], G + 1)
                need(act, S["tw_done"], TPG * (G - 2) + TPG)
                a.copy(eaT[:, h, :], ps[:, 6, :]).then_inc(S["ea_ready"], 1)

            def messages(q, first, last):
                for u in range(UN):
                    i, G, h = UN * q + u, 2 * q + u // TPG, u // TPG
                    if u % TPG == 0 and not (last and h == 1):
                        edge_T(G + 1, 1 - h)
                    if u % TPG == 0 and not last:
                        edge_hi(G + 2, h)
                    act.wait_ge(S["t_ready"], i + 1)
                    need(act, S["ag2_done"], i - 3)
                    cols_ = slice(MS if u % TPG else 0, D)
                    if u % TPG:
                        a.activation(m_hi[:, u % 4, :], zbuf[:, u % 4, 0:MS], ACT.Relu)
                    a.activation(zbuf[:, 4 + u % 4, cols_], zbuf[:, u % 4, cols_], ACT.Relu).then_inc(S["m2_ready"], 1)

            act.wait_ge(S["we_in"], 32)
            a.copy(We_hi[:], We2[:]).then_inc(S["We_ready"], 1)
            edge_hi(0, 0)
            edge_hi(1, 1)
            for t in range(NT - 2, NT):
                root(rstd[:, t:t + 1])
            edge_T(0, 0)
            messages(0, True, False)
            with act.Fori(1, Q - 1) as q:
                messages(q, False, False)
            messages(Q - 1, False, True)

            for t in range(NT):
                act.wait_ge(S["hhT_p"], t + 1)
                a.copy(hT[:, :, t * P:(t + 1) * P], ps[:, t % 2, :].rearrange("p (c n) -> p c n", c=FC)).then_inc(S["hhT_ready"], 1)
            def silu(t_, f, n, ready):
                act.wait_ge(S["bn_scaled"], n)
                a.activation(t_[:, f, 0:N], t_[:, f, 0:N], ACT.Silu, bias=bnsh[:, f:f + 1],
                             scale=bnsc[:, f:f + 1]).then_inc(ready, 1)

            n = 0
            early = F2 // P - 2
            for f in range(F2 // P):
                for ch in range(3):
                    w = min(D, N - ch * D)
                    act.wait_ge(S["u_mm"], n + 1)
                    a.activation(uT[:, f, ch * D:ch * D + w], ps[:, f1_bank[n % 4], 0:w], ACT.Identity,
                                 bias=c1c[:, f:f + 1]).then_inc(S["u_cp"], 1)
                    n += 1
                    if f == early and ch == 2:
                        root(bnsc[:, 0:early])
                    if f == early + 1:
                        for j in range(2 * ch, 2 * ch + 2):
                            silu(uT, j, 1, S["sT_ready"])
            root(bnsc[:, early:F2 // P])
            for f in range(early, F2 // P):
                silu(uT, f, 2, S["sT_ready"])
            n = 0
            for f in range(FC):
                for ch in range(3):
                    w = min(D, N - ch * D)
                    act.wait_ge(S["y_mm"], n + 1)
                    a.activation(yT[:, f, ch * D:ch * D + w], ps[:, 4 + n % 2, 0:w], ACT.Identity,
                                 bias=c2c[:, f:f + 1]).then_inc(S["y_cp"], 1)
                    n += 1
                    if f == FC - 1 and ch == 0:
                        root(bnsc[:, 0:FC - 1])
                        for j in range(FC - 1):
                            silu(yT, j, 3, S["yT_ready"])
            root(bnsc[:, FC - 1:FC])
            silu(yT, FC - 1, 4, S["yT_ready"])
            for t0 in range(0, NT, NT // 2):
                root(rstd[:, t0:t0 + NT // 2])

        @block.vector
        def _(dve):
            v = nc.vector
            count = [0]

            def link(ins):
                count[0] += 1
                ins.then_inc(S["dvec"], 1)
                dve.wait_ge(S["dvec"], count[0])

            v.memset(ones[:], 1.0).then_inc(S["cstv"], 1)
            dve.wait_ge(S["cst"], 9)
            link(v.tensor_copy(iota[:], iota_i[:]))
            link(v.tensor_copy(bounds[:], bounds_i[:]))
            link(v.tensor_copy(iotaK[:], iotaK_i[:]))
            rp, cn, kn, ginc, gexc, bs, db, zr, first, final = (rows[:, j, 0:NT] for j in range(10))

            def count_edges():
                dve.wait_ge(S["dst_in"], 16)
                link(v.tensor_copy(dst_f[0:125, :], dst_i[0:125, :]))
                link(v.tensor_tensor(cmp[0:125], dst_f[0:125, :].unsqueeze(1).broadcast_to([125, NT, E // 125]),
                                     bounds[0:125, 0:NT].unsqueeze(2).broadcast_to([125, NT, E // 125]), ALU.is_lt))
                v.tensor_reduce(cnt[0:125, 0:NT], cmp[0:125], AX, ALU.add).then_inc(S["cnt_ready"], 1)

            def tables_of_tiles():
                link(v.memset(rows[:], 0.0))
                dve.wait_ge(S["rp_ready"], 1)
                v.tensor_copy(par[:, NPAR1:NPAR], ps[:, 7, P + NPAR1:P + NPAR]).then_inc(S["par_ready"], 1)
                link(v.tensor_copy(rp, ps[0:1, 7, 0:NT]))
                link(v.memset(rows[:, 0, NT:NT + 1], float(E)))
                link(v.tensor_tensor(cn, rows[:, 0, 1:NT + 1], rp, ALU.subtract))
                for edge, op, o in ((rp, ALU.is_ge, first), (rows[:, 0, 1:NT + 1], ALU.is_gt, final)):
                    link(v.tensor_tensor(kcmp[:], edge.unsqueeze(2).broadcast_to([1, NT, NC - 1]),
                                         iotaK[:, 1:NC].unsqueeze(1).broadcast_to([1, NT, NC - 1]), op))
                    link(v.tensor_reduce(o, kcmp[:], AX, ALU.add))
                link(v.tensor_scalar(cn, cn, 0.0, None, ALU.is_gt))
                link(v.scalar_tensor_tensor(kn, first, -1.0, final, ALU.mult, ALU.add))
                link(v.scalar_tensor_tensor(kn, kn, 1.0, cn, ALU.add, ALU.mult))
                link(v.tensor_tensor_scan(ginc, kn, zr, 0.0, ALU.add, ALU.add))
                link(v.tensor_tensor(gexc, ginc, kn, ALU.subtract))
                link(v.scalar_tensor_tensor(bs, gexc, -1.0, first, ALU.mult, ALU.add))
                link(v.tensor_copy(rows[:, 6, 0:1], rows[:, 5, 0:1]))
                link(v.tensor_tensor(rows[:, 6, 1:NT], rows[:, 5, 1:NT], rows[:, 5, 0:NT - 1], ALU.subtract))

            def tables_of_groups():
                link(v.tensor_tensor(gcmp[:], iota[0:1, 0:NG].unsqueeze(2).broadcast_to([1, NG, NT]),
                                     gexc.unsqueeze(1).broadcast_to([1, NG, NT]), ALU.is_ge))
                link(v.tensor_tensor(gprod[:], gcmp[:], db.unsqueeze(1).broadcast_to([1, NG, NT]), ALU.mult))
                link(v.tensor_reduce(ngf[:], gcmp[:], AX, ALU.add))
                link(v.tensor_scalar(ngf[:], ngf[:], -1.0, None, ALU.add))
                link(v.tensor_reduce(sf[:], gprod[:], AX, ALU.add))
                link(v.tensor_tensor(sf[:], sf[:], iota[0:1, 0:NG], ALU.add))
                link(v.tensor_scalar(sf[:], sf[:], float(NC - 1), None, ALU.min))
                v.tensor_copy(ng_i[:], ngf[:])
                v.tensor_scalar(s_i[:], sf[:], float(GE), None, ALU.mult).then_inc(S["tab_ready"], 1)

            def group_columns():
                dve.wait_ge(S["ngb_ready"], 1)
                v.tensor_copy(chunk_i[:], ps[0:NG, 6, NG:NG + 1]).then_inc(S["chunk_ready"], 1)
                link(v.tensor_copy(ngb[:], ps[:, 6, 0:NG]))

            def lists_in():
                dve.wait_ge(S["lists_in"], 32)
                for j in range(2):
                    v.tensor_copy(lst_f[:, j, :], lst_i[:, j, :]).then_inc(S["lists_f"], 1)

            def lists_by_tile():
                dve.wait_ge(S["listT"], 2)

                def by_tile(t_):
                    return t_[:].rearrange("p (g k) -> p g k", k=TPG)

                def from_lists(bank):
                    return ps[:, bank, 0:TPG * NG].rearrange("p (k g) -> p g k", k=TPG)

                ngb_t = ngb[:].unsqueeze(2).broadcast_to([P, NG, TPG])
                v.tensor_copy(by_tile(src_idx), from_lists(7)).then_inc(S["lists_ready"], 1)
                link(v.tensor_copy(by_tile(dcol), from_lists(6)))
                link(v.scalar_tensor_tensor(by_tile(drel), ngb_t, -float(P), by_tile(dcol), ALU.mult, ALU.add))
                link(v.tensor_copy(drel_b[:], drel[:]))
                link(v.scalar_tensor_tensor(by_tile(key), ngb_t, float(KEY), by_tile(dcol), ALU.mult, ALU.add))
                link(v.tensor_scalar(key[:], key[:], 1.0, None, ALU.add))
                v.memset(cols[:], 0.0).then_inc(S["lists_ready"], 1)
                for b in range(CT):
                    i = v.tensor_copy(permk[:, b * P:(b + 1) * P].rearrange("p (j h) -> p j h", j=CH),
                                      key[:].rearrange("p (j b) -> p b j", b=CT)[:, b, :].unsqueeze(2).broadcast_to([P, CH, H]))
                i.then_inc(S["permk_ready"], 1)


            def score_vectors():
                dve.wait_ge(S["cst"], 15)
                v.tensor_copy(iota_b[:], iota[:])
                v.tensor_copy(ident_r[:], ident[:])
                link(v.tensor_copy(ident_b[:], ident[:]))
                dve.wait_ge(S["par_ready"], 1)
                link(v.memset(att_parts[:].bitcast(F32), 0.0))
                link(v.tensor_scalar(att8[:], attc, 0.8, None, ALU.mult))
                for i in range(2):
                    r, d = slice(i * C, (i + 1) * C), 2 * H + 2
                    link(v.tensor_copy(att_parts[r, i::d][:, 0:FC], att8[r, :]))
                    v.tensor_tensor(att_parts[r, H + i::d], att8[r, :], att_parts[r, i::d][:, 0:FC].bitcast(F32),
                                    ALU.subtract).then_inc(S["cstv"], 1)
                dve.wait_ge(S["bc_in"], 5 * 16)
                link(v.tensor_scalar(att_bc[:], att_bc[:], 0.2, None, ALU.mult))


            roots = [0]

            def inverse_roots(o, var, eps):
                roots[0] += 1
                v.tensor_scalar(o, var, eps, None, ALU.add).then_inc(S["var_ready"], 1)
                dve.wait_ge(S["root_ready"], roots[0])
                link(v.reciprocal(o, o))

            def ln_stats(src, t0, t1, wait=None):
                for t in range(t0, t1):
                    if wait:
                        wait(t)
                    i = v.bn_stats(stats[:, t, :], src(t))
                link(i)
                for t in range(t0, t1):
                    i = v.bn_aggr(mv[:, t, :], stats[:, t, :])
                link(i)
                inverse_roots(rstd[:, t0:t1], mv[:, t0:t1, 1], LN_EPS)

            def ln_rows(o, i, t):
                return v.tensor_scalar(o, i, mv[:, t, 0:1], rstd[:, t:t + 1], ALU.subtract, ALU.mult)

            ln_stats(lambda t: x_sb[:, t, :], 0, NT, lambda t: dve.wait_ge(x_part[t // 3], 16))
            dve.wait_ge(S["par_T"], 1)
            v.tensor_copy(par[:, 0:NPAR1], ps[:, 7, P:P + NPAR1]).then_inc(S["par_ready"], 1)
            def z_rows(t):
                if t >= 4:
                    dve.wait_ge(S["ztT"], t - 3)
                ln_rows(zt[:, t % 4, :], x_sb[:, t, :], t).then_inc(S["zt_ready"], 1)

            z_rows(0)
            z_rows(1)
            for t in range(NT + 2):
                if t + 2 < NT:
                    z_rows(t + 2)
                if t == 1:
                    score_vectors()
                    count_edges()
                if t >= 2:
                    u = t - 2
                    dve.wait_ge(S["xl_cp"], u + 1)
                    if u:
                        dve.wait_ge(S["xl_dve"], u)
                    link(v.tensor_tensor(prod[:], xl_sb[:, u % 2, 0:D], att_bc[:], ALU.mult))
                    v.tensor_reduce(xl_sb[:, u % 2, D:RW], prod[:].rearrange("p (h c) -> p h c", h=H), AX,
                                    ALU.add).then_inc(S["xl_dve"], 1)
                    dve.wait_ge(S["xr_cp"], u + 1)
                    if u == NT - 1:
                        dve.wait_ge(S["cst"], 3)
                    v.tensor_tensor(xr_lo[:, u, :], ps[:, 4 + u % 2, :], xr_hi[:, u, :].bitcast(F32),
                                    ALU.subtract).then_inc(S["xr_dve"], 1)
                for at_, step in ((3, tables_of_tiles), (4, tables_of_groups), (6, group_columns), (8, lists_in),
                                  (9, lists_by_tile)):
                    if t == at_:
                        step()
            def build_onehot(G, h, ready, to):
                ramp, d = (iota_b, drel_b) if to is onehot_b else (iota, drel)
                v.tensor_tensor(to[:, h], ramp[:].unsqueeze(1).broadcast_to([P, TPG, P]),
                                d[:, bass.ds(TPG * G, TPG)].unsqueeze(2).broadcast_to([P, TPG, P]),
                                ALU.is_equal).then_inc(ready, 1)

            def stage_rows(G, h):
                n = dve.value_load(ng_i[0:1, bass.ds(G, 1)], min_val=0, max_val=NT - 1)
                need(dve, S["t_done"], FC * (G - 1))
                v.tensor_copy(xr_now[:, h].unsqueeze(1), xr_tab[:, bass.ds(n, 1)]).then_inc(S["xr_staged"], 1)

            def split_rows(q, first, last):
                for u in range(GA * FC):
                    i, G, c = GA * FC * q + u, GA * q + u // FC, u % FC
                    h = u // FC % 2
                    dve.wait_ge(S["hi_ready"], i + 1)
                    v.scalar_tensor_tensor(zr_lo[:, c, :], ps[:, c, :], 0.0, zr_hi[:, c, :].bitcast(F32), ALU.max,
                                           ALU.subtract).then_inc(S["lo_ready"], 1)
                    if c == 0:
                        k0 = u // FC * TPG
                        for k in range(k0, k0 + TPG):
                            dve.wait_ge(gath["a"][k], 16 * q + 16)
                        v.tensor_copy(e_all[:, bass.ds(G * TPG * H, TPG * H)].rearrange("p (k h) -> p k h", k=TPG),
                                      gat_a[:, k0:k0 + TPG, D:RW].bitcast(F32)).then_inc(S["slin_ready"], 1)
                    if last and u // FC >= GA - 2:
                        continue
                    if c == 1:
                        dve.wait_ge(S["ot_p"], G + 1)
                        build_onehot(G + 2, h, S["o_ready"], onehot_b)
                    if c == 3:
                        stage_rows(G + 2, h)

            dve.wait_ge(S["kT"], 6)
            dve.wait_ge(S["xr_dve"], NT)
            for G in range(2):
                build_onehot(G, G, S["o_ready"], onehot_b)
                stage_rows(G, G)
            split_rows(0, True, False)
            with dve.Fori(1, QA - 1) as q:
                split_rows(q, False, False)
            split_rows(QA - 1, False, True)

            dve.wait_ge(S["slin_ready"], NG)
            dve.wait_ge(S["t_done"], T)
            v.tensor_copy(perm[:].rearrange("p (b j h) -> p b j h", b=CT, j=CH),
                          e_all[:].rearrange("p (j b h) -> p b j h", j=CH, b=CT)).then_inc(S["perm_ready"], 1)
            def stage_indices(G, slot):
                v.tensor_copy(idx_stage[:, slot * TPG:(slot + 1) * TPG],
                              src_idx[:, bass.ds(TPG * G, TPG)]).then_inc(staged["c"], 1)

            for G in range(GA):
                stage_indices(G, G)
            build_onehot(0, 0, S["o2_ready"], onehot)
            dve.wait_ge(S["k_ready"], 6)
            link(v.tensor_copy(cols[:, 0:1], runs[:, 1:2]))
            link(v.tensor_copy(cols[:, 1:2], runs[:, CL:CL + 1]))
            link(v.tensor_tensor(cols[:, 2:3], cols[:, 0:1], cols[:, 1:2], ALU.is_equal))
            link(v.tensor_tensor(runs[:, 1:CL], runs[:, 1:CL], runs[:, 2:CL + 1], ALU.subtract))
            link(v.memset(runs[:, 0:1], 0.0))
            link(v.memset(runs[:, CL:CL + 1], 0.0))
            v.memset(rowbuf[:], 0.0).then_inc(S["colp"], 1)
            dve.wait_ge(S["es_hi"], H * 16)
            for b in range(6):
                w = min(4, CT - 4 * b) * P
                dve.wait_ge(S["xk_p"], b + 1)
                v.tensor_tensor(X[:, b * D:b * D + w], X[:, b * D:b * D + w], ps[:, b, 0:w],
                                ALU.add).then_inc(S["xs_ready"], 1)
            dve.wait_ge(S["xs_ready"], 6)
            dve.wait_ge(S["es_lo"], H * 16)
            link(v.tensor_tensor(X[:], X[:], X2[:], ALU.add))
            for way in range(2):
                o = fwd if way == 0 else bwd
                step = 1 if way == 0 else -1
                data = X if way == 0 else fwd
                p_ = runs[:, 0:CL] if way == 0 else runs[:, 1:CL + 1]

                def scan(initial):
                    return v.tensor_tensor_scan(o[:, ::step], p_[:, ::step], data[:, ::step], initial, ALU.add, ALU.max)

                link(scan(-BIG))
                endcol = CL - 1 if way == 0 else 0
                k0 = 3 + 6 * way
                link(v.tensor_copy(cols[:, k0:k0 + 1], o[:, endcol:endcol + 1]))
                dve.wait_ge(S["colp_p"], way + 1)
                link(v.tensor_tensor(cols[:, k0 + 1:k0 + 2], ps[:, 0, 2 * way:2 * way + 1], cols[:, way:way + 1], ALU.is_equal))
                link(v.tensor_tensor(cols[:, k0 + 2:k0 + 3], cols[:, k0 + 1:k0 + 2], cols[:, 2:3], ALU.mult))
                link(v.tensor_scalar(cols[:, k0 + 1:k0 + 3], cols[:, k0 + 1:k0 + 3], -1.0, BIG, ALU.add, ALU.mult))
                v.memset(cols[:, k0 + 3:k0 + 4], 0.0).then_inc(S["colp"], 1)
                dve.wait_ge(S["rowp"], way + 1)
                for j in range(2):
                    link(v.tensor_copy(rowbuf[:, j, :].rearrange("p (h j) -> p h j", h=H),
                                       ps[0:1, 1, j * P:(j + 1) * P].rearrange("p (j h) -> p h j", h=H)))
                link(v.tensor_tensor_scan(rowbuf[:, 2, ::step], rowbuf[:, 1, ::step], rowbuf[:, 0, ::step], -BIG,
                                          ALU.add, ALU.max))
                v.tensor_copy(rowbuf[:, 3, :].rearrange("p (j h) -> p j h", h=H),
                              rowbuf[:, 2, :].rearrange("p (h j) -> p j h", h=H)).then_inc(S["rowv"], 1)
                dve.wait_ge(S["carry_p"], 2 * way + 1)
                v.tensor_copy(cols[:, k0 + 4:k0 + 5], ps[:, 2, 0:1]).then_inc(S["carry_c"], 1)
                dve.wait_ge(S["carry_p"], 2 * way + 2)
                link(v.tensor_tensor(cols[:, k0 + 5:k0 + 6], ps[:, 2, 2:3], cols[:, k0 + 1:k0 + 2], ALU.add))
                link(scan(cols[:, k0 + 5:k0 + 6]))
            for b in range(6):
                w = slice(b * D, min(b * D + D, CL))
                v.tensor_tensor(X[:, w], X[:, w], bwd[:, w], ALU.subtract).then_inc(S["m_ready"], 1)
            for b in range(6):
                n = min(4, CT - 4 * b)
                dve.wait_ge(S["exT"], b + 1)
                v.tensor_copy(e_all[:].rearrange("p (j b h) -> p b j h", j=CH, b=CT)[:, 4 * b:4 * b + n],
                              ps[:, b % 4, 0:n * P].rearrange("p (b j h) -> p b j h", b=n, j=CH)).then_inc(S["ex_back"], 1)

            def add_sums(G, h, src_ps, width, done, agg):
                n = dve.value_load(ng_i[0:1, bass.ds(G, 1)], min_val=0, max_val=NT - 1)
                dve.wait_ge(agg, TPG * G + TPG)
                need(dve, done, G)
                v.tensor_tensor(acc[:, bass.ds(n, 1), 0:width], acc[:, bass.ds(n, 1), 0:width],
                                src_ps.unsqueeze(1), ALU.add).then_inc(done, 1)

            def weigh_rows(q, first, last):
                for u in range(GA * TPG):
                    i, G, j = GA * TPG * q + u, GA * q + u // TPG, u // TPG
                    h = j % 2
                    dve.wait_ge(gath["c"][u], 16 * q + 16 * QA + 16)
                    v.tensor_tensor(gat_c[:, u, 0:D].rearrange("p (h c) -> p h c", h=H),
                                    gat_c[:, u, 0:D].rearrange("p (h c) -> p h c", h=H),
                                    e_all[:, bass.ds(i * H, H)].unsqueeze(2).broadcast_to([P, H, C]),
                                    ALU.mult).then_inc(S["msg_ready"], 1)
                    if u % TPG == 1 and not (first and j == 0):
                        add_sums(G - 1, 1 - h, ps_row[1 - h], RW, S["acc_done"], S["agg_done"])
                    if u % TPG == 2 and not (last and j == GA - 1):
                        need(dve, S["agg_done"], TPG * G)
                        build_onehot(G + 1, 1 - h, S["o2_ready"], onehot)
                    if u % TPG == 3 and not (first and j == 0) and not (last and j > 0):
                        stage_indices(G + GA - 1, (j - 1) % GA)

            dve.wait_ge(S["acc_zero"], 1)
            dve.wait_ge(S["ex_back"], 6)
            weigh_rows(0, True, False)
            with dve.Fori(1, QA - 1) as q:
                weigh_rows(q, False, False)
            weigh_rows(QA - 1, False, True)
            add_sums(NG - 1, 1, ps_row[1], RW, S["acc_done"], S["agg_done"])

            dve.wait_ge(S["acc_done"], NG)
            den = acc[:, :, D:RW]
            link(v.tensor_scalar(den, den, 1e-16, None, ALU.add))
            link(v.reciprocal(den, den))

            def attention_rows(t0, t1):
                for t in range(t0, t1):
                    i = v.tensor_tensor(acc[:, t, 0:D].rearrange("p (h c) -> p h c", h=H),
                                        acc[:, t, 0:D].rearrange("p (h c) -> p h c", h=H),
                                        acc[:, t, D:RW].unsqueeze(2).broadcast_to([P, H, C]), ALU.mult)
                link(i)
                dve.wait_ge(S["xg_ready"], NT + 1)
                for t in range(t0, t1):
                    i = v.tensor_tensor(acc[:, t, 0:D], acc[:, t, 0:D], x_sb[:, t, :], ALU.add)
                link(i)
                ln_stats(lambda t: acc[:, t, 0:D], t0, t1)
                for t in range(t0, t1):
                    if t >= 2:
                        dve.wait_ge(S["z2T"], t - 1)
                    ln_rows(lnz[:, t % 2, :], acc[:, t, 0:D], t).then_inc(S["z2_ready"], 1)

            attention_rows(0, TPG)
            attention_rows(TPG, NT)
            link(v.tensor_tensor(x_sb[:], x_sb[:], acc[:, :, 0:D], ALU.add))
            for t in range(NT):
                i = v.tensor_tensor(x_sb[:, t, :], x_sb[:, t, :], b2_bc[:], ALU.add)
            link(i)
            link(v.tensor_scalar(cols[:, 15:16], epsc[:], 1.0, None, ALU.add))

            def layer1_rows(t0, t1):
                for t in range(t0, t1):
                    dve.wait_ge(S["f2_mm"], t + 1)
                    r = min(P, N - t * P)
                    v.tensor_tensor(x_sb[0:r, t, :], x_sb[0:r, t, :], ps[0:r, 4 + t % 2, :], ALU.add).then_inc(S["u_ready"], 1)
                dve.wait_ge(S["u_ready"], t1)
                ln_stats(lambda t: x_sb[:, t, :], t0, t1)
                for t in range(t0, t1):
                    i = ln_rows(x_sb[:, t, :], x_sb[:, t, :], t)
                link(i)
                for t in range(t0, t1):
                    if t >= 4:
                        dve.wait_ge(x2_stored[t % 4], 16 * (t // 4))
                    v.tensor_tensor(vrow[:, t % 4, :], x_sb[:, t, :], be_bc[:], ALU.add).then_inc(S["x2_ready"], 1)
                link(v.tensor_scalar(acc[:, t0:t1, 0:D], x_sb[:, t0:t1, :], cols[:, 15:16], None, ALU.mult))

            layer1_rows(0, NT - 2)
            def edge_rest(G, h):
                dve.wait_ge(S["ea_hi"], G + 1)
                v.tensor_tensor(ea_hl[:, h, :, ED:2 * ED], ea_g[:, h, :].rearrange("p (k c) -> p k c", k=TPG),
                                ea_hl[:, h, :, 0:ED].bitcast(F32), ALU.subtract).then_inc(S["ea_split"], 1)

            def message_rest(i, u):
                dve.wait_ge(S["m2_ready"], i + 1)
                v.scalar_tensor_tensor(m_lo[:, u % 4, :], zbuf[:, u % 4, 0:MS], 0.0, m_hi[:, u % 4, :].bitcast(F32),
                                       ALU.max, ALU.subtract).then_inc(S["m2_rest"], 1)

            def edge_sum(q, first, last):
                for u in range(UN):
                    i, G, h = UN * q + u, 2 * q + u // TPG, u // TPG
                    dve.wait_ge(gath["d"][u], 16 * q + 16)
                    dve.wait_ge(S["tw_done"], i + 1)
                    if u % TPG:
                        need(dve, S["m2_rest"], (TPG - 1) * G + u % TPG - TPG + 1)
                    else:
                        need(dve, S["m2_ready"], i - 3)
                    v.tensor_tensor(zbuf[:, u % 4, 0:D], gat[:, u, 0:D], ps[:, pr_bank[u % 4], :], ALU.add).then_inc(S["t_ready"], 1)
                    if (u - 2) % TPG and not (first and u < 2):
                        message_rest(i - 2, (u - 2) % UN)
                    if u % TPG == 0 and not last:
                        edge_rest(G + 2, h)
                    if u % TPG == 3 and not (first and h == 0):
                        add_sums(G - 1, 1 - h, ps[:, 2 * (1 - h), :], D, S["acc2_done"], S["ag2_done"])
                    if u % TPG == 3 and not (last and h == 1):
                        need(dve, S["ag2_done"], TPG * G)
                        build_onehot(G + 1, 1 - h, S["o3_ready"], onehot)

            dve.wait_ge(S["We_ready"], 1)
            v.tensor_tensor(We_lo[:], We2[:], We_hi[:].bitcast(F32), ALU.subtract).then_inc(S["We_ready"], 1)
            edge_rest(0, 0)
            edge_rest(1, 1)
            for t in range(NT - 2, NT):
                layer1_rows(t, t + 1)
            for j in range(4):
                dve.wait_ge(x2_stored[j], len(range(j, NT, 4)) * 16)
            build_onehot(0, 0, S["o3_ready"], onehot)
            edge_sum(0, True, False)
            with dve.Fori(1, Q - 1) as q:
                edge_sum(q, False, False)
            edge_sum(Q - 1, False, True)
            message_rest(T - 2, UN - 2)
            message_rest(T - 1, UN - 1)
            add_sums(NG - 1, 1, ps[:, 2, :], D, S["acc2_done"], S["ag2_done"])

            def bn(data, f0, f1, cp, g_, be_):
                fs = slice(f0, f1)
                for f in range(f0, f1):
                    dve.wait_ge(cp, 3 * f + 3)
                    for ch in range(3):
                        w = min(D, N - ch * D)
                        i = v.bn_stats(bnst[:, f, ch, :], data[:, f, ch * D:ch * D + w])
                link(i)
                for f in range(f0, f1):
                    i = v.bn_aggr(bnmv[:, f, :], bnst[:, f, :, :].rearrange("p a b -> p (a b)"))
                link(i)
                inverse_roots(bnsc[:, fs], bnmv[:, fs, 1], 1e-5)
                link(v.tensor_tensor(bnsc[:, fs], bnsc[:, fs], g_[:, fs], ALU.mult))
                link(v.tensor_tensor(bnsh[:, fs], bnmv[:, fs, 0], bnsc[:, fs], ALU.mult))
                v.tensor_tensor(bnsh[:, fs], be_[:, fs], bnsh[:, fs], ALU.subtract).then_inc(S["bn_scaled"], 1)

            bn(uT, 0, F2 // P - 2, S["u_cp"], g1c, be1c)
            bn(uT, F2 // P - 2, F2 // P, S["u_cp"], g1c, be1c)
            dve.wait_ge(S["sT_ready"], F2 // P)
            bn(yT, 0, FC - 1, S["y_cp"], g2c, be2c)
            def add_result():
                for t in range(NT):
                    dve.wait_ge(S["yb_p"], t + 1)
                    r = min(P, N - t * P)
                    v.tensor_tensor(acc[0:r, t, 0:D - P], x_sb[0:r, t, 0:D - P], ps[0:r, early_bank[t % 6], 0:D - P],
                                    ALU.add).then_inc(S["v_ready"], 1)

            bn(yT, FC - 1, FC, S["y_cp"], g2c, be2c)
            add_result()
            for t0 in range(0, NT, NT // 2):
                for t in range(t0, t0 + NT // 2):
                    r = min(P, N - t * P)
                    dve.wait_ge(S["yb_last"], t + 1)
                    v.tensor_tensor(acc[0:r, t, D - P:D], x_sb[0:r, t, D - P:D], ps[0:r, 4 + t % 2, t // 2 % 4 * P:t // 2 % 4 * P + P],
                                    ALU.add).then_inc(S["v_last"], 1)
                dve.wait_ge(S["v_last"], t0 + NT // 2)
                ln_stats(lambda t: acc[:, t, 0:D], t0, t0 + NT // 2)
                for t in range(t0, t0 + NT // 2):
                    ln_rows(fin[:, t, :], acc[:, t, 0:D], t).then_inc(S["fin_ready"], 1)

        @block.tensor
        def _(pe):
            tm = nc.tensor
            pe.wait_ge(S["cst"], 15)
            pe.wait_ge(S["par_in"], 16 * 3)
            tm.transpose(ps[:, 7, P:P + NPAR1], par_row[:], ident[0:NPAR1, 0:NPAR1]).then_inc(S["par_T"], 1)

            def edge_counts():
                pe.wait_ge(S["par2_in"], 16 * (len(PAR) - 3))
                pe.wait_ge(S["par_ready"], 1)
                tm.transpose(ps[:, 7, P + NPAR1:P + NPAR], par_row2[:], ident[0:NPAR - NPAR1, 0:NPAR - NPAR1])
                pe.wait_ge(S["cnt_ready"], 1)
                pe.wait_ge(S["cstv"], 1)
                tm.matmul(ps[0:1, 7, 0:NT], ones[0:125, 0:1], cnt[0:125, 0:NT], start=True, stop=True).then_inc(S["rp_ready"], 1)

            def group_columns():
                pe.wait_ge(S["tab_ready"], 1)
                tm.matmul(ps[:, 6, 0:NG], ones[0:1, :], ngf[:], start=True, stop=True)
                tm.matmul(ps[0:NG, 6, NG:NG + 1], sf[:], ones[0:1, 0:1], start=True, stop=True).then_inc(S["ngb_ready"], 1)

            def group_lists():
                for j in range(2):
                    pe.wait_ge(S["lists_f"], j + 1)
                    for k in range(TPG):
                        m = tm.transpose(ps[:, 6 + j, k * NG:(k + 1) * NG], lst_f[:, j, k * P:(k + 1) * P], ident[0:NG, 0:NG])
                    m.then_inc(S["listT"], 1)

            def transpose_rows(o, i):
                for c in range(FC):
                    m = tm.transpose(o[:, c * P:(c + 1) * P], i[:, c * P:(c + 1) * P], ident[:])
                return m

            for t in range(NT + 1):
                for at_, step in ((3, edge_counts), (6, group_columns), (9, group_lists)):
                    if t == at_:
                        step()
                if t < NT:
                    pe.wait_ge(S["zt_ready"], t + 1)
                    if t >= 2:
                        pe.wait_ge(S["hT_ready"], t - 1)
                    transpose_rows(ps[:, t % 2, :], zt[:, t % 4, :]).then_inc(S["ztT"], 1)
                if t > 0:
                    u = t - 1
                    pe.wait_ge(S["hT_ready"], u + 1)
                    if u == 0:
                        pe.wait_ge(S["wqkv_in"], 32)
                    for w, bank, done in ((0, 2, S["xl_mm"]), (1, 4, S["xr_mm"])):
                        if u >= 2:
                            pe.wait_ge(S["xl_cp" if w == 0 else "xr_dve"], u - 1)
                        for c in range(FC):
                            m = tm.matmul(ps[:, bank + u % 2, :], hT[:, c, u * P:(u + 1) * P], Wlr[:, w, c, :],
                                          start=(c == 0), stop=(c == FC - 1))
                        m.then_inc(done, 1)
            pe.wait_ge(S["permk_ready"], 1)
            for b in range(6):
                if b < 2:
                    pe.wait_ge(S["hT_ready"], NT)
                else:
                    pe.wait_ge(S["k_ready"], b - 1)
                for k in range(min(4, CT - 4 * b)):
                    m = tm.transpose(ps[:, b % 2, k * P:(k + 1) * P], permk[:, (4 * b + k) * P:(4 * b + k + 1) * P], ident[:])
                m.then_inc(S["kT"], 1)
            pe.wait_ge(S["k_ready"], 6)

            def onehot_T(G, h):
                pe.wait_ge(S["o_ready"], G + 1)
                need(pe, S["ot_ready"], G - 1)
                for k in range(TPG):
                    m = tm.transpose(ps_bf[h][:, k * P:(k + 1) * P], onehot_b[:, h, k, :], ident_b[:])
                m.then_inc(S["ot_p"], 1)

            def source_rows(i, q, u):
                c, k0 = u % FC, u // FC * TPG
                need(pe, S["lo_ready"], i - 3)
                for k in range(TPG):
                    if c == 0:
                        pe.wait_ge(gath["a"][k0 + k], 16 * q + 16)
                    tm.matmul(ps[:, c, k * P:(k + 1) * P].bitcast(FR), gat_a[:, k0 + k, c * P:(c + 1) * P], ident_r[:],
                              start=(k == 0), stop=False, is_transpose=True)

            def destination_rows(u, G, h):
                c = u % FC
                if c == 0:
                    pe.wait_ge(S["ot_ready"], G + 1)
                    pe.wait_ge(S["xr_staged"], G + 1)
                for part in range(2):
                    m = tm.matmul(ps[:, c, :], xr_now[:, h, part, c * P:(c + 1) * P], onehotT[:, h, :], start=False, stop=(part == 1))
                m.then_inc(S["t_done"], 1)

            def scores(i, G, h, c):
                pe.wait_ge(S["lo_ready"], i + 1)
                if c == 0:
                    need(pe, S["e_out"], G - 1)
                w, o = slice(c * 2 * H, (c + 1) * 2 * H), ps[0:2 * H, 4 + h, :]
                tm.matmul(o, att_parts[:, w], zr_hi[:, c, :], start=(c == 0), stop=False)
                tm.matmul(o, att_parts[:, w], zr_lo[:, c, :], start=False, stop=(c == FC - 1)).then_inc(S["sc_done"], 1)

            def phase_a(q, first, last):
                for u in range(GA * FC):
                    i, j = GA * FC * q + u, u // FC
                    source_rows(i, q, u)
                    if not (first and u < 3):
                        scores(i - 3, GA * q + (u - 3) // FC, (u - 3) // FC % 2, (u - 3) % FC)
                    destination_rows(u, GA * q + j, j % 2)
                    if u % FC == 0 and not (last and j == GA - 1):
                        onehot_T(GA * q + j + 1, 1 - j % 2)

            pe.wait_ge(S["lists_ready"], 2)
            pe.wait_ge(S["xr_dve"], NT)
            pe.wait_ge(S["xr_cp"], NT)
            pe.wait_ge(S["xl_dve"], NT)
            pe.wait_ge(S["cstv"], 3)
            onehot_T(0, 0)
            phase_a(0, True, False)
            with pe.Fori(1, QA - 1) as q:
                phase_a(q, False, False)
            phase_a(QA - 1, False, True)
            for c in range(1, FC):
                scores(T - FC + c, NG - 1, 1, c)

            pe.wait_ge(S["e_out"], NG)
            pe.wait_ge(S["perm_ready"], 1)
            for b in range(6):
                for k in range(min(4, CT - 4 * b)):
                    m = tm.transpose(ps[:, b, k * P:(k + 1) * P], perm[:, (4 * b + k) * P:(4 * b + k + 1) * P], ident[:])
                m.then_inc(S["xk_p"], 1)
            pe.wait_ge(S["xs_ready"], 6)
            for way in range(2):
                shift = shift_dn if way == 0 else shift_up
                k0 = 3 + 6 * way
                pe.wait_ge(S["colp"], 1 + way)
                tm.matmul(ps[:, 0, 2 * way:2 * way + 1], shift[:], cols[:, 1 - way:2 - way], start=True, stop=True).then_inc(S["colp_p"], 1)
                pe.wait_ge(S["colp"], 2 + way)
                tm.matmul(ps[0:1, 1, 0:P], cols[:, k0:k0 + 1], ident[:], start=True, stop=True)
                tm.matmul(ps[0:1, 1, P:2 * P], cols[:, k0 + 2:k0 + 3], ident[:], start=True, stop=True).then_inc(S["rowp"], 1)
                pe.wait_ge(S["rowv"], way + 1)
                tm.matmul(ps[:, 2, 0:1], rowbuf[:, 3, :], ones[0:1, 0:1], start=True, stop=True).then_inc(S["carry_p"], 1)
                pe.wait_ge(S["carry_c"], way + 1)
                tm.matmul(ps[:, 2, 2:3], shift[:], cols[:, k0 + 4:k0 + 5], start=True, stop=True).then_inc(S["carry_p"], 1)
            for b in range(6):
                pe.wait_ge(S["ex_ready"], b + 1)
                if b >= 4:
                    pe.wait_ge(S["ex_back"], b - 3)
                for k in range(min(4, CT - 4 * b)):
                    m = tm.transpose(ps[:, b % 4, k * P:(k + 1) * P], X[:, (4 * b + k) * P:(4 * b + k + 1) * P], ident[:])
                m.then_inc(S["exT"], 1)

            def sum_by_dst(q):
                for u in range(GA * TPG):
                    i, G, k = GA * TPG * q + u, GA * q + u // TPG, u % TPG
                    h = u // TPG % 2
                    if k == 0:
                        pe.wait_ge(S["o2_ready"], G + 1)
                        need(pe, S["acc_done"], G - 1)
                    pe.wait_ge(S["msg_ready"], i + 1)
                    o = ps_row[h]
                    tm.matmul(o[:, 0:D], onehot[:, h, k, :].bitcast(F32), gat_c[:, u, 0:D], start=(k == 0), stop=(k == TPG - 1))
                    tm.matmul(o[:, D:RW], onehot[:, h, k, :].bitcast(F32), e_all[:, bass.ds(i * H, H)], start=(k == 0),
                              stop=(k == TPG - 1)).then_inc(S["agg_done"], 1)

            pe.wait_ge(S["ex_back"], 6)
            sum_by_dst(0)
            with pe.Fori(1, QA) as q:
                sum_by_dst(q)

            pe.wait_ge(S["acc_done"], NG)
            def z2_T(t):
                pe.wait_ge(S["z2_ready"], t + 1)
                if t >= 2:
                    pe.wait_ge(S["h2T_ready"], t - 1)
                transpose_rows(ps[:, t % 2, :], lnz[:, t % 2, :]).then_inc(S["z2T"], 1)

            for t in range(TPG):
                z2_T(t)
            pe.wait_ge(S["w_in"], (FC + F1 // P) * 16)
            n = 0
            for ch in range(3):
                w = min(D, N - ch * D)
                pe.wait_ge(S["h2T_ready"], min(TPG * (ch + 1), NT))
                for f in range(F1 // P):
                    if TPG <= n < NT:
                        z2_T(n)
                    if n >= 4:
                        pe.wait_ge(S["hid_ready"], n - 3)
                    for c in range(FC):
                        m = tm.matmul(ps[:, f1_bank[n % 4], 0:w], W1_sb[:, c, f * P:(f + 1) * P], hT[:, c, ch * D:ch * D + w],
                                      start=(c == 0), stop=(c == FC - 1))
                    m.then_inc(S["f1_mm"], 1)
                    n += 1
                for t in range(4 * ch, 4 * ch + (w + P - 1) // P):
                    r = min(P, N - t * P)
                    if t >= 2:
                        pe.wait_ge(S["u_ready"], t - 1)
                    for f in range(F1 // P):
                        if t == 4 * ch:
                            pe.wait_ge(S["hid_ready"], ch * (F1 // P) + f + 1)
                        m = tm.matmul(ps[0:r, 4 + t % 2, :], hid[:, f, (t - 4 * ch) * P:(t - 4 * ch) * P + r], W2_sb[:, f, :],
                                      start=(f == 0), stop=(f == F1 // P - 1))
                    m.then_inc(S["f2_mm"], 1)

            def edge_T(G, h):
                pe.wait_ge(S["ea_split"], G + 1)
                need(pe, S["ea_ready"], G)
                for k in range(TPG):
                    m = tm.transpose(ps[:, 6, k * P:(k + 1) * P].bitcast(FR), ea_hl[:, h, k, :], ident_r[:])
                m.then_inc(S["ea_p"], 1)

            def edge_project(i, u, G, h):
                k = u % TPG
                if k == 0:
                    pe.wait_ge(S["ea_ready"], G + 1)
                need(pe, S["t_ready"], i - 3)
                for part, tab in enumerate((We_hi, We_lo)):
                    m = tm.matmul(ps[:, pr_bank[u % 4], :], eaT[:, h, k * P:(k + 1) * P], tab[:], start=(part == 0), stop=(part == 1))
                m.then_inc(S["tw_done"], 1)

            def sum_messages(i, u, G, h):
                k = u % TPG
                if k == 0:
                    pe.wait_ge(S["o3_ready"], G + 1)
                    need(pe, S["acc2_done"], G - 1)
                pe.wait_ge(S["m2_ready"], i + 1)
                o, w = ps[:, 2 * h, :], onehot[:, h, k, :]
                if k == 0:
                    tm.matmul(o, w.bitcast(F32), zbuf[:, 4 + u % 4, 0:D], start=True, stop=False).then_inc(S["ag2_done"], 1)
                    return
                tm.matmul(o[:, MS:D], w.bitcast(F32), zbuf[:, 4 + u % 4, MS:D], start=False, stop=False)
                pe.wait_ge(S["m2_rest"], (TPG - 1) * G + k)
                tm.matmul(o[:, 0:MS], w, m_hi[:, u % 4, :], start=False, stop=False)
                tm.matmul(o[:, 0:MS], w, m_lo[:, u % 4, :], start=False, stop=(k == TPG - 1)).then_inc(S["ag2_done"], 1)

            def phase_d(q, first, last):
                for u in range(UN):
                    i, G, h = UN * q + u, 2 * q + u // TPG, u // TPG
                    if not (last and h == 1):
                        edge_project(i + TPG, u, G + 1, 1 - h)
                    if u % TPG == 1 and not last:
                        edge_T(G + 2, h)
                    sum_messages(i, u, G, h)

            edge_T(0, 0)
            edge_T(1, 1)
            pe.wait_ge(S["u_ready"], NT)
            pe.wait_ge(S["We_ready"], 2)
            for u in range(TPG):
                edge_project(u, u, 0, 0)
            phase_d(0, True, False)
            with pe.Fori(1, Q - 1) as q:
                phase_d(q, False, False)
            phase_d(Q - 1, False, True)

            pe.wait_ge(S["acc2_done"], NG)
            for t in range(NT):
                if t >= 2:
                    pe.wait_ge(S["hhT_ready"], t - 1)
                transpose_rows(ps[:, t % 2, :], acc[:, t, :]).then_inc(S["hhT_p"], 1)
            pe.wait_ge(S["v_in"], 16)
            pe.wait_ge(S["hhT_ready"], NT)
            n = 0
            for f in range(F2 // P):
                for ch in range(3):
                    w = min(D, N - ch * D)
                    if n >= 4:
                        pe.wait_ge(S["u_cp"], n - 3)
                    for c in range(FC):
                        m = tm.matmul(ps[:, f1_bank[n % 4], 0:w], V1_sb[:, c, f * P:(f + 1) * P], hT[:, c, ch * D:ch * D + w],
                                      start=(c == 0), stop=(c == FC - 1))
                    m.then_inc(S["u_mm"], 1)
                    n += 1
            n = 0
            pe.wait_ge(S["v2_in"], 16)
            for f in range(FC):
                for ch in range(3):
                    w = min(D, N - ch * D)
                    if n >= 2:
                        pe.wait_ge(S["y_cp"], n - 1)
                    for k in range(F2 // P):
                        if n == 0:
                            pe.wait_ge(S["sT_ready"], k + 1)
                        m = tm.matmul(ps[:, 4 + n % 2, 0:w], V2_sb[:, k, f * P:(f + 1) * P], uT[:, k, ch * D:ch * D + w],
                                      start=(k == 0), stop=(k == F2 // P - 1))
                    m.then_inc(S["y_mm"], 1)
                    n += 1
            pe.wait_ge(S["yT_ready"], FC - 1)
            for t in range(NT):
                if t >= 6:
                    pe.wait_ge(S["v_ready"], t - 5)
                for f in range(FC - 1):
                    m = tm.transpose(ps[0:min(P, N - t * P), early_bank[t % 6], f * P:(f + 1) * P], yT[:, f, t * P:min(N, (t + 1) * P)], ident[:])
                m.then_inc(S["yb_p"], 1)
            pe.wait_ge(S["yT_ready"], FC)
            for t in range(NT):
                if t >= 2:
                    pe.wait_ge(S["v_last"], t - 1)
                tm.transpose(ps[0:min(P, N - t * P), 4 + t % 2, t // 2 % 4 * P:t // 2 % 4 * P + P], yT[:, FC - 1, t * P:min(N, (t + 1) * P)],
                             ident[:]).then_inc(S["yb_last"], 1)


_INS = ['x', 'src', 'dst', 'edge_attr_64', 'L0_gnn_ln1_g', 'L0_gnn_ln1_b', 'L0_gnn_Wl', 'L0_gnn_Wr', 'L0_gnn_att',
        'L0_gnn_gat_bias', 'L0_gnn_ln2_g', 'L0_gnn_ln2_b', 'L0_gnn_W1', 'L0_gnn_b1', 'L0_gnn_W2', 'L0_gnn_b2',
        'L1_gnn_W_e', 'L1_gnn_b_e', 'L1_gnn_W1', 'L1_gnn_b1', 'L1_gnn_g1', 'L1_gnn_beta1', 'L1_gnn_W2', 'L1_gnn_b2',
        'L1_gnn_g2', 'L1_gnn_beta2', 'L1_gnn_eps']
_OUTS = [((1250, 512), 'float32')]


def kernel(**inputs):
    import numpy as _np
    import concourse.bacc as _bacc
    from concourse import mybir as _mybir
    from concourse.bass_utils import run_bass_kernel_spmd as _run

    nc = _bacc.Bacc("TRN2", target_bir_lowering=False, num_devices=1)
    arrays, args = {}, []
    for name in _INS:
        a = _np.ascontiguousarray(inputs[name])
        if a.ndim == 0:
            a = a.reshape(1)
        arrays[f"in_{name}_dram"] = a
        args.append(nc.dram_tensor(f"in_{name}_dram", a.shape, _mybir.dt.from_np(a.dtype), kind="ExternalInput").ap())
    for i, (shape, dtype) in enumerate(_OUTS):
        dt = _mybir.dt.from_np(_np.dtype(dtype))
        args.append(nc.dram_tensor(f"out_{i}_dram", shape, dt, kind="ExternalOutput").ap())
    gnn_kernel(nc, *args)
    r = _run(nc, [arrays], core_ids=[0])
    got = tuple(r.results[0][f"out_{i}_dram"] for i in range(len(_OUTS)))
    return got[0]
```
